# Optimizing a Trainium2 kernel written in Bass

```python
import numpy as np
import jax
import jax.numpy as jnp

def _softmax(x, axis=-1):
    return jax.nn.softmax(x, axis=axis)

def _gelu(x):
    return jax.nn.gelu(x, approximate=True)

def _silu(x):
    return jax.nn.silu(x)

def _sigmoid(x):
    return jax.nn.sigmoid(x)

def _layernorm(x, axis=-1, eps=1e-05):
    m = jnp.mean(x, axis=axis, keepdims=True)
    v = jnp.var(x, axis=axis, keepdims=True)
    return (x - m) / jnp.sqrt(v + eps)

def _scatter_add(tgt, idx, src, axis=0):
    return tgt.at[idx].add(src)

def _segment_sum(src, seg, n):
    return jax.ops.segment_sum(src, seg, n)
kernel_name = 'mk_gnn_preln_d1_gnn_r64_6fc7b8'

def setup_inputs(seed: int=0):
    np.random.seed(seed)
    _w = jnp.asarray

    def _rec_inputs():
        import jax
        import jax.numpy as jnp
        _gk = jax.random.key(seed)
        x = -0.0003713 + 1 * jax.random.normal(jax.random.fold_in(_gk, 1), (100000, 256), jnp.float32)
        src = jax.random.randint(jax.random.fold_in(_gk, 2), (25000,), 0, 100000, jnp.int32)
        dst = jax.random.randint(jax.random.fold_in(_gk, 3), (25000,), 0, 100000, jnp.int32)
        _o = jnp.argsort(dst, stable=True)
        src = src[_o]
        dst = dst[_o]
        return (x, src, dst)
    x, src, dst = _rec_inputs()

    def _L0_gnn_setup():
        import jax, jax.numpy as jnp
        import numpy as np
        N = 50000
        E = 12500
        F = 256
        H = 4
        D = 64
        HD = H * D
        key = jax.random.key(seed)
        ks = jax.random.split(key, 16)
        s = 0.05
        inp = {'feat': jax.random.normal(ks[0], (N, F), jnp.float32), 'src': jax.random.randint(ks[1], (E,), 0, N, dtype=jnp.int32), 'dst': jax.random.randint(ks[2], (E,), 0, N, dtype=jnp.int32), 'Wq': jax.random.normal(ks[3], (F, HD), jnp.float32) * s, 'bq': jnp.zeros((HD,), jnp.float32), 'Wk': jax.random.normal(ks[4], (F, HD), jnp.float32) * s, 'bk': jnp.zeros((HD,), jnp.float32), 'Wv': jax.random.normal(ks[5], (F, HD), jnp.float32) * s, 'bv': jnp.zeros((HD,), jnp.float32), 'Wskip': jax.random.normal(ks[6], (F, HD), jnp.float32) * s, 'bskip': jnp.zeros((HD,), jnp.float32), 'Wg': jax.random.normal(ks[7], (3 * HD, 1), jnp.float32) * s, 'bg': jnp.zeros((1,), jnp.float32), 'ln_scale': jnp.ones((HD,), jnp.float32), 'ln_bias': jnp.zeros((HD,), jnp.float32), 'prelu_alpha': jnp.asarray(0.25, jnp.float32)}
        return inp
    _L0_gnn_all = _L0_gnn_setup()
    _L0_gnn_in = {k: v for k, v in _L0_gnn_all.items() if k in ('Wq', 'bq', 'Wk', 'bk', 'Wv', 'bv', 'Wskip', 'bskip', 'Wg', 'bg', 'ln_scale', 'ln_bias', 'prelu_alpha')}
    del _L0_gnn_all
    return {'x': x, 'src': src, 'dst': dst, 'L0_gnn_Wq': _L0_gnn_in['Wq'], 'L0_gnn_bq': _L0_gnn_in['bq'], 'L0_gnn_Wk': _L0_gnn_in['Wk'], 'L0_gnn_bk': _L0_gnn_in['bk'], 'L0_gnn_Wv': _L0_gnn_in['Wv'], 'L0_gnn_bv': _L0_gnn_in['bv'], 'L0_gnn_Wskip': _L0_gnn_in['Wskip'], 'L0_gnn_bskip': _L0_gnn_in['bskip'], 'L0_gnn_Wg': _L0_gnn_in['Wg'], 'L0_gnn_bg': _L0_gnn_in['bg'], 'L0_gnn_ln_scale': _L0_gnn_in['ln_scale'], 'L0_gnn_ln_bias': _L0_gnn_in['ln_bias'], 'L0_gnn_prelu_alpha': _L0_gnn_in['prelu_alpha']}

def reference(x, src, dst, L0_gnn_Wq, L0_gnn_bq, L0_gnn_Wk, L0_gnn_bk, L0_gnn_Wv, L0_gnn_bv, L0_gnn_Wskip, L0_gnn_bskip, L0_gnn_Wg, L0_gnn_bg, L0_gnn_ln_scale, L0_gnn_ln_bias, L0_gnn_prelu_alpha):
    import jax
    import jax.numpy as jnp

    def _L0_gnn_ref(feat, src, dst, Wq, bq, Wk, bk, Wv, bv, Wskip, bskip, Wg, bg, ln_scale, ln_bias, prelu_alpha):
        import jax, jax.numpy as jnp
        import numpy as np
        N = 50000
        E = 12500
        F = 256
        H = 4
        D = 64
        HD = H * D
        n = feat.shape[0]
        q = (feat @ Wq + bq).reshape(n, H, D)
        k = (feat @ Wk + bk).reshape(n, H, D)
        v = (feat @ Wv + bv).reshape(n, H, D)
        score = jnp.einsum('ehd,ehd->eh', q[src], k[dst]) / np.sqrt(D).astype(np.float32)
        m = jax.ops.segment_max(score, dst, num_segments=n)
        a = jnp.exp(score - m[dst])
        denom = jax.ops.segment_sum(a, dst, num_segments=n)
        sa = a / denom[dst]
        agg = jax.ops.segment_sum(v[src] * sa[..., None], dst, num_segments=n)
        rst = agg.reshape(n, HD)
        skip = feat @ Wskip + bskip
        gate = jax.nn.sigmoid(jnp.concatenate([skip, rst, skip - rst], axis=-1) @ Wg + bg)
        rst = gate * skip + (1.0 - gate) * rst
        mu = rst.mean(axis=-1, keepdims=True)
        var = rst.var(axis=-1, keepdims=True)
        rst = (rst - mu) * jax.lax.rsqrt(var + 1e-05) * ln_scale + ln_bias
        return jnp.where(rst > 0, rst, prelu_alpha * rst)
    h = jnp.maximum(_layernorm(x, axis=-1), 0.0)
    x = x + _L0_gnn_ref(h, src, dst, L0_gnn_Wq, L0_gnn_bq, L0_gnn_Wk, L0_gnn_bk, L0_gnn_Wv, L0_gnn_bv, L0_gnn_Wskip, L0_gnn_bskip, L0_gnn_Wg, L0_gnn_bg, L0_gnn_ln_scale, L0_gnn_ln_bias, L0_gnn_prelu_alpha)
    return x

_drawn_inputs = setup_inputs


def setup_inputs(seed=0):
    import zlib

    import numpy as np

    out = dict(_drawn_inputs(seed))
    spreads = {'L0_gnn_bq': (0.0, 0.8),
     'L0_gnn_bk': (0.0, 0.8),
     'L0_gnn_bv': (0.0, 0.273),
     'L0_gnn_bskip': (0.0, 0.1),
     'L0_gnn_ln_scale': (1.0, 0.2),
     'L0_gnn_ln_bias': (0.0, 0.1)}
    factors = {'L0_gnn_Wq': 8.0, 'L0_gnn_Wk': 8.0}
    for name, (base, spread) in spreads.items():
        noise = np.random.default_rng([zlib.crc32(name.encode()), seed]).standard_normal(out[name].shape)
        drawn = base * np.exp(spread * noise) if base else spread * noise
        out[name] = jnp.asarray(drawn.astype(out[name].dtype))
    for name, factor in factors.items():
        out[name] = (out[name] * factor).astype(out[name].dtype)
    return out
```

```python
import concourse.bass as bass
from concourse import mybir
from contextlib import ExitStack


def gnn_layer(nc, x, src, dst, w_q, b_q, w_k, b_k, w_v, b_v, w_skip, b_skip, w_gate, b_gate,
              ln_scale, ln_bias, prelu_alpha, out):
    fp32 = mybir.dt.float32
    bf16 = mybir.dt.bfloat16
    i32 = mybir.dt.int32
    ALU = mybir.AluOpType
    ACT = mybir.ActivationFunctionType
    AX = mybir.AxisListType

    P = 128
    N, F = x.shape
    C = F // P
    EPS = 1e-5
    R = 4
    ROWS = P * R
    BLOCKS = -(-N // ROWS)
    XS = 8
    US = 4
    AHEAD = 5
    MAIN = (BLOCKS - 1 - AHEAD) // XS

    E = src.shape[0]
    H = 4
    D = F // H
    V = D + 2
    T = -(-E // P)
    G = -(-T // R)
    TP = G * R
    HALF = TP // 2
    SCORE_SCALE = float(D) ** -0.5
    BIG = 1e30
    SKIP_ROW = float(1 << 20)
    META = 2 * R + R * H
    EU = 8
    EMAIN = (G - 2) // EU
    WB = dict(q=0, k=F, v=2 * F, s=2 * F + H * (D + 1), d=2 * F + H * (D + 1) + F + 1)
    BW = WB['d'] + F + 1

    def block_rows(tensor, k, j=None):
        if isinstance(k, int) and k == BLOCKS - 1:
            return tensor[N - ROWS:N, :].rearrange("(p r) f -> p (r f)", r=R)
        blocks = tensor[0:(BLOCKS - 1) * ROWS, :].rearrange("(n p r) f -> n p (r f)", p=P, r=R)
        if isinstance(k, int):
            return blocks[k, :, :]
        return blocks[bass.ds(k, 1), :, :].rearrange("n p m -> p (n m)")

    ctx = ExitStack()
    with ctx:
        def sb(name, shape, dt=fp32):
            return ctx.enter_context(nc.sbuf_tensor(name, shape, dt))

        def ps(name, shape, dt=fp32):
            return ctx.enter_context(nc.psum_tensor(name, shape, dt))

        def sem(name):
            return ctx.enter_context(nc.semaphore(name))

        wskip_sb = sb("wskip_sb", [P, C, F + 1])
        wq_sb = sb("wq_sb", [P, C, F])
        wk_sb = sb("wk_sb", [P, C, F])
        wv_sb = sb("wv_sb", [P, C, H, D + 1])
        bq_bc = sb("bq_bc", [P, F])
        bk_bc = sb("bk_bc", [P, F])
        bv_bc = sb("bv_bc", [P, F])
        g23_bc = sb("g23_bc", [P, F])
        negalpha_bc = sb("negalpha_bc", [P, 1])
        last_row = sb("last_row", [P, P])
        wd_sb = sb("wd_sb", [P, C, F + 1])
        gate_rows = sb("gate_rows", [P, 3, F])
        g13_bc = sb("g13_bc", [P, F])
        bskip_bc = sb("bskip_bc", [P, F])
        lns_bc = sb("lns_bc", [P, F + 1])
        lnb_bc = sb("lnb_bc", [P, F])
        alpha_bc = sb("alpha_bc", [P, 1])
        bgate_bc = sb("bgate_bc", [P, 1])
        ident = sb("ident", [P, P])
        ones3 = sb("ones3", [3, P], bf16)
        setup_scr = sb("setup_scr", [P, F])
        wmean = sb("wmean", [P, C + 1])
        ubias = sb("ubias", [P, H])
        bias3 = sb("bias3", [3, BW], bf16)
        nhalf = sb("nhalf", [P, 2 * R])
        none = sb("none", [P, R])
        one4 = sb("one4", [P, R])
        eps4 = sb("eps4", [P, 2 * R])

        xt = sb("xt", [P, XS, R * F])
        xn = sb("xn", [P, 2, R * F])
        hT = sb("hT", [P, 2, R * C * P])
        wy = sb("wy", [P, 2, R, F + 1])
        ut = sb("ut", [P, US, R * F])
        pos = sb("pos", [P, 2, R * F])
        neg = sb("neg", [P, 2, R * F])
        bias_row = pos[0:3, :, :].rearrange("p a b -> p (a b)")[:, 0:BW]
        bias_left = neg[0:3, :, :].rearrange("p a b -> p (a b)")[:, 0:BW]
        bias_sel = wy[0:3, :, :, :].rearrange("p a b c -> p (a b c)")[:, 0:BW]
        bias_part = ut[0:3, :, :].rearrange("p a b -> p (a b)").bitcast(bf16)[:, 0:3 * BW].rearrange("p (a b) -> p a b", a=3)

        nat_i = sb("nat_i", [HALF, 3, 2 * P], i32)
        nat_f = sb("nat_f", [HALF, 5, 2 * P])
        key_cols = sb("key_cols", [P, TP + 1])
        eq_cols = sb("eq_cols", [P, TP])
        meta = sb("meta", [P, G, META])
        rows_idx = sb("rows_idx", [P, G, 3 * R], i32)
        meta_b = sb("meta_b", [P, 2, META])
        idx_b = sb("idx_b", [P, EU, 3 * R], i32)
        xsrc = sb("xsrc", [P, 4, R * F])
        emv = sb("emv", [P, 2, 2 * R, 2])
        estats = sb("estats", [P, 2, 2 * R, 6])
        erstd = sb("erstd", [P, 2, 2 * R])
        q_sb = sb("q_sb", [P, 2, F])
        v_ring = sb("v_ring", [P, 4, R * H, V])
        sk_ring = sb("sk_ring", [P, 4, R, F + 1])
        score = sb("score", [P, 2, R * H])
        seg_mask = sb("seg_mask", [R * H, P + 1])
        run_max = sb("run_max", [R * H, P])
        seg_maxT = sb("seg_maxT", [P, P])
        tile_max = sb("tile_max", [P, R * H])
        same = sb("same", [P, 2, R * P])
        carry_max = sb("carry_max", [P, R, H])
        maxes = sb("maxes", [P, 2, R, H])
        expo = sb("expo", [P, 2, R * H])
        aw = sb("aw", [P, 2, 2, R * H])
        vals = sb("vals", [P, R, H * V])
        carried = sb("carried", [P, H * V])
        state = sb("state", [P, 2, R, H * V])
        rden = sb("rden", [P, R * H])
        ugate = sb("ugate", [P, R * H])
        logit = sb("logit", [P, R])
        eexp = sb("eexp", [P, 2, R])
        egt = sb("egt", [P, R])
        omg = sb("omg", [P, R])
        coef = sb("coef", [P, R * H])
        mix = wy[:, 0, :, 0:F]
        mstats = sb("mstats", [P, R, 6])
        mmv = sb("mmv", [P, R, 2])
        mrstd = sb("mrstd", [P, R])
        xstats = sb("xstats", [P, 2, R, 6])
        xmv = sb("xmv", [P, 2, R, 2])
        xrstd = sb("xrstd", [P, 2, R])
        pool_mark = sb("pool_mark", [P, 1])
        wait_mark = sb("wait_mark", [P, 1])
        sq_scr = sb("sq_scr", [P, R, F])
        ssq = sb("ssq", [P, 2, R])
        egate = sb("egate", [P, 2, R])
        gate = sb("gate", [P, 2, R])
        gate2 = sb("gate2", [P, 2, R])
        yscale = sb("yscale", [P, 2, R])

        prod = sq_scr[:, :, :]

        hT_ps = ps("hT_ps", [P, 2, 512])
        y_ps = ps("y_ps", [P, R, 512])
        agg_ps = ps("agg_ps", [P, 512])
        carry_ps = ps("carry_ps", [P, 512])
        ehT_ps = hT_ps[:, 0, :]
        q_ps, k_ps = y_ps[:, 0, 0:F], y_ps[:, 0, F:2 * F]
        v_ps = y_ps[:, 1, 0:H * (D + 1)]
        sk_ps = y_ps[:, 2, 0:F + 1]
        keyrow_ps = y_ps[:, 3, :]
        scoreT_ps = hT_ps[0:R * H, 1, 0:P]
        eqT_ps = hT_ps[0:R * H, 1, P:2 * P]
        tmax_ps = hT_ps[:, 1, 2 * P:3 * P]
        cmax_ps = hT_ps[:, 1, 3 * P:3 * P + H]

        loaded = sem("weights_loaded")
        ident_ready = sem("ident_ready")
        setup_step = sem("setup_step")
        setup_done = sem("setup_done")
        x_loaded = [sem(f"x_loaded{s}") for s in range(XS)]
        u_stored = [sem(f"u_stored{s}") for s in range(US)]
        xstats_ready = sem("xstats_ready")
        xmv_ready = sem("xmv_ready")
        xvar_ready = sem("xvar_ready")
        xrstd_ready = sem("xrstd_ready")
        xn_ready = sem("xn_ready")
        hTps_ready = sem("hTps_ready")
        hT_ready = sem("hT_ready")
        y_ready = sem("y_ready")
        ysq_ready = sem("ysq_ready")
        egate_ready = sem("egate_ready")
        yscaled = sem("yscaled")
        gstep = sem("gstep")
        yscale_ready = sem("yscale_ready")
        u_ready = sem("u_ready")
        pos_ready = sem("pos_ready")
        neg_ready = sem("neg_ready")
        prelu_ready = sem("prelu_ready")
        row_ready = sem("row_ready")
        NLOAD = 9 + 4 * C
        e_stats_ready = sem("e_stats_ready")
        e_mv_ready = sem("e_mv_ready")
        e_rstd_ready = sem("e_rstd_ready")
        e_rstep = sem("e_rstep")
        e_xn_ready = sem("e_xn_ready")
        e_hTps_ready = sem("e_hTps_ready")
        e_hT_ready = sem("e_hT_ready")
        e_qk_ps_ready = sem("e_qk_ps_ready")
        e_vsk_ps_ready = sem("e_vsk_ps_ready")
        e_q_copied = sem("e_q_copied")
        e_vsk_copied = sem("e_vsk_copied")
        e_prod_ready = sem("e_prod_ready")
        e_score_ready = sem("e_score_ready")
        e_scoreT_ready = sem("e_scoreT_ready")
        e_scan = sem("e_scan")
        e_tmax_ps_ready = sem("e_tmax_ps_ready")
        e_tmax_ready = sem("e_tmax_ready")
        e_keyrow_ready = sem("e_keyrow_ready")
        e_same_ready = sem("e_same_ready")
        e_cmax_ps_ready = sem("e_cmax_ps_ready")
        e_cmax_ready = sem("e_cmax_ready")
        e_max_ready = sem("e_max_ready")
        e_meta_ready = sem("e_meta_ready")
        e_expo_ready = sem("e_expo_ready")
        e_aw_ready = sem("e_aw_ready")
        e_vals_ready = sem("e_vals_ready")
        e_agg_ps_ready = sem("e_agg_ps_ready")
        e_carried = sem("e_carried")
        e_state_ready = sem("e_state_ready")
        e_gstep = sem("e_gstep")
        e_logit_ready = sem("e_logit_ready")
        e_eexp_ready = sem("e_eexp_ready")
        e_mix = sem("e_mix")
        e_mmv_ready = sem("e_mmv_ready")
        e_mrstep = sem("e_mrstep")
        e_mrstd_ready = sem("e_mrstd_ready")
        e_u0 = sem("e_u0")
        e_u_ready = sem("e_u_ready")
        e_relu_ready = sem("e_relu_ready")
        e_prelu_ready = sem("e_prelu_ready")
        e_row_ready = sem("e_row_ready")
        e_idx_ready = sem("e_idx_ready")
        table_step = sem("table_step")
        table_ps_ready = sem("table_ps_ready")
        table_ready = sem("table_ready")
        edges_loaded = sem("edges_loaded")
        dense_written = sem("dense_written")
        e_v_ones = sem("e_v_ones")
        src_loaded = [sem(f"src_loaded{s}") for s in range(4)]
        dst_loaded = [sem(f"dst_loaded{s}") for s in range(XS)]
        scattered = [sem(f"scattered{s}") for s in range(US)]

        block = ctx.enter_context(nc.Block())

        LOOP_TURN = [None]

        def steady(engine, step, first, last):
            for k in range(first, XS):
                step(k, k)
            with engine.Fori(1, MAIN) as i:
                LOOP_TURN[0] = i
                for j in range(XS):
                    step(i * XS + j, j)
            for k in range(MAIN * XS, last):
                step(k, k % XS)

        def live(k, shift):
            return not isinstance(k, int) or 0 <= k + shift < BLOCKS

        def turns(k, j, n, shift):
            if isinstance(k, int):
                return (k + shift) // n
            return LOOP_TURN[0] * (XS // n) + (j + shift) // n

        @block.sync
        def _(sp):
            sp.dma_start(gate_rows[:, :, :], w_gate.rearrange("(o a f) c -> o (a f c)", o=1, a=3).to_broadcast([P, 3 * F])).then_inc(loaded, 16)
            for c in range(C):
                for w_sb, w in ((wskip_sb[:, c, 0:F], w_skip), (wq_sb[:, c, :], w_q), (wk_sb[:, c, :], w_k)):
                    sp.dma_start(w_sb, w[c * P:(c + 1) * P, :]).then_inc(loaded, 16)
                sp.dma_start(wv_sb[:, c, :, 0:D], w_v[c * P:(c + 1) * P, :].rearrange("p (h d) -> p h d", h=H)).then_inc(loaded, 16)
            for row, vec, n in ((bskip_bc, b_skip, F), (bq_bc, b_q, F), (bk_bc, b_k, F), (bv_bc, b_v, F), (lns_bc, ln_scale, F), (lnb_bc, ln_bias, F),
                                (alpha_bc, prelu_alpha, 1), (bgate_bc, b_gate, 1)):
                sp.dma_start(row[:, 0:n], vec.rearrange("(o f) -> o f", o=1).to_broadcast([P, n])).then_inc(loaded, 16)

            def load(k, j):
                s = (j + 0) % XS
                sp.dma_start(xt[:, s, :], block_rows(x, k)).then_inc(x_loaded[s], 16)

            def step(k, j):
                if live(k, AHEAD):
                    if not isinstance(k, int) or k + AHEAD >= XS:
                        sp.wait_ge(row_ready, k + AHEAD - XS + 1)
                    s = (j + AHEAD) % XS
                    sp.dma_start(xt[:, s, :], block_rows(x, k + AHEAD)).then_inc(x_loaded[s], 16)
                if live(k, -2):
                    sp.wait_ge(row_ready, k - 1)
                    if isinstance(k, int) and k - 2 == BLOCKS - 1:
                        for s in range(US):
                            sp.wait_ge(u_stored[s], 16 * ((BLOCKS - 1) // US + (s < (BLOCKS - 1) % US)))
                    s = (j - 2) % US
                    sp.dma_start(block_rows(out, k - 2), ut[:, s, :]).then_inc(u_stored[s], 16)

            sp.wait_ge(table_step, 1)
            full = E // (2 * P)
            for n, (vec, shift) in enumerate(((src, 0), (dst, 0), (dst, 1))):
                left = E - full * 2 * P - shift
                sp.dma_start(nat_i[0:full, n, :], vec[shift:shift + full * 2 * P].rearrange("(p m) -> p m", p=full)).then_inc(edges_loaded, 16)
                sp.dma_start(nat_i[full:full + 1, n, 0:left],
                             vec[full * 2 * P + shift:E].rearrange("(p m) -> p m", p=1)).then_inc(edges_loaded, 16)

            for k in range(AHEAD):
                sp.dma_start(xt[:, k, :], block_rows(x, k)).then_inc(x_loaded[k], 16)
            steady(sp, step, 0, BLOCKS + 2)
            for s in range(US):
                sp.wait_ge(u_stored[s], 16 * (BLOCKS // US + (s < BLOCKS % US)))
            sp.sem_inc(dense_written, 1)

        def e_steady(engine, step, first, last):
            for g in range(first, EU):
                step(g, g)
            with engine.Fori(1, EMAIN) as i:
                LOOP_TURN[0] = i
                for j in range(EU):
                    step(i * EU + j, j)
            for g in range(EMAIN * EU, last):
                step(g, g % EU)

        def e_live(g, shift):
            return not isinstance(g, int) or 0 <= g + shift < G

        def e_past(g, shift):
            return not isinstance(g, int) or g + shift >= 0

        def e_turns(g, j, n, shift):
            if isinstance(g, int):
                return (g + shift) // n
            return LOOP_TURN[0] * (EU // n) + (j + shift) // n

        @block.gpsimd
        def _(pool):
            nc.gpsimd.memset(ones3[:, :], 1.0).then_inc(ident_ready, 1)
            nc.gpsimd.memset(nhalf[:, :], -0.5).then_inc(ident_ready, 1)
            nc.gpsimd.memset(none[:, :], -1.0).then_inc(ident_ready, 1)
            nc.gpsimd.memset(one4[:, :], 1.0).then_inc(ident_ready, 1)
            nc.gpsimd.memset(eps4[:, :], EPS).then_inc(ident_ready, 1)
            nc.gpsimd.memset(ident[:, :], 0.0).then_inc(ident_ready, 1)
            nc.gpsimd.memset(last_row[:, :], 0.0).then_inc(ident_ready, 1)
            nc.gpsimd.memset(nat_i[:, 0, :], 0).then_inc(ident_ready, 1)
            nc.gpsimd.memset(nat_i[:, 1, :], N).then_inc(ident_ready, 1)
            nc.gpsimd.memset(nat_i[:, 2, :], N + 1).then_inc(ident_ready, 1)
            pool.wait_ge(ident_ready, 10)
            nc.gpsimd.affine_select(out=ident[:, :], in_=ident[:, :], compare_op=ALU.not_equal, fill=1.0, base=0,
                                    pattern=[[-1, P]], channel_multiplier=1).then_inc(ident_ready, 1)
            nc.gpsimd.affine_select(out=last_row[:, :], in_=last_row[:, :], compare_op=ALU.not_equal, fill=1.0, base=-(P - 1),
                                    pattern=[[0, P]], channel_multiplier=1).then_inc(ident_ready, 1)
            pool.wait_ge(ident_ready, 12)
            nc.gpsimd.memset(key_cols[:, 0:1], -1.0).then_inc(table_step, 1)

            def x_rstd(k, b):
                pool.wait_ge(xmv_ready, k + 1)
                nc.gpsimd.tensor_tensor(xrstd[:, b, :], xmv[:, b, :, 1], eps4[:, 0:R], ALU.add).then_inc(xvar_ready, 1)
                pool.wait_ge(xvar_ready, k + 1)
                nc.gpsimd.tensor_tensor(xrstd[:, b, :], xrstd[:, b, :], nhalf[:, 0:R], ALU.pow).then_inc(xrstd_ready, 1)

            def y_scale(k, b):
                pool.wait_ge(egate_ready, k + 1)
                nc.gpsimd.tensor_tensor(gate[:, b, :], egate[:, b, :], one4[:, :], ALU.add).then_inc(gstep, 1)
                pool.wait_ge(gstep, 5 * k + 1)
                nc.gpsimd.tensor_tensor(gate[:, b, :], gate[:, b, :], none[:, :], ALU.pow).then_inc(gstep, 1)
                pool.wait_ge(gstep, 5 * k + 2)
                nc.gpsimd.tensor_tensor(gate2[:, b, :], gate[:, b, :], gate[:, b, :], ALU.mult).then_inc(gstep, 1)
                pool.wait_ge(gstep, 5 * k + 3)
                nc.gpsimd.tensor_tensor(gate2[:, b, :], gate2[:, b, :], ssq[:, b, :], ALU.mult).then_inc(gstep, 1)
                pool.wait_ge(gstep, 5 * k + 4)
                nc.gpsimd.tensor_tensor(gate2[:, b, :], gate2[:, b, :], eps4[:, 0:R], ALU.add).then_inc(gstep, 1)
                pool.wait_ge(gstep, 5 * k + 5)
                nc.gpsimd.tensor_tensor(gate2[:, b, :], gate2[:, b, :], nhalf[:, 0:R], ALU.pow).then_inc(yscale_ready, 1)
                pool.wait_ge(yscale_ready, 2 * k + 1)
                nc.gpsimd.tensor_tensor(yscale[:, b, :], gate2[:, b, :], gate[:, b, :], ALU.mult).then_inc(yscale_ready, 1)

            def step(k, j):
                if live(k, -1):
                    y_scale(k - 1, (j - 1) % 2)
                if live(k, 2):
                    x_rstd(k + 2, j % 2)
                if live(k, -2):
                    pool.wait_ge(pos_ready, k - 1)
                    pool.wait_ge(neg_ready, k - 1)
                    s = (j - 2) % US
                    nc.gpsimd.tensor_tensor(ut[:, s, :], pos[:, j % 2, :], neg[:, j % 2, :], ALU.add).then_inc(prelu_ready, 1)
                    pool.wait_ge(prelu_ready, k - 1)
                    nc.gpsimd.tensor_tensor(ut[:, s, :], ut[:, s, :], xt[:, (j - 2) % XS, :], ALU.add).then_inc(row_ready, 1)

            x_rstd(0, 0)
            x_rstd(1, 1)
            steady(pool, step, 0, BLOCKS + 2)

            last_node = pool.to_reg(N - 1)

            def gather(g, j):
                if e_past(g, -EU):
                    pool.wait_ge(scattered[j % US], 16 * R * (e_turns(g, j, US, -EU) + 1))
                pool.wait_ge(table_ready, 1)
                if isinstance(g, int):
                    nc.gpsimd.tensor_copy(idx_b[:, j % EU, :], rows_idx[:, g, :]).then_inc(e_idx_ready, 1)
                else:
                    nc.gpsimd.tensor_copy(idx_b[:, j % EU, :], rows_idx[:, bass.ds(g, 1), :].rearrange("p a b -> p (a b)")).then_inc(e_idx_ready, 1)
                pool.wait_ge(e_idx_ready, g + 1)
                if e_past(g, -4):
                    pool.wait_ge(e_xn_ready, g - 3)
                nc.gpsimd.tensor_tensor(pool_mark[:, :], one4[:, 0:1], one4[:, 0:1], ALU.add)
                for r in range(R):
                    nc.gpsimd.indirect_dma_start(
                        out=xsrc[:, j % 4, r * F:(r + 1) * F], out_offset=None, in_=x[:, :],
                        in_offset=bass.IndirectOffsetOnAxis(ap=idx_b[:, j % EU, r:r + 1], axis=0),
                        bounds_check=last_node, oob_is_err=True).then_inc(src_loaded[j % 4], 16)
                    nc.gpsimd.indirect_dma_start(
                        out=xt[:, j % XS, r * F:(r + 1) * F], out_offset=None, in_=x[:, :],
                        in_offset=bass.IndirectOffsetOnAxis(ap=idx_b[:, j % EU, R + r:R + r + 1], axis=0),
                        bounds_check=last_node, oob_is_err=True).then_inc(dst_loaded[j % XS], 16)

            def edge_rstd(g, b):
                pool.wait_ge(e_mv_ready, g + 1)
                nc.gpsimd.tensor_tensor(erstd[:, b, :], emv[:, b, :, 1], eps4[:, :], ALU.add).then_inc(e_rstep, 1)
                pool.wait_ge(e_rstep, g + 1)
                nc.gpsimd.tensor_tensor(erstd[:, b, :], erstd[:, b, :], nhalf[:, :], ALU.pow).then_inc(e_rstd_ready, 1)

            def e_step(g, j):
                if e_live(g, 2):
                    gather(g + 2, j + 2)
                if e_live(g, 1):
                    edge_rstd(g + 1, (j + 1) % 2)
                if e_live(g, -3):
                    pool.wait_ge(e_mmv_ready, g - 2)
                    nc.gpsimd.tensor_tensor(mrstd[:, :], mmv[:, :, 1], eps4[:, 0:R], ALU.add).then_inc(e_mrstep, 1)
                    pool.wait_ge(e_mrstep, g - 2)
                    nc.gpsimd.tensor_tensor(mrstd[:, :], mrstd[:, :], nhalf[:, 0:R], ALU.pow).then_inc(e_mrstd_ready, 1)
                if e_live(g, -4):
                    s = (j - 4) % US
                    pool.wait_ge(e_prelu_ready, g - 3)
                    nc.gpsimd.tensor_tensor(ut[:, s, :], ut[:, s, :], xt[:, (j - 4) % XS, :], ALU.add).then_inc(e_row_ready, 1)
                    pool.wait_ge(e_row_ready, g - 3)
                    nc.gpsimd.tensor_tensor(pool_mark[:, :], one4[:, 0:1], one4[:, 0:1], ALU.add)
                    for r in range(R):
                        nc.gpsimd.indirect_dma_start(
                            out=out[:, :], out_offset=bass.IndirectOffsetOnAxis(ap=idx_b[:, (j - 4) % EU, 2 * R + r:2 * R + r + 1], axis=0),
                            in_=ut[:, s, r * F:(r + 1) * F], in_offset=None,
                            bounds_check=last_node, oob_is_err=False).then_inc(scattered[s], 16)

            pool.wait_ge(row_ready, BLOCKS)
            gather(0, 0)
            gather(1, 1)
            edge_rstd(0, 0)
            pool.wait_ge(dense_written, 1)
            e_steady(pool, e_step, 0, G + 4)
            for s in range(US):
                pool.wait_ge(scattered[s], 16 * R * (G // US + (s < G % US)))

        @block.vector
        def _(dve):
            setup_count = [0]

            def chain(ins):
                setup_count[0] += 1
                ins.then_inc(setup_step, 1)
                dve.wait_ge(setup_step, setup_count[0])

            dve.wait_ge(loaded, 16 * NLOAD)
            dve.wait_ge(ident_ready, 12)
            chain(nc.vector.memset(lns_bc[:, F:F + 1], 1.0))
            chain(nc.vector.tensor_tensor(g13_bc[:, :], gate_rows[:, 0, :], gate_rows[:, 2, :], ALU.add))
            chain(nc.vector.tensor_tensor(g23_bc[:, :], gate_rows[:, 1, :], gate_rows[:, 2, :], ALU.subtract))
            for c in range(C):
                chain(nc.vector.reduce_sum(wmean[:, c:c + 1], wskip_sb[:, c, 0:F], AX.X))
                chain(nc.vector.tensor_scalar(wmean[:, c:c + 1], wmean[:, c:c + 1], 1.0 / F, None, ALU.mult))
                chain(nc.vector.tensor_scalar(wd_sb[:, c, 0:F], wskip_sb[:, c, 0:F], wmean[:, c:c + 1], None, ALU.subtract))
                chain(nc.vector.tensor_tensor_reduce(out=setup_scr[:, :], in0=wskip_sb[:, c, 0:F], in1=g13_bc[:, :], scale=1.0,
                                                     scalar=0.0, op0=ALU.mult, op1=ALU.add, accum_out=wd_sb[:, c, F:F + 1]))
            chain(nc.vector.reduce_sum(wmean[:, C:C + 1], bskip_bc[:, :], AX.X))
            chain(nc.vector.tensor_scalar(wmean[:, C:C + 1], wmean[:, C:C + 1], 1.0 / F, None, ALU.mult))
            bd = WB['d']
            chain(nc.vector.tensor_scalar(bias_row[:, bd:bd + F], bskip_bc[0:3, :], wmean[0:3, C:C + 1], None, ALU.subtract))
            chain(nc.vector.tensor_tensor_reduce(out=setup_scr[:, :], in0=bskip_bc[:, :], in1=g13_bc[:, :], scale=1.0,
                                                 scalar=0.0, op0=ALU.mult, op1=ALU.add, accum_out=wmean[:, C:C + 1]))
            chain(nc.vector.tensor_tensor(bias_row[:, bd + F:bd + F + 1], wmean[0:3, C:C + 1], bgate_bc[0:3, :], ALU.add))
            for c in range(C):
                chain(nc.vector.tensor_copy(wskip_sb[:, c, F:F + 1], wd_sb[:, c, F:F + 1]))
                chain(nc.vector.tensor_tensor(setup_scr[:, :].rearrange("p (h d) -> p h d", h=H), wv_sb[:, c, :, 0:D],
                                              g23_bc[:, :].rearrange("p (h d) -> p h d", h=H), ALU.mult))
                chain(nc.vector.reduce_sum(wv_sb[:, c, :, D], setup_scr[:, :].rearrange("p (h d) -> p h d", h=H), AX.X))
            chain(nc.vector.tensor_tensor(setup_scr[:, :], bv_bc[:, :], g23_bc[:, :], ALU.mult))
            chain(nc.vector.reduce_sum(ubias[:, :], setup_scr[:, :].rearrange("p (h d) -> p h d", h=H), AX.X))
            bv_row = bias_row[:, WB['v']:WB['v'] + H * (D + 1)].rearrange("p (h d) -> p h d", h=H)
            for row, val in ((bias_row[:, 0:F], bq_bc[0:3, :]), (bias_row[:, WB['k']:WB['k'] + F], bk_bc[0:3, :]),
                             (bv_row[:, :, 0:D], bv_bc[0:3, :].rearrange("p (h d) -> p h d", h=H)), (bv_row[:, :, D], ubias[0:3, :]),
                             (bias_row[:, WB['s']:WB['s'] + F], bskip_bc[0:3, :]),
                             (bias_row[:, WB['s'] + F:WB['s'] + F + 1], bias_row[:, bd + F:bd + F + 1])):
                chain(nc.vector.tensor_copy(row, val))
            chain(nc.vector.tensor_copy(bias_part[:, 0, :], bias_row))
            chain(nc.vector.tensor_tensor(bias_left, bias_row, bias_part[:, 0, :], ALU.subtract))
            chain(nc.vector.tensor_copy(bias_part[:, 1, :], bias_left))
            chain(nc.vector.tensor_tensor(bias_left, bias_left, bias_part[:, 1, :], ALU.subtract))
            chain(nc.vector.tensor_copy(bias_part[:, 2, :], bias_left))
            chain(nc.vector.tensor_scalar(bias_sel, bias_part[:, 0, :], ident[0:3, 0:1], None, ALU.mult))
            chain(nc.vector.scalar_tensor_tensor(out=bias_sel, in0=bias_part[:, 1, :], scalar=ident[0:3, 1:2],
                                                 in1=bias_sel, op0=ALU.mult, op1=ALU.add))
            nc.vector.scalar_tensor_tensor(out=bias3[:, :], in0=bias_part[:, 2, :], scalar=ident[0:3, 2:3],
                                           in1=bias_sel, op0=ALU.mult, op1=ALU.add).then_inc(setup_done, 1)
            chain(nc.vector.tensor_scalar(negalpha_bc[:, :], alpha_bc[:, :], -1.0, None, ALU.mult))
            chain(nc.vector.memset(v_ring[:, :, :, 0], 1.0))
            chain(nc.vector.memset(seg_mask[:, :], 0.0))
            chain(nc.vector.memset(seg_maxT[:, :], 0.0))
            chain(nc.vector.memset(state[:, 1, R - 1, :], 0.0))
            chain(nc.vector.memset(maxes[:, 1, R - 1, :], 0.0))

            dve.wait_ge(edges_loaded, 16 * 6)
            SRC, DST, DSTROW, OUTROW, EQNEXT = range(5)
            chain(nc.vector.tensor_copy(nat_f[:, SRC, :], nat_i[:, 0, :]))
            chain(nc.vector.tensor_copy(nat_f[:, DST, :], nat_i[:, 1, :]))
            chain(nc.vector.tensor_copy(nat_f[:, DSTROW, :], nat_i[:, 2, :]))
            chain(nc.vector.tensor_tensor(nat_f[:, EQNEXT, :], nat_f[:, DST, :], nat_f[:, DSTROW, :], ALU.is_equal))
            chain(nc.vector.scalar_tensor_tensor(out=nat_f[:, OUTROW, :], in0=nat_f[:, EQNEXT, :], scalar=SKIP_ROW,
                                                 in1=nat_f[:, DST, :], op0=ALU.mult, op1=ALU.add))
            nc.vector.tensor_scalar(nat_f[:, DSTROW, :], nat_f[:, DST, :], float(N - 1), None, ALU.min).then_inc(table_step, 1)
            dve.wait_ge(table_ps_ready, 1)

            def column(n, h):
                return y_ps[:, n % 4, (n // 4) * 256 + h * 128:(n // 4) * 256 + h * 128 + HALF]

            for h in range(2):
                tiles = rows_idx[:, :, :].rearrange("p g (n r) -> p g n r", n=3)
                for n, k in ((SRC, 0), (DSTROW, 1), (OUTROW, 2)):
                    for q in range(R // 2):
                        chain(nc.vector.tensor_copy(tiles[:, :, k, 2 * q + h], column(n, h)[:, q:HALF:R // 2]))
                chain(nc.vector.tensor_copy(key_cols[:, 1 + h:1 + TP:2], column(DST, h)))
                chain(nc.vector.tensor_copy(eq_cols[:, h:TP:2], column(EQNEXT, h)))
            key_g = key_cols[:, 1:1 + TP].rearrange("p (g r) -> p g r", r=R)
            chain(nc.vector.tensor_copy(meta[:, :, 0:R], key_g))
            for r in range(R):
                for h in range(H):
                    chain(nc.vector.tensor_copy(meta[:, :, 2 * R + r * H + h],
                                                eq_cols[:, :].rearrange("p (g r) -> p g r", r=R)[:, :, r]))
            nc.vector.memset(wait_mark[:, :], 0.0).then_inc(table_step, 1)
            dve.wait_ge(table_ps_ready, 2)
            last_key = y_ps[:, 0, 0:TP].rearrange("p (g r) -> p g r", r=R)
            chain(nc.vector.tensor_tensor(meta[:, :, R:2 * R], key_g, last_key, ALU.not_equal))
            nc.vector.tensor_scalar(meta[:, :, R:2 * R], meta[:, :, R:2 * R], -BIG, None, ALU.mult).then_inc(table_ready, 1)
            dve.wait_ge(table_ready, 1)

            def x_stats(k, j):
                b = j % 2
                dve.wait_ge(x_loaded[j % XS], 16 * (turns(k, j, XS, 0) + 1))
                for r in range(R):
                    last = nc.vector.bn_stats(xstats[:, b, r, :], xt[:, j % XS, r * F:(r + 1) * F])
                last.then_inc(xstats_ready, 1)
                dve.wait_ge(xstats_ready, k + 1)
                nc.vector.memset(wait_mark[:, :], 0.0)
                for r in range(R):
                    last = nc.vector.bn_aggr(xmv[:, b, r, :], xstats[:, b, r, :])
                last.then_inc(xmv_ready, 1)

            def x_norm(k, j):
                b = j % 2
                dve.wait_ge(xrstd_ready, k + 1)
                if not isinstance(k, int) or k >= 2:
                    dve.wait_ge(hTps_ready, 2 * (k - 1))
                for r in range(R):
                    last = nc.vector.tensor_scalar(xn[:, b, r * F:(r + 1) * F], xt[:, j % XS, r * F:(r + 1) * F],
                                                   xmv[:, b, r, 0:1], xrstd[:, b, r:r + 1], ALU.subtract, ALU.mult)
                last.then_inc(xn_ready, 1)

            def step(k, j):
                if live(k, 2):
                    x_stats(k + 2, j + 2)
                if live(k, 0):
                    for half in range(2):
                        dve.wait_ge(ysq_ready, 4 * k + 2 * half + 2)
                        sl = slice(2 * half, 2 * half + 2)
                        nc.vector.tensor_tensor(wy[:, j % 2, sl, :], y_ps[:, sl, 0:F + 1],
                                                lns_bc[:, None, :].to_broadcast([P, 2, F + 1]), ALU.mult).then_inc(yscaled, 1)
                if live(k, 2):
                    x_norm(k + 2, j + 2)
                if live(k, -1):
                    s = (j - 1) % US
                    dve.wait_ge(yscale_ready, 2 * k)
                    dve.wait_ge(yscaled, 2 * k)
                    if not isinstance(k, int) or k - 1 >= US:
                        dve.wait_ge(u_stored[s], 16 * turns(k, j, US, -1))
                    for r in range(R):
                        last = nc.vector.scalar_tensor_tensor(out=ut[:, s, r * F:(r + 1) * F], in0=wy[:, (j - 1) % 2, r, 0:F],
                                                              scalar=yscale[:, (j - 1) % 2, r:r + 1], in1=lnb_bc[:, :],
                                                              op0=ALU.mult, op1=ALU.add)
                    last.then_inc(u_ready, 1)
                    dve.wait_ge(u_ready, k)
                    if not isinstance(k, int) or k >= 3:
                        dve.wait_ge(prelu_ready, k - 2)
                    nc.vector.tensor_scalar(neg[:, (j - 1) % 2, :], ut[:, s, :], 0.0, alpha_bc[:, 0:1],
                                            ALU.min, ALU.mult).then_inc(neg_ready, 1)

            for k in range(2):
                x_stats(k, k)
                x_norm(k, k)
            steady(dve, step, 0, BLOCKS + 1)

            def edge_stats(g, j):
                b = j % 2
                dve.wait_ge(src_loaded[j % 4], 16 * R * (e_turns(g, j, 4, 0) + 1))
                dve.wait_ge(dst_loaded[j % XS], 16 * R * (e_turns(g, j, XS, 0) + 1))
                for r in range(R):
                    nc.vector.bn_stats(estats[:, b, r, :], xsrc[:, j % 4, r * F:(r + 1) * F])
                for r in range(R):
                    last = nc.vector.bn_stats(estats[:, b, R + r, :], xt[:, j % XS, r * F:(r + 1) * F])
                last.then_inc(e_stats_ready, 1)
                dve.wait_ge(e_stats_ready, g + 1)
                nc.vector.memset(wait_mark[:, :], 0.0)
                for r in range(2 * R):
                    last = nc.vector.bn_aggr(emv[:, b, r, :], estats[:, b, r, :])
                last.then_inc(e_mv_ready, 1)

            def edge_norm(g, j):
                b = j % 2
                dve.wait_ge(e_rstd_ready, g + 1)
                if e_past(g, -1):
                    dve.wait_ge(e_hTps_ready, R * g)
                for r in range(2 * R):
                    rows = xsrc[:, j % 4, :] if r < R else xt[:, j % XS, :]
                    c = r % R
                    last = nc.vector.tensor_scalar(xn[:, r // R, c * F:(c + 1) * F], rows[:, c * F:(c + 1) * F],
                                                   emv[:, b, r, 0:1], erstd[:, b, r:r + 1], ALU.subtract, ALU.mult)
                last.then_inc(e_xn_ready, 1)

            def edge_meta(g, j):
                rows = meta[:, g, :] if isinstance(g, int) else meta[:, bass.ds(g, 1), :].rearrange("p a b -> p (a b)")
                nc.vector.tensor_copy(meta_b[:, j % 2, :], rows).then_inc(e_meta_ready, 1)

            def edge_product(g, j, r):
                dve.wait_ge(e_q_copied, R * g + r + 1)
                nc.vector.tensor_tensor(prod[:, r, :], q_sb[:, r % 2, :], k_ps, ALU.mult).then_inc(e_prod_ready, 1)

            def edge_score(g, j):
                dve.wait_ge(e_prod_ready, R * g + R)
                nc.vector.reduce_sum(score[:, j % 2, :], prod[:, :, :].rearrange("p r (h d) -> p (r h) d", h=H),
                                     AX.X).then_inc(e_score_ready, 1)

            def edge_scan(g, j):
                dve.wait_ge(e_scoreT_ready, g + 1)
                nc.vector.tensor_scalar(seg_mask[:, 1:P + 1], eqT_ps, 1.0, BIG, ALU.subtract, ALU.mult).then_inc(e_scan, 1)
                dve.wait_ge(e_scan, 2 * g + 1)
                nc.vector.tensor_tensor_scan(run_max[:, :], seg_mask[:, 0:P], scoreT_ps, -BIG, ALU.add, ALU.max).then_inc(e_scan, 1)
                dve.wait_ge(e_scan, 2 * g + 2)
                nc.vector.tensor_tensor_scan(seg_maxT[0:R * H, ::-1], seg_mask[:, P:0:-1], run_max[:, ::-1], -BIG,
                                             ALU.add, ALU.max).then_inc(e_tmax_ready, 1)

            def edge_tile_max(g, j):
                dve.wait_ge(e_tmax_ps_ready, g + 1)
                nc.vector.tensor_copy(tile_max[:, :], tmax_ps[:, 0:R * H]).then_inc(e_tmax_ready, 1)
                dve.wait_ge(e_keyrow_ready, g + 1)
                nc.vector.tensor_tensor(same[:, j % 2, :].rearrange("p (r e) -> p r e", r=R),
                                        keyrow_ps.rearrange("p (r e) -> p r e", r=R),
                                        meta_b[:, j % 2, 0:R].unsqueeze(2).to_broadcast([P, R, P]), ALU.is_equal).then_inc(e_same_ready, 1)

            def edge_max(g, j, r):
                dve.wait_ge(e_cmax_ps_ready, R * g + r + 1)
                if r == 0:
                    dve.wait_ge(e_tmax_ready, 2 * g + 2)
                nc.vector.tensor_tensor(carry_max[:, r, :], cmax_ps, meta_b[:, j % 2, R + r:R + r + 1].to_broadcast([P, H]), ALU.add).then_inc(e_cmax_ready, 1)
                dve.wait_ge(e_cmax_ready, R * g + r + 1)
                nc.vector.tensor_tensor(maxes[:, j % 2, r, :], tile_max[:, r * H:(r + 1) * H], carry_max[:, r, :],
                                        ALU.max).then_inc(e_max_ready, 1)

            def edge_exponents(g, j):
                dve.wait_ge(e_max_ready, R * g + R)
                m = maxes[:, j % 2, :, :].rearrange("p r h -> p (r h)")
                nc.vector.tensor_tensor(expo[:, 0, :], score[:, j % 2, :], m, ALU.subtract)
                nc.vector.tensor_tensor(expo[:, 1, :], carry_max[:, :, :].rearrange("p r h -> p (r h)"), m,
                                        ALU.subtract).then_inc(e_expo_ready, 1)

            def edge_values(g, j):
                dve.wait_ge(e_aw_ready, g + 1)
                dve.wait_ge(e_vsk_copied, 2 * (R * g + R))
                if e_past(g, -1):
                    dve.wait_ge(e_agg_ps_ready, R * g)
                nc.vector.tensor_tensor(vals[:, :, :].rearrange("p r (h v) -> p (r h) v", h=H), v_ring[:, j % 4, :, :],
                                        aw[:, j % 2, 0, :].unsqueeze(2).to_broadcast([P, R * H, V]), ALU.mult).then_inc(e_vals_ready, 1)

            def edge_aggregate(g, j, r):
                dve.wait_ge(e_agg_ps_ready, R * g + r + 1)
                nc.vector.tensor_tensor(carried[:, :].rearrange("p (h v) -> p h v", h=H),
                                        carry_ps[:, 0:H * V].rearrange("p (h v) -> p h v", h=H),
                                        aw[:, j % 2, 1, r * H:(r + 1) * H].unsqueeze(2).to_broadcast([P, H, V]),
                                        ALU.mult).then_inc(e_carried, 1)
                dve.wait_ge(e_carried, R * g + r + 1)
                nc.vector.tensor_tensor(state[:, j % 2, r, :], agg_ps[:, 0:H * V], carried[:, :], ALU.add).then_inc(e_state_ready, 1)

            def edge_logit(g, j):
                st = state[:, j % 2, :, :].rearrange("p r (h v) -> p (r h) v", h=H)
                dve.wait_ge(e_state_ready, R * g + R)
                nc.vector.reciprocal(rden[:, :], st[:, :, 0]).then_inc(e_gstep, 1)
                dve.wait_ge(e_gstep, 6 * g + 1)
                nc.vector.tensor_tensor(ugate[:, :], st[:, :, V - 1], rden[:, :], ALU.mult).then_inc(e_gstep, 1)
                dve.wait_ge(e_gstep, 6 * g + 2)
                nc.vector.reduce_sum(logit[:, :], ugate[:, :].rearrange("p (r h) -> p r h", h=H), AX.X).then_inc(e_gstep, 1)
                dve.wait_ge(e_gstep, 6 * g + 3)
                nc.vector.tensor_tensor(logit[:, :], logit[:, :], sk_ring[:, j % 4, :, F], ALU.add).then_inc(e_logit_ready, 1)

            def edge_mix(g, j):
                st = state[:, j % 2, :, :].rearrange("p r (h v) -> p (r h) v", h=H)
                dve.wait_ge(e_eexp_ready, g + 1)
                nc.vector.tensor_scalar(egt[:, :], eexp[:, j % 2, :], 1.0, None, ALU.add).then_inc(e_gstep, 1)
                dve.wait_ge(e_gstep, 6 * g + 4)
                nc.vector.reciprocal(egt[:, :], egt[:, :]).then_inc(e_gstep, 1)
                dve.wait_ge(e_gstep, 6 * g + 5)
                nc.vector.tensor_scalar(omg[:, :], egt[:, :], -1.0, 1.0, ALU.mult, ALU.add).then_inc(e_gstep, 1)
                dve.wait_ge(e_gstep, 6 * g + 6)
                nc.vector.tensor_tensor(coef[:, :].rearrange("p (r h) -> p r h", h=H), rden[:, :].rearrange("p (r h) -> p r h", h=H),
                                        omg[:, :].unsqueeze(2).to_broadcast([P, R, H]), ALU.mult).then_inc(e_mix, 1)
                dve.wait_ge(e_mix, 4 * g + 1)
                nc.vector.tensor_tensor(mix.rearrange("p r (h d) -> p r h d", h=H),
                                        st[:, :, 1:D + 1].rearrange("p (r h) d -> p r h d", h=H),
                                        coef[:, :].rearrange("p (r h) -> p r h", h=H).unsqueeze(3).to_broadcast([P, R, H, D]),
                                        ALU.mult).then_inc(e_mix, 1)
                dve.wait_ge(e_mix, 4 * g + 2)
                for r in range(R):
                    last = nc.vector.scalar_tensor_tensor(out=mix[:, r, :], in0=sk_ring[:, j % 4, r, 0:F], scalar=egt[:, r:r + 1],
                                                          in1=mix[:, r, :], op0=ALU.mult, op1=ALU.add)
                last.then_inc(e_mix, 1)
                dve.wait_ge(e_mix, 4 * g + 3)
                for r in range(R):
                    last = nc.vector.bn_stats(mstats[:, r, :], mix[:, r, :])
                last.then_inc(e_mix, 1)
                dve.wait_ge(e_mix, 4 * g + 4)
                nc.vector.memset(wait_mark[:, :], 0.0)
                for r in range(R):
                    last = nc.vector.bn_aggr(mmv[:, r, :], mstats[:, r, :])
                last.then_inc(e_mmv_ready, 1)

            def edge_layernorm(g, j):
                s = j % US
                dve.wait_ge(e_mmv_ready, g + 1)
                for r in range(R):
                    last = nc.vector.scalar_tensor_tensor(out=mix[:, r, :], in0=mix[:, r, :], scalar=mmv[:, r, 0:1],
                                                          in1=lns_bc[:, 0:F], op0=ALU.subtract, op1=ALU.mult)
                last.then_inc(e_u0, 1)
                dve.wait_ge(e_u0, g + 1)
                dve.wait_ge(e_mrstd_ready, g + 1)
                if e_past(g, -US):
                    dve.wait_ge(scattered[s], 16 * R * e_turns(g, j, US, 0))
                for r in range(R):
                    last = nc.vector.scalar_tensor_tensor(out=ut[:, s, r * F:(r + 1) * F], in0=mix[:, r, :],
                                                          scalar=mrstd[:, r:r + 1], in1=lnb_bc[:, :], op0=ALU.mult, op1=ALU.add)
                last.then_inc(e_u_ready, 1)

            def edge_prelu(g, j):
                dve.wait_ge(e_relu_ready, 2 * g + 2)
                nc.vector.scalar_tensor_tensor(out=ut[:, j % US, :], in0=neg[:, j % 2, :], scalar=negalpha_bc[:, 0:1],
                                               in1=pos[:, j % 2, :], op0=ALU.mult, op1=ALU.add).then_inc(e_prelu_ready, 1)

            def e_step(g, j):
                if e_live(g, -3):
                    edge_logit(g - 3, j - 3)
                if e_live(g, -2):
                    edge_values(g - 2, j - 2)
                if e_live(g, 0):
                    edge_meta(g, j)
                if e_live(g, 1):
                    edge_stats(g + 1, j + 1)
                if e_live(g, -1):
                    edge_scan(g - 1, j - 1)
                if e_live(g, 0):
                    edge_product(g, j, 0)
                if e_live(g, -2):
                    edge_aggregate(g - 2, j - 2, 0)
                if e_live(g, -1):
                    edge_tile_max(g - 1, j - 1)
                if e_live(g, 0):
                    edge_product(g, j, 1)
                if e_live(g, -1):
                    edge_max(g - 1, j - 1, 0)
                if e_live(g, -3):
                    edge_mix(g - 3, j - 3)
                if e_live(g, -2):
                    edge_aggregate(g - 2, j - 2, 1)
                if e_live(g, -1):
                    edge_max(g - 1, j - 1, 1)
                if e_live(g, 0):
                    edge_product(g, j, 2)
                if e_live(g, -1):
                    edge_max(g - 1, j - 1, 2)
                if e_live(g, 1):
                    edge_norm(g + 1, j + 1)
                if e_live(g, -2):
                    edge_aggregate(g - 2, j - 2, 2)
                if e_live(g, -1):
                    edge_max(g - 1, j - 1, 3)
                    edge_exponents(g - 1, j - 1)
                if e_live(g, 0):
                    edge_product(g, j, 3)
                if e_live(g, -3):
                    edge_layernorm(g - 3, j - 3)
                if e_live(g, -2):
                    edge_aggregate(g - 2, j - 2, 3)
                if e_live(g, 0):
                    edge_score(g, j)
                if e_live(g, -4):
                    edge_prelu(g - 4, j - 4)

            edge_stats(0, 0)
            edge_norm(0, 0)
            e_steady(dve, e_step, 0, G + 4)

        @block.scalar
        def _(act):
            act.wait_ge(loaded, 16 * NLOAD)

            def relu_transposed(k, b):
                if not isinstance(k, int) or k >= 2:
                    act.wait_ge(y_ready, 2 * (k - 1))
                for half in range(2):
                    act.wait_ge(hTps_ready, 2 * k + half + 1)
                    nc.scalar.activation(hT[:, b, half * 512:(half + 1) * 512], hT_ps[:, half, :], ACT.Relu).then_inc(hT_ready, 1)

            def step(k, j):
                if live(k, 1):
                    relu_transposed(k + 1, (j + 1) % 2)
                if live(k, 0):
                    for r in range(R):
                        if r % 2 == 0:
                            act.wait_ge(y_ready, 2 * k + r // 2 + 1)
                        nc.scalar.activation(sq_scr[:, r, :], y_ps[:, r, 0:F], ACT.Square, scale=F ** -0.5,
                                             accum_out=ssq[:, j % 2, r:r + 1]).then_inc(ysq_ready, 1)
                    act.wait_ge(yscaled, 2 * k + 2)
                    nc.scalar.activation(egate[:, j % 2, :], wy[:, j % 2, :, F], ACT.Exp, scale=-1.0).then_inc(egate_ready, 1)
                if live(k, -1):
                    act.wait_ge(u_ready, k)
                    if not isinstance(k, int) or k >= 3:
                        act.wait_ge(prelu_ready, k - 2)
                    s = (j - 1) % US
                    nc.scalar.activation(pos[:, (j - 1) % 2, :], ut[:, s, :], ACT.Relu).then_inc(pos_ready, 1)

            relu_transposed(0, 0)
            steady(act, step, 0, BLOCKS + 1)

            def edge_relu(t, b):
                act.wait_ge(e_hTps_ready, t + 1)
                nc.scalar.activation(hT[:, b, 0:512], ehT_ps, ACT.Relu).then_inc(e_hT_ready, 1)

            def e_step(g, j):
                for r in range(R):
                    t = g * R + r
                    if e_live(g, 0):
                        if r < R - 1 or e_live(g, 1):
                            if e_past(g, -1) or r >= 1:
                                act.wait_ge(e_vsk_ps_ready, t)
                            edge_relu(t + 1, (r + 1) % 2)
                        act.wait_ge(e_qk_ps_ready, t + 1)
                        if e_past(g, -1) or r >= 2:
                            act.wait_ge(e_prod_ready, t - 1)
                        nc.scalar.copy(q_sb[:, r % 2, :], q_ps).then_inc(e_q_copied, 1)
                        act.wait_ge(e_vsk_ps_ready, t + 1)
                        if r == 0 and e_past(g, -4):
                            act.wait_ge(e_vals_ready, g - 3)
                            act.wait_ge(e_mmv_ready, g - 3)
                        nc.scalar.copy(v_ring[:, j % 4, r * H:(r + 1) * H, 1:V], v_ps.rearrange("p (h v) -> p h v", h=H)).then_inc(e_vsk_copied, 1)
                        nc.scalar.copy(sk_ring[:, j % 4, r, :], sk_ps).then_inc(e_vsk_copied, 1)
                    if r == 0 and e_live(g, -3):
                        act.wait_ge(e_logit_ready, g - 2)
                        nc.scalar.activation(eexp[:, (j - 3) % 2, :], logit[:, :], ACT.Exp, scale=-1.0).then_inc(e_eexp_ready, 1)
                    if r == 0 and e_live(g, -4):
                        act.wait_ge(e_u_ready, g - 3)
                        if e_past(g, -6):
                            act.wait_ge(e_prelu_ready, g - 5)
                        u = ut[:, (j - 4) % US, :]
                        nc.scalar.activation(pos[:, j % 2, :], u, ACT.Relu).then_inc(e_relu_ready, 1)
                        nc.scalar.activation(neg[:, j % 2, :], u, ACT.Relu, scale=-1.0).then_inc(e_relu_ready, 1)
                if e_live(g, -1):
                    act.wait_ge(e_expo_ready, g)
                    nc.scalar.activation(aw[:, (j - 1) % 2, :, :], expo[:, :, :], ACT.Exp, scale=SCORE_SCALE).then_inc(e_aw_ready, 1)

            edge_relu(0, 0)
            e_steady(act, e_step, 0, G + 4)

        @block.tensor
        def _(pe):
            pe.wait_ge(ident_ready, 12)
            pe.wait_ge(table_step, 2)
            for n in range(5):
                for h in range(2):
                    at = (n // 4) * 256 + h * 128
                    last = nc.tensor.transpose(y_ps[:, n % 4, at:at + HALF], nat_f[:, n, h * P:(h + 1) * P], ident[0:HALF, 0:HALF])
            last.then_inc(table_ps_ready, 1)
            pe.wait_ge(table_step, 3)
            nc.tensor.matmul(y_ps[:, 0, 0:TP], last_row[:, :], key_cols[:, 0:TP], start=True, stop=True).then_inc(table_ps_ready, 1)
            pe.wait_ge(table_ready, 1)
            pe.wait_ge(setup_done, 1)

            def transposes(k, b):
                pe.wait_ge(xn_ready, k + 1)
                for half in range(2):
                    if not isinstance(k, int) or k >= 1:
                        pe.wait_ge(hT_ready, 2 * (k - 1) + half + 1)
                    for q in range(4):
                        c = 4 * half + q
                        last = nc.tensor.transpose(hT_ps[:, half, q * P:(q + 1) * P], xn[:, b, c * P:(c + 1) * P], ident[:, :])
                    last.then_inc(hTps_ready, 1)

            def project(k, b):
                for r in range(R):
                    if r % 2 == 0:
                        pe.wait_ge(hT_ready, 2 * k + r // 2 + 1)
                        if not isinstance(k, int) or k >= 1:
                            pe.wait_ge(yscaled, 2 * (k - 1) + r // 2 + 1)
                    nc.tensor.matmul(y_ps[:, r, 0:F + 1], ones3[:, :], bias3[:, WB["d"]:WB["d"] + F + 1], start=True, stop=False)
                    for c in range(C):
                        last = nc.tensor.matmul(y_ps[:, r, 0:F + 1], hT[:, b, (C * r + c) * P:(C * r + c + 1) * P],
                                                wd_sb[:, c, :], start=False, stop=(c == C - 1))
                    if r % 2 == 1:
                        last.then_inc(y_ready, 1)

            def step(k, j):
                if live(k, 1):
                    transposes(k + 1, (j + 1) % 2)
                if live(k, 0):
                    project(k, j % 2)

            transposes(0, 0)
            steady(pe, step, 0, BLOCKS)

            def edge_transposes(g, r, xb):
                t = g * R + r
                pe.wait_ge(e_xn_ready, g + 1)
                if e_past(g, -1) or r >= 1:
                    pe.wait_ge(e_hT_ready, t)
                for side in range(2):
                    for c in range(C):
                        last = nc.tensor.transpose(ehT_ps[:, (side * C + c) * P:(side * C + c + 1) * P],
                                                   xn[:, side, (C * r + c) * P:(C * r + c + 1) * P], ident[:, :])
                last.then_inc(e_hTps_ready, 1)

            def project_edges(out_ps, side, r, weights, at, n):
                nc.tensor.matmul(out_ps, ones3[:, :], bias3[:, at:at + n], start=True, stop=False)
                for c in range(C):
                    last = nc.tensor.matmul(out_ps, hT[:, r % 2, (side * C + c) * P:(side * C + c + 1) * P], weights[c],
                                            start=False, stop=(c == C - 1))
                return last

            def score_rows(g, j):
                pe.wait_ge(e_score_ready, g + 1)
                pe.wait_ge(e_meta_ready, g + 1)
                if e_past(g, -1):
                    pe.wait_ge(e_max_ready, R * g)
                nc.tensor.transpose(scoreT_ps, score[:, j % 2, :], ident[:, :])
                nc.tensor.transpose(eqT_ps, meta_b[:, j % 2, 2 * R:META], ident[:, :]).then_inc(e_scoreT_ready, 1)

            def tile_maxima(g, j):
                pe.wait_ge(e_tmax_ready, 2 * g + 1)
                nc.tensor.transpose(tmax_ps, seg_maxT[:, :], ident[:, :]).then_inc(e_tmax_ps_ready, 1)
                if e_past(g, -1):
                    pe.wait_ge(e_same_ready, g)
                for r in range(R):
                    last = nc.tensor.transpose(keyrow_ps[:, r * P:(r + 1) * P], meta_b[:, j % 2, r:r + 1].to_broadcast([P, P]), ident[:, :])
                last.then_inc(e_keyrow_ready, 1)

            def carried_max(g, j, r):
                if r == 0:
                    pe.wait_ge(e_tmax_ready, 2 * g + 2)
                if e_past(g, -1) or r >= 1:
                    pe.wait_ge(e_max_ready, R * g + r)
                prev = maxes[:, (j - (r == 0)) % 2, (r - 1) % R, :]
                nc.tensor.matmul(cmax_ps, last_row[:, :], prev, start=True, stop=True).then_inc(e_cmax_ps_ready, 1)

            def aggregate(g, j, r):
                pe.wait_ge(e_vals_ready, g + 1)
                pe.wait_ge(e_same_ready, g + 1)
                if e_past(g, -1) or r >= 1:
                    pe.wait_ge(e_state_ready, R * g + r)
                nc.tensor.matmul(agg_ps[:, 0:H * V], same[:, j % 2, r * P:(r + 1) * P], vals[:, r, :], start=True, stop=True)
                prev = state[:, (j - (r == 0)) % 2, (r - 1) % R, :]
                nc.tensor.matmul(carry_ps[:, 0:H * V], last_row[:, :], prev, start=True, stop=True).then_inc(e_agg_ps_ready, 1)

            def e_step(g, j):
                for r in range(R):
                    t = g * R + r
                    if e_live(g, 0):
                        if r < R - 1:
                            edge_transposes(g, r + 1, 0)
                        elif e_live(g, 1):
                            edge_transposes(g + 1, 0, 0)
                        pe.wait_ge(e_hT_ready, t + 1)
                        if e_past(g, -1) or r >= 1:
                            pe.wait_ge(e_prod_ready, t)
                        project_edges(q_ps, 0, r, [wq_sb[:, c, :] for c in range(C)], WB['q'], F)
                        project_edges(k_ps, 1, r, [wk_sb[:, c, :] for c in range(C)], WB['k'], F).then_inc(e_qk_ps_ready, 1)
                    if r == 0 and e_live(g, -1):
                        score_rows(g - 1, j - 1)
                    if r == 1 and e_live(g, -1):
                        carried_max(g - 1, j - 1, 0)
                    if r == 2 and e_live(g, -1):
                        carried_max(g - 1, j - 1, 2)
                    if e_live(g, 0):
                        if e_past(g, -1) or r >= 1:
                            pe.wait_ge(e_vsk_copied, 2 * t)
                        project_edges(v_ps, 0, r, [wv_sb[:, c, :, :].rearrange("p h v -> p (h v)") for c in range(C)], WB['v'], H * (D + 1))
                        project_edges(sk_ps, 1, r, [wskip_sb[:, c, :] for c in range(C)], WB['s'], F + 1).then_inc(e_vsk_ps_ready, 1)
                    if e_live(g, -2):
                        aggregate(g - 2, j - 2, r)
                    if r == 0 and e_live(g, -1):
                        tile_maxima(g - 1, j - 1)
                    if r == 1 and e_live(g, -1):
                        carried_max(g - 1, j - 1, 1)
                    if r == 2 and e_live(g, -1):
                        carried_max(g - 1, j - 1, 3)

            edge_transposes(0, 0, 0)
            e_steady(pe, e_step, 0, G + 2)


_NAMES = ['x', 'src', 'dst', 'L0_gnn_Wq', 'L0_gnn_bq', 'L0_gnn_Wk', 'L0_gnn_bk', 'L0_gnn_Wv', 'L0_gnn_bv',
          'L0_gnn_Wskip', 'L0_gnn_bskip', 'L0_gnn_Wg', 'L0_gnn_bg', 'L0_gnn_ln_scale', 'L0_gnn_ln_bias',
          'L0_gnn_prelu_alpha']


def kernel(**inputs):
    import numpy as np
    import concourse.bacc as bacc
    from concourse.bass_utils import run_bass_kernel_spmd

    nc = bacc.Bacc("TRN2", target_bir_lowering=False, num_devices=1)
    arrays, args = {}, []
    for name in _NAMES:
        a = np.ascontiguousarray(inputs[name])
        if a.ndim == 0:
            a = a.reshape(1)
        arrays[f"in_{name}"] = a
        args.append(nc.dram_tensor(f"in_{name}", a.shape, mybir.dt.from_np(a.dtype), kind="ExternalInput").ap())
    shape = inputs['x'].shape
    args.append(nc.dram_tensor("out_rows", shape, mybir.dt.float32, kind="ExternalOutput").ap())
    gnn_layer(nc, *args)
    r = run_bass_kernel_spmd(nc, [arrays], core_ids=[0])
    return r.results[0]["out_rows"]
```

```python
import concourse.bass as bass
from concourse import mybir
from contextlib import ExitStack


def gnn_layer(nc, x, src, dst, w_q, b_q, w_k, b_k, w_v, b_v, w_skip, b_skip, w_gate, b_gate,
              ln_scale, ln_bias, prelu_alpha, out):
    fp32 = mybir.dt.float32
    bf16 = mybir.dt.bfloat16
    i32 = mybir.dt.int32
    ALU = mybir.AluOpType
    ACT = mybir.ActivationFunctionType
    AX = mybir.AxisListType

    P = 128
    N, F = x.shape
    C = F // P
    EPS = 1e-5
    R = 4
    ROWS = P * R
    BLOCKS = -(-N // ROWS)
    XS = 8
    US = 4
    AHEAD = 5
    MAIN = (BLOCKS - 1 - AHEAD) // XS

    E = src.shape[0]
    H = 4
    D = F // H
    V = D + 2
    T = -(-E // P)
    G = -(-T // R)
    TP = G * R
    HALF = TP // 2
    SCORE_SCALE = float(D) ** -0.5
    BIG = 1e30
    SKIP_ROW = float(1 << 20)
    META = 2 * R + R * H
    EU = 8
    EMAIN = (G - 2) // EU
    WB = dict(q=0, k=F, v=2 * F, s=2 * F + H * (D + 1), d=2 * F + H * (D + 1) + F + 1)
    BW = WB['d'] + F + 1

    def block_rows(tensor, k, j=None):
        if isinstance(k, int) and k == BLOCKS - 1:
            return tensor[N - ROWS:N, :].rearrange("(p r) f -> p (r f)", r=R)
        blocks = tensor[0:(BLOCKS - 1) * ROWS, :].rearrange("(n p r) f -> n p (r f)", p=P, r=R)
        if isinstance(k, int):
            return blocks[k, :, :]
        return blocks[bass.ds(k, 1), :, :].rearrange("n p m -> p (n m)")

    ctx = ExitStack()
    with ctx:
        def sb(name, shape, dt=fp32):
            return ctx.enter_context(nc.sbuf_tensor(name, shape, dt))

        def ps(name, shape, dt=fp32):
            return ctx.enter_context(nc.psum_tensor(name, shape, dt))

        def sem(name):
            return ctx.enter_context(nc.semaphore(name))

        wskip_sb = sb("wskip_sb", [P, C, F + 1])
        wq_sb = sb("wq_sb", [P, C, F])
        wk_sb = sb("wk_sb", [P, C, F])
        wv_sb = sb("wv_sb", [P, C, H, D + 1])
        bq_bc = sb("bq_bc", [P, F])
        bk_bc = sb("bk_bc", [P, F])
        bv_bc = sb("bv_bc", [P, F])
        g23_bc = sb("g23_bc", [P, F])
        negalpha_bc = sb("negalpha_bc", [P, 1])
        last_row = sb("last_row", [P, P])
        wd_sb = sb("wd_sb", [P, C, F + 1])
        gate_rows = sb("gate_rows", [P, 3, F])
        g13_bc = sb("g13_bc", [P, F])
        bskip_bc = sb("bskip_bc", [P, F])
        lns_bc = sb("lns_bc", [P, F + 1])
        lnb_bc = sb("lnb_bc", [P, F])
        alpha_bc = sb("alpha_bc", [P, 1])
        bgate_bc = sb("bgate_bc", [P, 1])
        ident = sb("ident", [P, P])
        ones3 = sb("ones3", [3, P], bf16)
        setup_scr = sb("setup_scr", [P, F])
        wmean = sb("wmean", [P, C + 1])
        ubias = sb("ubias", [P, H])
        bias3 = sb("bias3", [3, BW], bf16)
        nhalf = sb("nhalf", [P, 2 * R])
        one4 = sb("one4", [P, R])
        eps4 = sb("eps4", [P, 2 * R])

        xt = sb("xt", [P, XS, R * F])
        xn = sb("xn", [P, 2, R * F])
        hT = sb("hT", [P, 2, R * C * P])
        wy = sb("wy", [P, 2, R, F + 1])
        ut = sb("ut", [P, US, R * F])
        pos = sb("pos", [P, 2, R * F])
        neg = sb("neg", [P, 2, R * F])
        bias_row = pos[0:3, :, :].rearrange("p a b -> p (a b)")[:, 0:BW]
        bias_left = neg[0:3, :, :].rearrange("p a b -> p (a b)")[:, 0:BW]
        bias_sel = wy[0:3, :, :, :].rearrange("p a b c -> p (a b c)")[:, 0:BW]
        bias_part = ut[0:3, :, :].rearrange("p a b -> p (a b)").bitcast(bf16)[:, 0:3 * BW].rearrange("p (a b) -> p a b", a=3)

        key_cols = sb("key_cols", [P, TP + 1])
        eq_cols = sb("eq_cols", [P, TP])
        meta = sb("meta", [P, G, META])
        rows_idx = sb("rows_idx", [P, G, 3 * R], i32)
        meta_b = sb("meta_b", [P, 2, META])
        idx_b = sb("idx_b", [P, EU, 3 * R], i32)
        xsrc = sb("xsrc", [P, 2, R * F])
        emv = sb("emv", [P, 2, 2 * R, 2])
        estats = sb("estats", [P, 2, 2 * R, 6])
        erstd = sb("erstd", [P, 2, 2 * R])
        ebias = sb("ebias", [P, 2, 2 * R])
        qk_ring = sb("qk_ring", [P, 2, R, 2 * F])
        v_ring = sb("v_ring", [P, 4, R * H, V])
        sk_ring = sb("sk_ring", [P, 4, R, F + 1])
        edge_scratch = sk_ring[0:HALF, :, :, :].rearrange("p a b c -> p (a b c)")
        nat_f = edge_scratch[:, 0:10 * P].rearrange("p (n e) -> p n e", n=5)
        nat_i = edge_scratch[:, 10 * P:16 * P].bitcast(i32).rearrange("p (n e) -> p n e", n=3)
        score = sb("score", [P, 2, R * H])
        seg_mask = sb("seg_mask", [R * H, P + 1])
        run_max = sb("run_max", [R * H, P])
        seg_maxT = sb("seg_maxT", [P, P])
        tile_max = sb("tile_max", [P, R * H])
        same = sb("same", [P, 2, R * P])
        carry_max = sb("carry_max", [P, R, H])
        maxes = sb("maxes", [P, 2, R, H])
        expo = sb("expo", [P, 2, R * H])
        aw = sb("aw", [P, 2, 2, R * H])
        vals = sb("vals", [P, R, H * V])
        carried = sb("carried", [P, H * V])
        state = sb("state", [P, 2, R, H * V])
        rden = sb("rden", [P, R * H])
        ugate = sb("ugate", [P, R * H])
        logit = sb("logit", [P, R])
        eexp = sb("eexp", [P, 2, R])
        egt = sb("egt", [P, R])
        omg = sb("omg", [P, R])
        coef = sb("coef", [P, R * H])
        mix = wy[:, 0, :, 0:F]
        mixn = wy[:, 1, :, 0:F]
        mbias = sb("mbias", [P, R])
        mstats = sb("mstats", [P, R, 6])
        mmv = sb("mmv", [P, R, 2])
        mrstd = sb("mrstd", [P, R])
        xstats = sb("xstats", [P, 2, R, 6])
        xmv = sb("xmv", [P, 2, R, 2])
        xrstd = sb("xrstd", [P, 2, R])
        pool_mark = sb("pool_mark", [P, 2, EU])
        wait_mark = sb("wait_mark", [P, 1])
        sq_scr = sb("sq_scr", [P, R, F])
        ssq = sb("ssq", [P, 2, R])
        egate = sb("egate", [P, 2, R])
        root_eps = sb("root_eps", [P, 1])
        xbias = sb("xbias", [P, 2, R])
        gate2 = sb("gate2", [P, 2, R])
        yscale = sb("yscale", [P, 2, R])


        hT_ps = ps("hT_ps", [P, 2, 512])
        y_ps = ps("y_ps", [P, R, 512])
        agg_ps = ps("agg_ps", [P, 512])
        carry_ps = ps("carry_ps", [P, 512])
        ehT_ps = hT_ps[:, 0, :]
        qk_ps = y_ps[:, 0, :]
        v_ps = y_ps[:, 1, 0:H * (D + 1)]
        sk_ps = y_ps[:, 2, 0:F + 1]
        keyrow_ps = y_ps[:, 3, :]
        scoreT_ps = hT_ps[0:R * H, 1, 0:P]
        eqT_ps = hT_ps[0:R * H, 1, P:2 * P]
        tmax_ps = hT_ps[:, 1, 2 * P:3 * P]
        cmax_ps = hT_ps[:, 1, 3 * P:3 * P + H]

        loaded = sem("weights_loaded")
        ident_ready = sem("ident_ready")
        setup_step = sem("setup_step")
        setup_done = sem("setup_done")
        x_loaded = [sem(f"x_loaded{s}") for s in range(XS)]
        u_stored = [sem(f"u_stored{s}") for s in range(US)]
        xstats_ready = sem("xstats_ready")
        xmv_ready = sem("xmv_ready")
        xvar_ready = sem("xvar_ready")
        xrstd_ready = sem("xrstd_ready")
        xbias_ready = sem("xbias_ready")
        e_xbias_ready = sem("e_xbias_ready")
        xn_ready = sem("xn_ready")
        hTps_ready = sem("hTps_ready")
        hT_ready = sem("hT_ready")
        y_ready = sem("y_ready")
        ysq_ready = sem("ysq_ready")
        egate_ready = sem("egate_ready")
        yscaled = sem("yscaled")
        gstep = sem("gstep")
        yscale_ready = sem("yscale_ready")
        u_ready = sem("u_ready")
        pos_ready = sem("pos_ready")
        neg_ready = sem("neg_ready")
        row_ready = sem("row_ready")
        NLOAD = 9 + 4 * C
        e_stats_ready = sem("e_stats_ready")
        e_mv_ready = sem("e_mv_ready")
        e_rstd_ready = sem("e_rstd_ready")
        e_rstep = sem("e_rstep")
        e_xn_ready = sem("e_xn_ready")
        e_hTps_ready = sem("e_hTps_ready")
        e_hT_ready = sem("e_hT_ready")
        e_qk_ps_ready = sem("e_qk_ps_ready")
        e_vsk_ps_ready = sem("e_vsk_ps_ready")
        e_qk_copied = sem("e_qk_copied")
        e_vsk_copied = sem("e_vsk_copied")
        e_prod_ready = sem("e_prod_ready")
        e_score_ready = sem("e_score_ready")
        e_scoreT_ready = sem("e_scoreT_ready")
        e_scan = sem("e_scan")
        e_tmax_ps_ready = sem("e_tmax_ps_ready")
        e_tmax_ready = sem("e_tmax_ready")
        e_keyrow_ready = sem("e_keyrow_ready")
        e_same_ready = sem("e_same_ready")
        e_cmax_ps_ready = sem("e_cmax_ps_ready")
        e_cmax_ready = sem("e_cmax_ready")
        e_max_ready = sem("e_max_ready")
        e_meta_ready = sem("e_meta_ready")
        e_expo_ready = sem("e_expo_ready")
        e_aw_ready = sem("e_aw_ready")
        e_vals_ready = sem("e_vals_ready")
        e_agg_ps_ready = sem("e_agg_ps_ready")
        e_carried = sem("e_carried")
        e_state_ready = sem("e_state_ready")
        e_gstep = sem("e_gstep")
        e_logit_ready = sem("e_logit_ready")
        e_eexp_ready = sem("e_eexp_ready")
        e_mix = sem("e_mix")
        e_mmv_ready = sem("e_mmv_ready")
        e_mrstep = sem("e_mrstep")
        e_mrstd_ready = sem("e_mrstd_ready")
        e_u0 = sem("e_u0")
        e_mbias_ready = sem("e_mbias_ready")
        e_mixn_ready = sem("e_mixn_ready")
        e_u_ready = sem("e_u_ready")
        e_relu_ready = sem("e_relu_ready")
        e_prelu_ready = sem("e_prelu_ready")
        e_row_ready = sem("e_row_ready")
        e_idx_ready = sem("e_idx_ready")
        table_step = sem("table_step")
        table_ps_ready = sem("table_ps_ready")
        table_ready = sem("table_ready")
        edges_loaded = sem("edges_loaded")
        dense_written = sem("dense_written")
        e_v_ones = sem("e_v_ones")
        src_loaded = [sem(f"src_loaded{s}") for s in range(2)]
        dst_loaded = [sem(f"dst_loaded{s}") for s in range(XS)]
        scattered = [sem(f"scattered{s}") for s in range(US)]

        block = ctx.enter_context(nc.Block())

        LOOP_TURN = [None]

        def steady(engine, step, first, last):
            for k in range(first, XS):
                step(k, k)
            with engine.Fori(1, MAIN) as i:
                LOOP_TURN[0] = i
                for j in range(XS):
                    step(i * XS + j, j)
            for k in range(MAIN * XS, last):
                step(k, k % XS)

        def live(k, shift):
            return not isinstance(k, int) or 0 <= k + shift < BLOCKS

        def turns(k, j, n, shift):
            if isinstance(k, int):
                return (k + shift) // n
            return LOOP_TURN[0] * (XS // n) + (j + shift) // n

        @block.sync
        def _(sp):
            sp.dma_start(gate_rows[:, :, :], w_gate.rearrange("(o a f) c -> o (a f c)", o=1, a=3).to_broadcast([P, 3 * F])).then_inc(loaded, 16)
            for c in range(C):
                for w_sb, w in ((wskip_sb[:, c, 0:F], w_skip), (wq_sb[:, c, :], w_q), (wk_sb[:, c, :], w_k)):
                    sp.dma_start(w_sb, w[c * P:(c + 1) * P, :]).then_inc(loaded, 16)
                sp.dma_start(wv_sb[:, c, :, 0:D], w_v[c * P:(c + 1) * P, :].rearrange("p (h d) -> p h d", h=H)).then_inc(loaded, 16)
            for row, vec, n in ((bskip_bc, b_skip, F), (bq_bc, b_q, F), (bk_bc, b_k, F), (bv_bc, b_v, F), (lns_bc, ln_scale, F), (lnb_bc, ln_bias, F),
                                (alpha_bc, prelu_alpha, 1), (bgate_bc, b_gate, 1)):
                sp.dma_start(row[:, 0:n], vec.rearrange("(o f) -> o f", o=1).to_broadcast([P, n])).then_inc(loaded, 16)

            def load(k, j):
                s = (j + 0) % XS
                sp.dma_start(xt[:, s, :], block_rows(x, k)).then_inc(x_loaded[s], 16)

            def step(k, j):
                if live(k, AHEAD):
                    if not isinstance(k, int) or k + AHEAD >= XS:
                        sp.wait_ge(pos_ready, k + AHEAD - XS + 1)
                    s = (j + AHEAD) % XS
                    sp.dma_start(xt[:, s, :], block_rows(x, k + AHEAD)).then_inc(x_loaded[s], 16)
                if live(k, -3):
                    sp.wait_ge(row_ready, k - 2)
                    if isinstance(k, int) and k - 3 == BLOCKS - 1:
                        for s in range(US):
                            sp.wait_ge(u_stored[s], 16 * ((BLOCKS - 1) // US + (s < (BLOCKS - 1) % US)))
                    s = (j - 3) % US
                    sp.dma_start(block_rows(out, k - 3), ut[:, s, :]).then_inc(u_stored[s], 16)

            sp.wait_ge(table_step, 1)
            full = E // (2 * P)
            for n, (vec, shift) in enumerate(((src, 0), (dst, 0), (dst, 1))):
                left = E - full * 2 * P - shift
                sp.dma_start(nat_i[0:full, n, :], vec[shift:shift + full * 2 * P].rearrange("(p m) -> p m", p=full)).then_inc(edges_loaded, 16)
                sp.dma_start(nat_i[full:full + 1, n, 0:left],
                             vec[full * 2 * P + shift:E].rearrange("(p m) -> p m", p=1)).then_inc(edges_loaded, 16)

            for k in range(AHEAD):
                sp.dma_start(xt[:, k, :], block_rows(x, k)).then_inc(x_loaded[k], 16)
            steady(sp, step, 0, BLOCKS + 3)
            for s in range(US):
                sp.wait_ge(u_stored[s], 16 * (BLOCKS // US + (s < BLOCKS % US)))
            sp.sem_inc(dense_written, 1)

        def e_steady(engine, step, first, last):
            for g in range(first, EU):
                step(g, g)
            with engine.Fori(1, EMAIN) as i:
                LOOP_TURN[0] = i
                for j in range(EU):
                    step(i * EU + j, j)
            for g in range(EMAIN * EU, last):
                step(g, g % EU)

        def e_live(g, shift):
            return not isinstance(g, int) or 0 <= g + shift < G

        def e_past(g, shift):
            return not isinstance(g, int) or g + shift >= 0

        def e_turns(g, j, n, shift):
            if isinstance(g, int):
                return (g + shift) // n
            return LOOP_TURN[0] * (EU // n) + (j + shift) // n

        @block.gpsimd
        def _(pool):
            nc.gpsimd.memset(ones3[:, :], 1.0).then_inc(ident_ready, 1)
            nc.gpsimd.memset(nhalf[:, :], -0.5).then_inc(ident_ready, 1)
            nc.gpsimd.memset(root_eps[:, :], EPS ** 0.5).then_inc(ident_ready, 1)
            nc.gpsimd.memset(one4[:, :], 1.0).then_inc(ident_ready, 1)
            nc.gpsimd.memset(eps4[:, :], EPS).then_inc(ident_ready, 1)
            nc.gpsimd.memset(ident[:, :], 0.0).then_inc(ident_ready, 1)
            nc.gpsimd.memset(last_row[:, :], 0.0).then_inc(ident_ready, 1)
            nc.gpsimd.memset(nat_i[:, 0, :], 0).then_inc(ident_ready, 1)
            nc.gpsimd.memset(nat_i[:, 1, :], N).then_inc(ident_ready, 1)
            nc.gpsimd.memset(nat_i[:, 2, :], N + 1).then_inc(ident_ready, 1)
            pool.wait_ge(ident_ready, 10)
            nc.gpsimd.affine_select(out=ident[:, :], in_=ident[:, :], compare_op=ALU.not_equal, fill=1.0, base=0,
                                    pattern=[[-1, P]], channel_multiplier=1).then_inc(ident_ready, 1)
            nc.gpsimd.affine_select(out=last_row[:, :], in_=last_row[:, :], compare_op=ALU.not_equal, fill=1.0, base=-(P - 1),
                                    pattern=[[0, P]], channel_multiplier=1).then_inc(ident_ready, 1)
            pool.wait_ge(ident_ready, 12)
            nc.gpsimd.memset(key_cols[:, 0:1], -1.0).then_inc(table_step, 1)

            def x_rstd(k, b):
                if not isinstance(k, int) or k >= 2:
                    pool.wait_ge(xn_ready, k - 1)
                pool.wait_ge(xmv_ready, k + 1)
                nc.gpsimd.tensor_tensor(xrstd[:, b, :], xmv[:, b, :, 1], eps4[:, 0:R], ALU.add).then_inc(xvar_ready, 1)
                pool.wait_ge(xvar_ready, k + 1)
                nc.gpsimd.tensor_tensor(xrstd[:, b, :], xrstd[:, b, :], nhalf[:, 0:R], ALU.pow).then_inc(xrstd_ready, 1)

            def y_scale(k, b):
                pool.wait_ge(egate_ready, 2 * k + 2)
                nc.gpsimd.tensor_tensor(yscale[:, b, :], gate2[:, b, :], ssq[:, b, :], ALU.add).then_inc(gstep, 1)
                pool.wait_ge(gstep, k + 1)
                nc.gpsimd.tensor_tensor(yscale[:, b, :], yscale[:, b, :], nhalf[:, 0:R], ALU.pow).then_inc(yscale_ready, 1)

            def step(k, j):
                if live(k, -1):
                    y_scale(k - 1, (j - 1) % 2)
                if live(k, 3):
                    x_rstd(k + 3, (j + 1) % 2)

            x_rstd(0, 0)
            x_rstd(1, 1)
            x_rstd(2, 0)
            steady(pool, step, 0, BLOCKS + 2)

            last_node = pool.to_reg(N - 1)

            def gather_first(g, j):
                if e_past(g, -EU):
                    pool.wait_ge(scattered[j % US], 16 * R * (e_turns(g, j, US, -EU) + 1))
                pool.wait_ge(table_ready, 1)
                if isinstance(g, int):
                    nc.gpsimd.tensor_copy(idx_b[:, j % EU, :], rows_idx[:, g, :]).then_inc(e_idx_ready, 1)
                else:
                    nc.gpsimd.tensor_copy(idx_b[:, j % EU, :], rows_idx[:, bass.ds(g, 1), :].rearrange("p a b -> p (a b)")).then_inc(e_idx_ready, 1)
                pool.wait_ge(e_idx_ready, g + 1)
                if e_past(g, -2):
                    pool.wait_ge(e_xn_ready, R * (g - 1))
                if e_past(g, -XS):
                    pool.wait_ge(e_prelu_ready, g - XS + 1)
                nc.gpsimd.tensor_tensor(pool_mark[:, 0, j % EU:j % EU + 1], one4[:, 0:1], one4[:, 0:1], ALU.add)
                gather_tiles(g, j, 0, R // 2)

            def gather_tiles(g, j, first, last):
                for r in range(first, last):
                    nc.gpsimd.indirect_dma_start(
                        out=xsrc[:, j % 2, r * F:(r + 1) * F], out_offset=None, in_=x[:, :],
                        in_offset=bass.IndirectOffsetOnAxis(ap=idx_b[:, j % EU, r:r + 1], axis=0),
                        bounds_check=last_node, oob_is_err=True).then_inc(src_loaded[j % 2], 16)
                    nc.gpsimd.indirect_dma_start(
                        out=xt[:, j % XS, r * F:(r + 1) * F], out_offset=None, in_=x[:, :],
                        in_offset=bass.IndirectOffsetOnAxis(ap=idx_b[:, j % EU, R + r:R + r + 1], axis=0),
                        bounds_check=last_node, oob_is_err=True).then_inc(dst_loaded[j % XS], 16)

            def edge_rstd(g, b):
                pool.wait_ge(e_mv_ready, g + 1)
                nc.gpsimd.tensor_tensor(erstd[:, b, :], emv[:, b, :, 1], eps4[:, :], ALU.add).then_inc(e_rstep, 1)
                pool.wait_ge(e_rstep, g + 1)
                nc.gpsimd.tensor_tensor(erstd[:, b, :], erstd[:, b, :], nhalf[:, :], ALU.pow).then_inc(e_rstd_ready, 1)

            def e_step(g, j):
                if e_live(g, 2):
                    gather_first(g + 2, j + 2)
                if e_live(g, 1):
                    edge_rstd(g + 1, (j + 1) % 2)
                if e_live(g, 2):
                    gather_tiles(g + 2, j + 2, R // 2, R)
                if e_live(g, -3):
                    pool.wait_ge(e_mmv_ready, g - 2)
                    nc.gpsimd.tensor_tensor(mrstd[:, :], mmv[:, :, 1], eps4[:, 0:R], ALU.add).then_inc(e_mrstep, 1)
                    pool.wait_ge(e_mrstep, g - 2)
                    nc.gpsimd.tensor_tensor(mrstd[:, :], mrstd[:, :], nhalf[:, 0:R], ALU.pow).then_inc(e_mrstd_ready, 1)
                if e_live(g, -4):
                    s = (j - 4) % US
                    pool.wait_ge(e_row_ready, g - 3)
                    nc.gpsimd.tensor_tensor(pool_mark[:, 1, j % EU:j % EU + 1], one4[:, 0:1], one4[:, 0:1], ALU.add)
                    for r in range(R):
                        nc.gpsimd.indirect_dma_start(
                            out=out[:, :], out_offset=bass.IndirectOffsetOnAxis(ap=idx_b[:, (j - 4) % EU, 2 * R + r:2 * R + r + 1], axis=0),
                            in_=ut[:, s, r * F:(r + 1) * F], in_offset=None,
                            bounds_check=last_node, oob_is_err=False).then_inc(scattered[s], 16)

            pool.wait_ge(pos_ready, BLOCKS)
            for g in range(2):
                gather_first(g, g)
                gather_tiles(g, g, R // 2, R)
            edge_rstd(0, 0)
            pool.wait_ge(dense_written, 1)
            e_steady(pool, e_step, 0, G + 4)
            for s in range(US):
                pool.wait_ge(scattered[s], 16 * R * (G // US + (s < G % US)))

        @block.vector
        def _(dve):
            setup_count = [0]

            def chain(ins):
                setup_count[0] += 1
                ins.then_inc(setup_step, 1)
                dve.wait_ge(setup_step, setup_count[0])

            dve.wait_ge(loaded, 16 * NLOAD)
            dve.wait_ge(ident_ready, 12)
            chain(nc.vector.memset(lns_bc[:, F:F + 1], 1.0))
            chain(nc.vector.tensor_tensor(g13_bc[:, :], gate_rows[:, 0, :], gate_rows[:, 2, :], ALU.add))
            chain(nc.vector.tensor_tensor(g23_bc[:, :], gate_rows[:, 1, :], gate_rows[:, 2, :], ALU.subtract))
            for c in range(C):
                chain(nc.vector.reduce_sum(wmean[:, c:c + 1], wskip_sb[:, c, 0:F], AX.X))
                chain(nc.vector.tensor_scalar(wmean[:, c:c + 1], wmean[:, c:c + 1], 1.0 / F, None, ALU.mult))
                chain(nc.vector.tensor_scalar(wd_sb[:, c, 0:F], wskip_sb[:, c, 0:F], wmean[:, c:c + 1], None, ALU.subtract))
                chain(nc.vector.tensor_tensor_reduce(out=setup_scr[:, :], in0=wskip_sb[:, c, 0:F], in1=g13_bc[:, :], scale=1.0,
                                                     scalar=0.0, op0=ALU.mult, op1=ALU.add, accum_out=wd_sb[:, c, F:F + 1]))
            chain(nc.vector.reduce_sum(wmean[:, C:C + 1], bskip_bc[:, :], AX.X))
            chain(nc.vector.tensor_scalar(wmean[:, C:C + 1], wmean[:, C:C + 1], 1.0 / F, None, ALU.mult))
            bd = WB['d']
            chain(nc.vector.tensor_scalar(bias_row[:, bd:bd + F], bskip_bc[0:3, :], wmean[0:3, C:C + 1], None, ALU.subtract))
            chain(nc.vector.tensor_tensor_reduce(out=setup_scr[:, :], in0=bskip_bc[:, :], in1=g13_bc[:, :], scale=1.0,
                                                 scalar=0.0, op0=ALU.mult, op1=ALU.add, accum_out=wmean[:, C:C + 1]))
            chain(nc.vector.tensor_tensor(bias_row[:, bd + F:bd + F + 1], wmean[0:3, C:C + 1], bgate_bc[0:3, :], ALU.add))
            for c in range(C):
                chain(nc.vector.tensor_copy(wskip_sb[:, c, F:F + 1], wd_sb[:, c, F:F + 1]))
                chain(nc.vector.tensor_tensor(setup_scr[:, :].rearrange("p (h d) -> p h d", h=H), wv_sb[:, c, :, 0:D],
                                              g23_bc[:, :].rearrange("p (h d) -> p h d", h=H), ALU.mult))
                chain(nc.vector.reduce_sum(wv_sb[:, c, :, D], setup_scr[:, :].rearrange("p (h d) -> p h d", h=H), AX.X))
            chain(nc.vector.tensor_tensor(setup_scr[:, :], bv_bc[:, :], g23_bc[:, :], ALU.mult))
            chain(nc.vector.reduce_sum(ubias[:, :], setup_scr[:, :].rearrange("p (h d) -> p h d", h=H), AX.X))
            bv_row = bias_row[:, WB['v']:WB['v'] + H * (D + 1)].rearrange("p (h d) -> p h d", h=H)
            for row, val in ((bias_row[:, 0:F], bq_bc[0:3, :]), (bias_row[:, WB['k']:WB['k'] + F], bk_bc[0:3, :]),
                             (bv_row[:, :, 0:D], bv_bc[0:3, :].rearrange("p (h d) -> p h d", h=H)), (bv_row[:, :, D], ubias[0:3, :]),
                             (bias_row[:, WB['s']:WB['s'] + F], bskip_bc[0:3, :]),
                             (bias_row[:, WB['s'] + F:WB['s'] + F + 1], bias_row[:, bd + F:bd + F + 1])):
                chain(nc.vector.tensor_copy(row, val))
            chain(nc.vector.tensor_copy(bias_part[:, 0, :], bias_row))
            chain(nc.vector.tensor_tensor(bias_left, bias_row, bias_part[:, 0, :], ALU.subtract))
            chain(nc.vector.tensor_copy(bias_part[:, 1, :], bias_left))
            chain(nc.vector.tensor_tensor(bias_left, bias_left, bias_part[:, 1, :], ALU.subtract))
            chain(nc.vector.tensor_copy(bias_part[:, 2, :], bias_left))
            chain(nc.vector.tensor_scalar(bias_sel, bias_part[:, 0, :], ident[0:3, 0:1], None, ALU.mult))
            chain(nc.vector.scalar_tensor_tensor(out=bias_sel, in0=bias_part[:, 1, :], scalar=ident[0:3, 1:2],
                                                 in1=bias_sel, op0=ALU.mult, op1=ALU.add))
            nc.vector.scalar_tensor_tensor(out=bias3[:, :], in0=bias_part[:, 2, :], scalar=ident[0:3, 2:3],
                                           in1=bias_sel, op0=ALU.mult, op1=ALU.add).then_inc(setup_done, 1)
            chain(nc.vector.tensor_scalar(negalpha_bc[:, :], alpha_bc[:, :], -1.0, None, ALU.mult))
            chain(nc.vector.memset(v_ring[:, :, :, 0], 1.0))
            chain(nc.vector.memset(seg_mask[:, :], 0.0))
            chain(nc.vector.memset(seg_maxT[:, :], 0.0))
            chain(nc.vector.memset(state[:, 1, R - 1, :], 0.0))
            chain(nc.vector.memset(maxes[:, 1, R - 1, :], 0.0))

            dve.wait_ge(edges_loaded, 16 * 6)
            SRC, DST, DSTROW, OUTROW, EQNEXT = range(5)
            chain(nc.vector.tensor_copy(nat_f[:, SRC, :], nat_i[:, 0, :]))
            chain(nc.vector.tensor_copy(nat_f[:, DST, :], nat_i[:, 1, :]))
            chain(nc.vector.tensor_copy(nat_f[:, DSTROW, :], nat_i[:, 2, :]))
            chain(nc.vector.tensor_tensor(nat_f[:, EQNEXT, :], nat_f[:, DST, :], nat_f[:, DSTROW, :], ALU.is_equal))
            chain(nc.vector.scalar_tensor_tensor(out=nat_f[:, OUTROW, :], in0=nat_f[:, EQNEXT, :], scalar=SKIP_ROW,
                                                 in1=nat_f[:, DST, :], op0=ALU.mult, op1=ALU.add))
            nc.vector.tensor_scalar(nat_f[:, DSTROW, :], nat_f[:, DST, :], float(N - 1), None, ALU.min).then_inc(table_step, 1)
            dve.wait_ge(table_ps_ready, 1)

            def column(n, h):
                return y_ps[:, n % 4, (n // 4) * 256 + h * 128:(n // 4) * 256 + h * 128 + HALF]

            for h in range(2):
                tiles = rows_idx[:, :, :].rearrange("p g (n r) -> p g n r", n=3)
                for n, k in ((SRC, 0), (DSTROW, 1), (OUTROW, 2)):
                    for q in range(R // 2):
                        chain(nc.vector.tensor_copy(tiles[:, :, k, 2 * q + h], column(n, h)[:, q:HALF:R // 2]))
                chain(nc.vector.tensor_copy(key_cols[:, 1 + h:1 + TP:2], column(DST, h)))
                chain(nc.vector.tensor_copy(eq_cols[:, h:TP:2], column(EQNEXT, h)))
            key_g = key_cols[:, 1:1 + TP].rearrange("p (g r) -> p g r", r=R)
            chain(nc.vector.tensor_copy(meta[:, :, 0:R], key_g))
            for r in range(R):
                for h in range(H):
                    chain(nc.vector.tensor_copy(meta[:, :, 2 * R + r * H + h],
                                                eq_cols[:, :].rearrange("p (g r) -> p g r", r=R)[:, :, r]))
            nc.vector.memset(wait_mark[:, :], 0.0).then_inc(table_step, 1)
            dve.wait_ge(table_ps_ready, 2)
            last_key = y_ps[:, 0, 0:TP].rearrange("p (g r) -> p g r", r=R)
            chain(nc.vector.tensor_tensor(meta[:, :, R:2 * R], key_g, last_key, ALU.not_equal))
            nc.vector.tensor_scalar(meta[:, :, R:2 * R], meta[:, :, R:2 * R], -BIG, None, ALU.mult).then_inc(table_ready, 1)
            dve.wait_ge(table_ready, 1)

            def x_stats(k, j):
                b = j % 2
                dve.wait_ge(x_loaded[j % XS], 16 * (turns(k, j, XS, 0) + 1))
                for r in range(R):
                    last = nc.vector.bn_stats(xstats[:, b, r, :], xt[:, j % XS, r * F:(r + 1) * F])
                last.then_inc(xstats_ready, 1)
                dve.wait_ge(xstats_ready, k + 1)
                nc.vector.memset(wait_mark[:, :], 0.0)
                for r in range(R):
                    last = nc.vector.bn_aggr(xmv[:, b, r, :], xstats[:, b, r, :])
                last.then_inc(xmv_ready, 1)

            def x_bias(k, j):
                b = j % 2
                dve.wait_ge(xrstd_ready, k + 1)
                if not isinstance(k, int) or k >= 2:
                    dve.wait_ge(xn_ready, k - 1)
                nc.vector.scalar_tensor_tensor(out=xbias[:, b, :], in0=xmv[:, b, :, 0], scalar=-1.0, in1=xrstd[:, b, :],
                                               op0=ALU.mult, op1=ALU.mult).then_inc(xbias_ready, 1)

            def step(k, j):
                if live(k, 2):
                    x_bias(k + 2, j + 2)
                if live(k, 3):
                    x_stats(k + 3, j + 3)
                if live(k, 0):
                    for half in range(2):
                        dve.wait_ge(ysq_ready, 4 * k + 2 * half + 2)
                        sl = slice(2 * half, 2 * half + 2)
                        nc.vector.tensor_tensor(wy[:, j % 2, sl, :], y_ps[:, sl, 0:F + 1],
                                                lns_bc[:, None, :].to_broadcast([P, 2, F + 1]), ALU.mult).then_inc(yscaled, 1)
                if live(k, -3):
                    s = (j - 3) % US
                    dve.wait_ge(neg_ready, k - 2)
                    dve.wait_ge(pos_ready, k - 2)
                    nc.vector.scalar_tensor_tensor(out=ut[:, s, :], in0=neg[:, (j - 3) % 2, :], scalar=negalpha_bc[:, 0:1],
                                                   in1=pos[:, (j - 3) % 2, :], op0=ALU.mult, op1=ALU.add).then_inc(row_ready, 1)
                if live(k, -1):
                    s = (j - 1) % US
                    dve.wait_ge(yscale_ready, k)
                    dve.wait_ge(yscaled, 2 * k)
                    if not isinstance(k, int) or k - 1 >= US:
                        dve.wait_ge(u_stored[s], 16 * turns(k, j, US, -1))
                    for r in range(R):
                        last = nc.vector.scalar_tensor_tensor(out=ut[:, s, r * F:(r + 1) * F], in0=wy[:, (j - 1) % 2, r, 0:F],
                                                              scalar=yscale[:, (j - 1) % 2, r:r + 1], in1=lnb_bc[:, :],
                                                              op0=ALU.mult, op1=ALU.add)
                    last.then_inc(u_ready, 1)
                    dve.wait_ge(u_ready, k)
                    nc.vector.scalar_tensor_tensor(out=pos[:, (j - 1) % 2, :], in0=ut[:, s, :], scalar=0.0,
                                                   in1=xt[:, (j - 1) % XS, :], op0=ALU.max, op1=ALU.add).then_inc(pos_ready, 1)

            for k in range(2):
                x_stats(k, k)
                x_bias(k, k)
            x_stats(2, 2)
            steady(dve, step, 0, BLOCKS + 3)

            def edge_stats(g, j):
                b = j % 2
                dve.wait_ge(src_loaded[j % 2], 16 * R * (e_turns(g, j, 2, 0) + 1))
                dve.wait_ge(dst_loaded[j % XS], 16 * R * (e_turns(g, j, XS, 0) + 1))
                for r in range(R):
                    nc.vector.bn_stats(estats[:, b, r, :], xsrc[:, j % 2, r * F:(r + 1) * F])
                for r in range(R):
                    last = nc.vector.bn_stats(estats[:, b, R + r, :], xt[:, j % XS, r * F:(r + 1) * F])
                last.then_inc(e_stats_ready, 1)
                dve.wait_ge(e_stats_ready, g + 1)
                nc.vector.memset(wait_mark[:, :], 0.0)
                for r in range(2 * R):
                    last = nc.vector.bn_aggr(emv[:, b, r, :], estats[:, b, r, :])
                last.then_inc(e_mv_ready, 1)

            def edge_bias(g, j):
                b = j % 2
                dve.wait_ge(e_rstd_ready, g + 1)
                nc.vector.scalar_tensor_tensor(out=ebias[:, b, :], in0=emv[:, b, :, 0], scalar=-1.0, in1=erstd[:, b, :],
                                               op0=ALU.mult, op1=ALU.mult).then_inc(e_xbias_ready, 1)

            def edge_meta(g, j):
                rows = meta[:, g, :] if isinstance(g, int) else meta[:, bass.ds(g, 1), :].rearrange("p a b -> p (a b)")
                nc.vector.tensor_copy(meta_b[:, j % 2, :], rows).then_inc(e_meta_ready, 1)

            def edge_score(g, j):
                dve.wait_ge(e_qk_copied, R * g + R)
                if e_past(g, -1):
                    dve.wait_ge(e_scoreT_ready, g)
                q, k = qk_ring[:, j % 2, :, 0:F], qk_ring[:, j % 2, :, F:2 * F]
                nc.vector.tensor_tensor(q, q, k, ALU.mult).then_inc(e_prod_ready, 1)
                dve.wait_ge(e_prod_ready, g + 1)
                nc.vector.tensor_reduce(score[:, j % 2, :].rearrange("p (r h) -> p r h", h=H), q.rearrange("p r (h d) -> p r h d", h=H),
                                        AX.X, ALU.add).then_inc(e_score_ready, 1)

            def edge_scan(g, j):
                dve.wait_ge(e_scoreT_ready, g + 1)
                nc.vector.tensor_scalar(seg_mask[:, 1:P + 1], eqT_ps, 1.0, BIG, ALU.subtract, ALU.mult).then_inc(e_scan, 1)
                dve.wait_ge(e_scan, 2 * g + 1)
                nc.vector.tensor_tensor_scan(run_max[:, :], seg_mask[:, 0:P], scoreT_ps, -BIG, ALU.add, ALU.max).then_inc(e_scan, 1)
                dve.wait_ge(e_scan, 2 * g + 2)
                nc.vector.tensor_tensor_scan(seg_maxT[0:R * H, ::-1], seg_mask[:, P:0:-1], run_max[:, ::-1], -BIG,
                                             ALU.add, ALU.max).then_inc(e_tmax_ready, 1)

            def edge_tile_max(g, j):
                dve.wait_ge(e_tmax_ps_ready, g + 1)
                nc.vector.tensor_copy(tile_max[:, :], tmax_ps[:, 0:R * H]).then_inc(e_tmax_ready, 1)

            def edge_same(g, j):
                dve.wait_ge(e_keyrow_ready, g + 1)
                nc.vector.tensor_tensor(same[:, j % 2, :].rearrange("p (r e) -> p r e", r=R),
                                        keyrow_ps.rearrange("p (r e) -> p r e", r=R),
                                        meta_b[:, j % 2, 0:R].unsqueeze(2).to_broadcast([P, R, P]), ALU.is_equal).then_inc(e_same_ready, 1)

            def edge_max(g, j, r):
                dve.wait_ge(e_cmax_ps_ready, R * g + r + 1)
                if r == 0:
                    dve.wait_ge(e_tmax_ready, 2 * g + 2)
                nc.vector.tensor_tensor(carry_max[:, r, :], cmax_ps, meta_b[:, j % 2, R + r:R + r + 1].to_broadcast([P, H]), ALU.add).then_inc(e_cmax_ready, 1)
                dve.wait_ge(e_cmax_ready, R * g + r + 1)
                nc.vector.tensor_tensor(maxes[:, j % 2, r, :], tile_max[:, r * H:(r + 1) * H], carry_max[:, r, :],
                                        ALU.max).then_inc(e_max_ready, 1)

            def edge_exponents(g, j):
                if e_past(g, -1):
                    dve.wait_ge(e_aw_ready, g)
                dve.wait_ge(e_max_ready, R * g + R)
                m = maxes[:, j % 2, :, :].rearrange("p r h -> p (r h)")
                nc.vector.tensor_tensor(expo[:, 0, :], score[:, j % 2, :], m, ALU.subtract)
                nc.vector.tensor_tensor(expo[:, 1, :], carry_max[:, :, :].rearrange("p r h -> p (r h)"), m,
                                        ALU.subtract).then_inc(e_expo_ready, 1)

            def edge_values(g, j):
                dve.wait_ge(e_aw_ready, g + 1)
                dve.wait_ge(e_vsk_copied, 2 * (R * g + R))
                if e_past(g, -1):
                    dve.wait_ge(e_agg_ps_ready, R * g)
                nc.vector.tensor_tensor(vals[:, :, :].rearrange("p r (h v) -> p (r h) v", h=H), v_ring[:, j % 4, :, :],
                                        aw[:, j % 2, 0, :].unsqueeze(2).to_broadcast([P, R * H, V]), ALU.mult).then_inc(e_vals_ready, 1)

            def edge_aggregate(g, j, r):
                dve.wait_ge(e_agg_ps_ready, R * g + r + 1)
                nc.vector.tensor_tensor(carried[:, :].rearrange("p (h v) -> p h v", h=H),
                                        carry_ps[:, 0:H * V].rearrange("p (h v) -> p h v", h=H),
                                        aw[:, j % 2, 1, r * H:(r + 1) * H].unsqueeze(2).to_broadcast([P, H, V]),
                                        ALU.mult).then_inc(e_carried, 1)
                dve.wait_ge(e_carried, R * g + r + 1)
                nc.vector.tensor_tensor(state[:, j % 2, r, :], agg_ps[:, 0:H * V], carried[:, :], ALU.add).then_inc(e_state_ready, 1)

            def edge_logit(g, j):
                st = state[:, j % 2, :, :].rearrange("p r (h v) -> p (r h) v", h=H)
                dve.wait_ge(e_state_ready, R * g + R)
                nc.vector.reciprocal(rden[:, :], st[:, :, 0]).then_inc(e_gstep, 1)
                dve.wait_ge(e_gstep, 6 * g + 1)
                nc.vector.tensor_tensor(ugate[:, :], st[:, :, V - 1], rden[:, :], ALU.mult).then_inc(e_gstep, 1)
                dve.wait_ge(e_gstep, 6 * g + 2)
                nc.vector.reduce_sum(logit[:, :], ugate[:, :].rearrange("p (r h) -> p r h", h=H), AX.X).then_inc(e_gstep, 1)
                dve.wait_ge(e_gstep, 6 * g + 3)
                nc.vector.tensor_tensor(logit[:, :], logit[:, :], sk_ring[:, j % 4, :, F], ALU.add).then_inc(e_logit_ready, 1)

            def edge_coefficients(g, j):
                dve.wait_ge(e_eexp_ready, g + 1)
                nc.vector.tensor_scalar(egt[:, :], eexp[:, j % 2, :], 1.0, None, ALU.add).then_inc(e_gstep, 1)
                dve.wait_ge(e_gstep, 6 * g + 4)
                nc.vector.reciprocal(egt[:, :], egt[:, :]).then_inc(e_gstep, 1)
                dve.wait_ge(e_gstep, 6 * g + 5)
                nc.vector.tensor_scalar(omg[:, :], egt[:, :], -1.0, 1.0, ALU.mult, ALU.add).then_inc(e_gstep, 1)
                dve.wait_ge(e_gstep, 6 * g + 6)
                nc.vector.tensor_tensor(coef[:, :].rearrange("p (r h) -> p r h", h=H), rden[:, :].rearrange("p (r h) -> p r h", h=H),
                                        omg[:, :].unsqueeze(2).to_broadcast([P, R, H]), ALU.mult).then_inc(e_mix, 1)

            def edge_mix(g, j):
                st = state[:, j % 2, :, :].rearrange("p r (h v) -> p (r h) v", h=H)
                dve.wait_ge(e_mix, 4 * g + 1)
                if e_past(g, -1):
                    dve.wait_ge(e_mixn_ready, g)
                nc.vector.tensor_tensor(mix.rearrange("p r (h d) -> p r h d", h=H),
                                        st[:, :, 1:D + 1].rearrange("p (r h) d -> p r h d", h=H),
                                        coef[:, :].rearrange("p (r h) -> p r h", h=H).unsqueeze(3).to_broadcast([P, R, H, D]),
                                        ALU.mult).then_inc(e_mix, 1)
                dve.wait_ge(e_mix, 4 * g + 2)
                for r in range(R):
                    last = nc.vector.scalar_tensor_tensor(out=mix[:, r, :], in0=sk_ring[:, j % 4, r, 0:F], scalar=egt[:, r:r + 1],
                                                          in1=mix[:, r, :], op0=ALU.mult, op1=ALU.add)
                last.then_inc(e_mix, 1)

            def edge_mix_stats(g, j):
                dve.wait_ge(e_mix, 4 * g + 3)
                for r in range(R):
                    last = nc.vector.bn_stats(mstats[:, r, :], mix[:, r, :])
                last.then_inc(e_mix, 1)
                dve.wait_ge(e_mix, 4 * g + 4)
                nc.vector.memset(wait_mark[:, :], 0.0)
                for r in range(R):
                    last = nc.vector.bn_aggr(mmv[:, r, :], mstats[:, r, :])
                last.then_inc(e_mmv_ready, 1)

            def edge_mix_bias(g, j):
                dve.wait_ge(e_mrstd_ready, g + 1)
                nc.vector.scalar_tensor_tensor(out=mbias[:, :], in0=mmv[:, :, 0], scalar=-1.0, in1=mrstd[:, :],
                                               op0=ALU.mult, op1=ALU.mult).then_inc(e_mbias_ready, 1)

            def edge_layernorm(g, j):
                s = j % US
                dve.wait_ge(e_mixn_ready, g + 1)
                nc.vector.tensor_tensor(mixn, mixn, lns_bc[:, None, 0:F].to_broadcast([P, R, F]), ALU.mult).then_inc(e_u0, 1)
                dve.wait_ge(e_u0, g + 1)
                if e_past(g, -US):
                    dve.wait_ge(scattered[s], 16 * R * e_turns(g, j, US, 0))
                nc.vector.tensor_tensor(ut[:, s, :].rearrange("p (r f) -> p r f", r=R), mixn,
                                        lnb_bc[:, None, :].to_broadcast([P, R, F]), ALU.add).then_inc(e_u_ready, 1)
                dve.wait_ge(e_u_ready, g + 1)
                nc.vector.scalar_tensor_tensor(out=pos[:, j % 2, :], in0=ut[:, s, :], scalar=0.0,
                                               in1=xt[:, j % XS, :], op0=ALU.max, op1=ALU.add).then_inc(e_prelu_ready, 1)

            def edge_row(g, j):
                dve.wait_ge(e_relu_ready, g + 1)
                dve.wait_ge(e_prelu_ready, g + 1)
                nc.vector.scalar_tensor_tensor(out=ut[:, j % US, :], in0=neg[:, j % 2, :], scalar=negalpha_bc[:, 0:1],
                                               in1=pos[:, j % 2, :], op0=ALU.mult, op1=ALU.add).then_inc(e_row_ready, 1)

            def e_step(g, j):
                if e_live(g, -1):
                    edge_score(g - 1, j - 1)
                if e_live(g, -3):
                    edge_logit(g - 3, j - 3)
                if e_live(g, 1):
                    edge_stats(g + 1, j + 1)
                if e_live(g, 0):
                    edge_meta(g, j)
                if e_live(g, -2):
                    edge_values(g - 2, j - 2)
                if e_live(g, -1):
                    edge_scan(g - 1, j - 1)
                if e_live(g, -3):
                    edge_coefficients(g - 3, j - 3)
                if e_live(g, 1):
                    edge_bias(g + 1, j + 1)
                if e_live(g, -2):
                    edge_aggregate(g - 2, j - 2, 0)
                if e_live(g, -4):
                    edge_layernorm(g - 4, j - 4)
                if e_live(g, -1):
                    edge_tile_max(g - 1, j - 1)
                    edge_max(g - 1, j - 1, 0)
                    edge_same(g - 1, j - 1)
                if e_live(g, -2):
                    edge_aggregate(g - 2, j - 2, 1)
                if e_live(g, -1):
                    edge_max(g - 1, j - 1, 1)
                if e_live(g, -3):
                    edge_mix(g - 3, j - 3)
                if e_live(g, -2):
                    edge_aggregate(g - 2, j - 2, 2)
                if e_live(g, -1):
                    edge_max(g - 1, j - 1, 2)
                if e_live(g, -3):
                    edge_mix_stats(g - 3, j - 3)
                if e_live(g, -4):
                    edge_row(g - 4, j - 4)
                if e_live(g, -2):
                    edge_aggregate(g - 2, j - 2, 3)
                if e_live(g, -1):
                    edge_max(g - 1, j - 1, 3)
                    edge_exponents(g - 1, j - 1)
                if e_live(g, -3):
                    edge_mix_bias(g - 3, j - 3)

            edge_stats(0, 0)
            edge_bias(0, 0)
            e_steady(dve, e_step, 0, G + 4)

        @block.scalar
        def _(act):
            act.wait_ge(loaded, 16 * NLOAD)
            act.wait_ge(ident_ready, 12)

            def x_norm(k, j):
                b = j % 2
                act.wait_ge(xbias_ready, k + 1)
                if not isinstance(k, int) or k >= 2:
                    act.wait_ge(hTps_ready, 2 * (k - 1))
                for r in range(R):
                    last = nc.scalar.activation(xn[:, b, r * F:(r + 1) * F], xt[:, j % XS, r * F:(r + 1) * F], ACT.Identity,
                                                bias=xbias[:, b, r:r + 1], scale=xrstd[:, b, r:r + 1])
                last.then_inc(xn_ready, 1)

            def relu_transposed(k, b):
                if not isinstance(k, int) or k >= 2:
                    act.wait_ge(y_ready, 2 * (k - 1))
                for half in range(2):
                    act.wait_ge(hTps_ready, 2 * k + half + 1)
                    nc.scalar.activation(hT[:, b, half * 512:(half + 1) * 512], hT_ps[:, half, :], ACT.Relu).then_inc(hT_ready, 1)

            def step(k, j):
                if live(k, -1):
                    b = (j - 1) % 2
                    act.wait_ge(yscaled, 2 * k)
                    nc.scalar.activation(egate[:, b, :], wy[:, b, :, F], ACT.Exp, scale=-1.0).then_inc(egate_ready, 1)
                    act.wait_ge(egate_ready, 2 * k - 1)
                    nc.scalar.activation(gate2[:, b, :], egate[:, b, :], ACT.Square, scale=EPS ** 0.5,
                                         bias=root_eps[:, 0:1]).then_inc(egate_ready, 1)
                if live(k, 1):
                    relu_transposed(k + 1, (j + 1) % 2)
                if live(k, 2):
                    x_norm(k + 2, j + 2)
                if live(k, 0):
                    for r in range(R):
                        if r == 0 and (not isinstance(k, int) or k >= 2):
                            act.wait_ge(gstep, k - 1)
                        if r % 2 == 0:
                            act.wait_ge(y_ready, 2 * k + r // 2 + 1)
                        nc.scalar.activation(sq_scr[:, r, :], y_ps[:, r, 0:F], ACT.Square, scale=F ** -0.5,
                                             accum_out=ssq[:, j % 2, r:r + 1]).then_inc(ysq_ready, 1)
                if live(k, -2):
                    act.wait_ge(u_ready, k - 1)
                    if not isinstance(k, int) or k >= 4:
                        act.wait_ge(row_ready, k - 3)
                    nc.scalar.activation(neg[:, j % 2, :], ut[:, (j - 2) % US, :], ACT.Relu, scale=-1.0).then_inc(neg_ready, 1)

            x_norm(0, 0)
            x_norm(1, 1)
            relu_transposed(0, 0)
            steady(act, step, 0, BLOCKS + 2)

            def edge_norm(g, j, r):
                b = j % 2
                act.wait_ge(e_xbias_ready, g + 1)
                if e_past(g, -1):
                    act.wait_ge(e_hTps_ready, R * (g - 1) + r + 1)
                for side, rows in enumerate((xsrc[:, j % 2, :], xt[:, j % XS, :])):
                    c = side * R + r
                    last = nc.scalar.activation(xn[:, side, r * F:(r + 1) * F], rows[:, r * F:(r + 1) * F], ACT.Identity,
                                                bias=ebias[:, b, c:c + 1], scale=erstd[:, b, c:c + 1])
                last.then_inc(e_xn_ready, 1)

            def edge_relu(t, b):
                act.wait_ge(e_hTps_ready, t + 1)
                nc.scalar.activation(hT[:, b, 0:512], ehT_ps, ACT.Relu).then_inc(e_hT_ready, 1)

            def e_step(g, j):
                for r in range(R):
                    t = g * R + r
                    if e_live(g, 0):
                        act.wait_ge(e_qk_ps_ready, t + 1)
                        if r == 0 and e_past(g, -2):
                            act.wait_ge(e_score_ready, g - 1)
                        nc.scalar.copy(qk_ring[:, j % 2, r, :], qk_ps).then_inc(e_qk_copied, 1)
                        if r < R - 1 or e_live(g, 1):
                            if e_past(g, -1) or r >= 1:
                                act.wait_ge(e_vsk_ps_ready, t)
                            edge_relu(t + 1, (r + 1) % 2)
                    if e_live(g, 0):
                        act.wait_ge(e_vsk_ps_ready, t + 1)
                        if r == 0 and e_past(g, -4):
                            act.wait_ge(e_vals_ready, g - 3)
                            act.wait_ge(e_mmv_ready, g - 3)
                        nc.scalar.copy(v_ring[:, j % 4, r * H:(r + 1) * H, 1:V], v_ps.rearrange("p (h v) -> p h v", h=H)).then_inc(e_vsk_copied, 1)
                        nc.scalar.copy(sk_ring[:, j % 4, r, :], sk_ps).then_inc(e_vsk_copied, 1)
                    if r == 0 and e_live(g, -2):
                        act.wait_ge(e_expo_ready, g - 1)
                        nc.scalar.activation(aw[:, j % 2, :, :], expo[:, :, :], ACT.Exp, scale=SCORE_SCALE).then_inc(e_aw_ready, 1)
                    if r == 0 and e_live(g, -3):
                        act.wait_ge(e_logit_ready, g - 2)
                        nc.scalar.activation(eexp[:, (j - 3) % 2, :], logit[:, :], ACT.Exp, scale=-1.0).then_inc(e_eexp_ready, 1)
                    if r == 2 and e_live(g, 1):
                        edge_norm(g + 1, j + 1, 0)
                        edge_norm(g + 1, j + 1, 1)
                        edge_norm(g + 1, j + 1, 2)
                    if r == 2 and e_live(g, -4):
                        act.wait_ge(e_u_ready, g - 3)
                        if e_past(g, -6):
                            act.wait_ge(e_row_ready, g - 5)
                        u = ut[:, (j - 4) % US, :]
                        nc.scalar.activation(neg[:, j % 2, :], u, ACT.Relu, scale=-1.0).then_inc(e_relu_ready, 1)
                    if r == 3 and e_live(g, 1):
                        edge_norm(g + 1, j + 1, 3)
                    if r == 1 and e_live(g, -4):
                        act.wait_ge(e_mbias_ready, g - 3)
                        if e_past(g, -5):
                            act.wait_ge(e_u_ready, g - 4)
                        for q in range(R):
                            last = nc.scalar.activation(mixn[:, q, :], mix[:, q, :], ACT.Identity,
                                                        bias=mbias[:, q:q + 1], scale=mrstd[:, q:q + 1])
                        last.then_inc(e_mixn_ready, 1)

            for r in range(R):
                edge_norm(0, 0, r)
            edge_relu(0, 0)
            e_steady(act, e_step, 0, G + 4)

        @block.tensor
        def _(pe):
            pe.wait_ge(ident_ready, 12)
            pe.wait_ge(table_step, 2)
            for n in range(5):
                for h in range(2):
                    at = (n // 4) * 256 + h * 128
                    last = nc.tensor.transpose(y_ps[:, n % 4, at:at + HALF], nat_f[:, n, h * P:(h + 1) * P], ident[0:HALF, 0:HALF])
            last.then_inc(table_ps_ready, 1)
            pe.wait_ge(table_step, 3)
            nc.tensor.matmul(y_ps[:, 0, 0:TP], last_row[:, :], key_cols[:, 0:TP], start=True, stop=True).then_inc(table_ps_ready, 1)
            pe.wait_ge(table_ready, 1)
            pe.wait_ge(setup_done, 1)

            def transposes(k, b):
                pe.wait_ge(xn_ready, k + 1)
                for half in range(2):
                    if not isinstance(k, int) or k >= 1:
                        pe.wait_ge(hT_ready, 2 * (k - 1) + half + 1)
                    for q in range(4):
                        c = 4 * half + q
                        last = nc.tensor.transpose(hT_ps[:, half, q * P:(q + 1) * P], xn[:, b, c * P:(c + 1) * P], ident[:, :])
                    last.then_inc(hTps_ready, 1)

            def project(k, b):
                for r in range(R):
                    if r % 2 == 0:
                        pe.wait_ge(hT_ready, 2 * k + r // 2 + 1)
                        if not isinstance(k, int) or k >= 1:
                            pe.wait_ge(yscaled, 2 * (k - 1) + r // 2 + 1)
                    nc.tensor.matmul(y_ps[:, r, 0:F + 1], ones3[:, :], bias3[:, WB["d"]:WB["d"] + F + 1], start=True, stop=False)
                    for c in range(C):
                        last = nc.tensor.matmul(y_ps[:, r, 0:F + 1], hT[:, b, (C * r + c) * P:(C * r + c + 1) * P],
                                                wd_sb[:, c, :], start=False, stop=(c == C - 1))
                    if r % 2 == 1:
                        last.then_inc(y_ready, 1)

            def step(k, j):
                if live(k, 1):
                    transposes(k + 1, (j + 1) % 2)
                if live(k, 0):
                    project(k, j % 2)

            transposes(0, 0)
            steady(pe, step, 0, BLOCKS)

            def edge_transposes(g, r):
                t = g * R + r
                pe.wait_ge(e_xn_ready, t + 1)
                if e_past(g, -1) or r >= 1:
                    pe.wait_ge(e_hT_ready, t)
                for side in range(2):
                    for c in range(C):
                        last = nc.tensor.transpose(ehT_ps[:, (side * C + c) * P:(side * C + c + 1) * P],
                                                   xn[:, side, (C * r + c) * P:(C * r + c + 1) * P], ident[:, :])
                last.then_inc(e_hTps_ready, 1)

            def project_edges(out_ps, side, r, weights, at, n):
                nc.tensor.matmul(out_ps, ones3[:, :], bias3[:, at:at + n], start=True, stop=False)
                for c in range(C):
                    last = nc.tensor.matmul(out_ps, hT[:, r % 2, (side * C + c) * P:(side * C + c + 1) * P], weights[c],
                                            start=False, stop=(c == C - 1))
                return last

            def score_rows(g, j):
                pe.wait_ge(e_score_ready, g + 1)
                pe.wait_ge(e_meta_ready, g + 1)
                if e_past(g, -1):
                    pe.wait_ge(e_max_ready, R * g)
                nc.tensor.transpose(scoreT_ps, score[:, j % 2, :], ident[:, :])
                nc.tensor.transpose(eqT_ps, meta_b[:, j % 2, 2 * R:META], ident[:, :]).then_inc(e_scoreT_ready, 1)

            def tile_maxima(g, j):
                pe.wait_ge(e_tmax_ready, 2 * g + 1)
                carried_max(g, j, 0)
                nc.tensor.transpose(tmax_ps, seg_maxT[:, :], ident[:, :]).then_inc(e_tmax_ps_ready, 1)
                if e_past(g, -1):
                    pe.wait_ge(e_same_ready, g)
                for r in range(R):
                    last = nc.tensor.transpose(keyrow_ps[:, r * P:(r + 1) * P], meta_b[:, j % 2, r:r + 1].to_broadcast([P, P]), ident[:, :])
                last.then_inc(e_keyrow_ready, 1)

            def carried_max(g, j, r):
                if e_past(g, -1) or r >= 1:
                    pe.wait_ge(e_max_ready, R * g + r)
                prev = maxes[:, (j - (r == 0)) % 2, (r - 1) % R, :]
                nc.tensor.matmul(cmax_ps, last_row[:, :], prev, start=True, stop=True).then_inc(e_cmax_ps_ready, 1)

            def aggregate(g, j, r):
                pe.wait_ge(e_vals_ready, g + 1)
                pe.wait_ge(e_same_ready, g + 1)
                if e_past(g, -1) or r >= 1:
                    pe.wait_ge(e_state_ready, R * g + r)
                nc.tensor.matmul(agg_ps[:, 0:H * V], same[:, j % 2, r * P:(r + 1) * P], vals[:, r, :], start=True, stop=True)
                prev = state[:, (j - (r == 0)) % 2, (r - 1) % R, :]
                nc.tensor.matmul(carry_ps[:, 0:H * V], last_row[:, :], prev, start=True, stop=True).then_inc(e_agg_ps_ready, 1)

            def e_step(g, j):
                for r in range(R):
                    t = g * R + r
                    if e_live(g, 0):
                        pe.wait_ge(e_hT_ready, t + 1)
                        if e_past(g, -1) or r >= 1:
                            pe.wait_ge(e_qk_copied, t)
                        project_edges(qk_ps[:, 0:F], 0, r, [wq_sb[:, c, :] for c in range(C)], WB['q'], F)
                        project_edges(qk_ps[:, F:2 * F], 1, r, [wk_sb[:, c, :] for c in range(C)], WB['k'], F).then_inc(e_qk_ps_ready, 1)
                        if r < R - 1:
                            edge_transposes(g, r + 1)
                        elif e_live(g, 1):
                            edge_transposes(g + 1, 0)
                    if e_live(g, -1):
                        if r == 1:
                            score_rows(g - 1, j - 1)
                        elif r == 2:
                            tile_maxima(g - 1, j - 1)
                        elif r == 3:
                            carried_max(g - 1, j - 1, 2)
                    if r == 3 and e_live(g, -2):
                        aggregate(g - 2, j - 2, 2)
                    if e_live(g, 0):
                        if e_past(g, -1) or r >= 1:
                            pe.wait_ge(e_vsk_copied, 2 * t)
                        project_edges(v_ps, 0, r, [wv_sb[:, c, :, :].rearrange("p h v -> p (h v)") for c in range(C)], WB['v'], H * (D + 1))
                        project_edges(sk_ps, 1, r, [wskip_sb[:, c, :] for c in range(C)], WB['s'], F + 1).then_inc(e_vsk_ps_ready, 1)
                    if r != 3 and r != 0 and e_live(g, -2):
                        aggregate(g - 2, j - 2, r - 1)
                    if r == 3 and e_live(g, -2):
                        aggregate(g - 2, j - 2, 3)
                    if r >= 2 and e_live(g, -1):
                        carried_max(g - 1, j - 1, 2 * r - 3)

            edge_transposes(0, 0)
            e_steady(pe, e_step, 0, G + 2)


_NAMES = ['x', 'src', 'dst', 'L0_gnn_Wq', 'L0_gnn_bq', 'L0_gnn_Wk', 'L0_gnn_bk', 'L0_gnn_Wv', 'L0_gnn_bv',
          'L0_gnn_Wskip', 'L0_gnn_bskip', 'L0_gnn_Wg', 'L0_gnn_bg', 'L0_gnn_ln_scale', 'L0_gnn_ln_bias',
          'L0_gnn_prelu_alpha']


def kernel(**inputs):
    import numpy as np
    import concourse.bacc as bacc
    from concourse.bass_utils import run_bass_kernel_spmd

    nc = bacc.Bacc("TRN2", target_bir_lowering=False, num_devices=1)
    arrays, args = {}, []
    for name in _NAMES:
        a = np.ascontiguousarray(inputs[name])
        if a.ndim == 0:
            a = a.reshape(1)
        arrays[f"in_{name}"] = a
        args.append(nc.dram_tensor(f"in_{name}", a.shape, mybir.dt.from_np(a.dtype), kind="ExternalInput").ap())
    shape = inputs['x'].shape
    args.append(nc.dram_tensor("out_rows", shape, mybir.dt.float32, kind="ExternalOutput").ap())
    gnn_layer(nc, *args)
    r = run_bass_kernel_spmd(nc, [arrays], core_ids=[0])
    return r.results[0]["out_rows"]
```

```python
import concourse.bass as bass
from concourse import mybir
from contextlib import ExitStack




def gnn_layer(nc, x, src, dst, w_q, b_q, w_k, b_k, w_v, b_v, w_skip, b_skip, w_gate, b_gate,
              ln_scale, ln_bias, prelu_alpha, out):
    fp32 = mybir.dt.float32
    bf16 = mybir.dt.bfloat16
    i32 = mybir.dt.int32
    ALU = mybir.AluOpType
    ACT = mybir.ActivationFunctionType
    AX = mybir.AxisListType

    P = 128
    N, F = x.shape
    C = F // P
    EPS = 1e-5
    R = 4
    ROWS = P * R
    BLOCKS = -(-N // ROWS)
    XS = 8
    US = 4
    AHEAD = 5
    FIRST_SLOT = BLOCKS % XS
    MAIN = (BLOCKS - 1 - AHEAD) // XS

    E = src.shape[0]
    H = 4
    D = F // H
    V = D + 2
    T = -(-E // P)
    G = -(-T // R)
    TP = G * R
    HALF = TP // 2
    SCORE_SCALE = float(D) ** -0.5
    BIG = 1e30
    SKIP_ROW = float(1 << 20)
    META = 2 * R + R * H
    EU = 8
    EMAIN = (G - 2) // EU
    WB = dict(q=0, k=F, v=2 * F, s=2 * F + H * (D + 1), d=2 * F + H * (D + 1) + F + 1)
    BW = WB['d'] + F + 1

    def block_rows(tensor, k, j=None):
        if isinstance(k, int) and k == BLOCKS - 1:
            return tensor[N - ROWS:N, :].rearrange("(p r) f -> p (r f)", r=R)
        blocks = tensor[0:(BLOCKS - 1) * ROWS, :].rearrange("(n p r) f -> n p (r f)", p=P, r=R)
        if isinstance(k, int):
            return blocks[k, :, :]
        return blocks[bass.ds(k, 1), :, :].rearrange("n p m -> p (n m)")

    ctx = ExitStack()
    with ctx:
        def sb(name, shape, dt=fp32):
            return ctx.enter_context(nc.sbuf_tensor(name, shape, dt))

        def ps(name, shape, dt=fp32):
            return ctx.enter_context(nc.psum_tensor(name, shape, dt))

        def sem(name):
            return ctx.enter_context(nc.semaphore(name))

        wskip_sb = sb("wskip_sb", [P, C, F + 1])
        wq_sb = sb("wq_sb", [P, C, F])
        wk_sb = sb("wk_sb", [P, C, F])
        wv_sb = sb("wv_sb", [P, C, H, D + 1])
        bq_bc = sb("bq_bc", [P, F])
        bk_bc = sb("bk_bc", [P, F])
        bv_bc = sb("bv_bc", [P, F])
        g23_bc = sb("g23_bc", [P, F])
        negalpha_bc = sb("negalpha_bc", [P, 1])
        last_row = sb("last_row", [P, P])
        wd_sb = sb("wd_sb", [P, C, F + 1])
        gate_rows = sb("gate_rows", [P, 3, F])
        g13_bc = sb("g13_bc", [P, F])
        bskip_bc = sb("bskip_bc", [P, F])
        lns_bc = sb("lns_bc", [P, F + 1])
        lnb_bc = sb("lnb_bc", [P, F])
        alpha_bc = sb("alpha_bc", [P, 1])
        bgate_bc = sb("bgate_bc", [P, 1])
        ident = sb("ident", [P, P])
        ones3 = sb("ones3", [3, P], bf16)
        setup_scr = sb("setup_scr", [P, F])
        wmean = sb("wmean", [P, C + 1])
        ubias = sb("ubias", [P, H])
        bias3 = sb("bias3", [3, BW], bf16)
        nhalf = sb("nhalf", [P, 2 * R])
        ones4 = sb("ones4", [P, R])
        eps4 = sb("eps4", [P, 2 * R])

        xt = sb("xt", [P, XS, R * F])
        xn = sb("xn", [P, 2, R * F])
        hT = sb("hT", [P, 2, R * C * P])
        wy = sb("wy", [P, 2, R, F + 1])
        ut = sb("ut", [P, US, R * F])
        pos = sb("pos", [P, 2, R * F])
        neg = sb("neg", [P, 2, R * F])
        bias_row = pos[0:3, :, :].rearrange("p a b -> p (a b)")[:, 0:BW]
        bias_left = neg[0:3, :, :].rearrange("p a b -> p (a b)")[:, 0:BW]
        bias_sel = wy[0:3, :, :, :].rearrange("p a b c -> p (a b c)")[:, 0:BW]
        bias_part = ut[0:3, :, :].rearrange("p a b -> p (a b)").bitcast(bf16)[:, 0:3 * BW].rearrange("p (a b) -> p a b", a=3)

        key_cols = sb("key_cols", [P, TP + 1])
        eq_cols = sb("eq_cols", [P, TP])
        meta = sb("meta", [P, G, META])
        rows_idx = sb("rows_idx", [P, G, 3 * R], i32)
        meta_b = sb("meta_b", [P, 2, META])
        idx_b = sb("idx_b", [P, EU, 3 * R], i32)
        xsrc = sb("xsrc", [P, 2, R * F])
        emv = sb("emv", [P, 2, 2 * R, 2])
        estats = sb("estats", [P, 2, 2 * R, 6])
        erstd = sb("erstd", [P, 2, 2 * R])
        ebias = sb("ebias", [P, 2, 2 * R])
        qk_ring = sb("qk_ring", [P, 2, R, 2 * F])
        v_ring = sb("v_ring", [P, 4, R * H, V])
        sk_ring = sb("sk_ring", [P, 4, R, F + 1])
        edge_scratch = sk_ring[0:HALF, :, :, :].rearrange("p a b c -> p (a b c)")
        nat_f = edge_scratch[:, 0:10 * P].rearrange("p (n e) -> p n e", n=5)
        nat_i = edge_scratch[:, 10 * P:16 * P].bitcast(i32).rearrange("p (n e) -> p n e", n=3)
        score = sb("score", [P, 2, R * H])
        seg_mask = sb("seg_mask", [R * H, P + 1])
        run_max = sb("run_max", [R * H, P])
        seg_maxT = sb("seg_maxT", [P, P])
        tile_max = sb("tile_max", [P, R * H])
        same = sb("same", [P, 2, R * P])
        carry_max = sb("carry_max", [P, R, H])
        maxes = sb("maxes", [P, 2, R, H])
        expo = sb("expo", [P, 2, R * H])
        aw = sb("aw", [P, 2, 2, R * H])
        vals = sb("vals", [P, R, H * V])
        carried = sb("carried", [P, H * V])
        state = sb("state", [P, 2, R, H * V])
        rden = sb("rden", [P, R * H])
        ugate = sb("ugate", [P, R * H])
        logit = sb("logit", [P, R])
        eexp = sb("eexp", [P, 2, R])
        egt = sb("egt", [P, R])
        omg = sb("omg", [P, R])
        coef = sb("coef", [P, R * H])
        mix = wy[:, 0, :, 0:F]
        mixn = wy[:, 1, :, 0:F]
        mbias = sb("mbias", [P, R])
        mstats = sb("mstats", [P, R, 6])
        mmv = sb("mmv", [P, R, 2])
        mrstd = sb("mrstd", [P, R])
        xstats = sb("xstats", [P, 2, R, 6])
        xmv = sb("xmv", [P, 2, R, 2])
        var_scale = sb("var_scale", [P, R])
        xrstd = sb("xrstd", [P, 2, R])
        pool_mark = sb("pool_mark", [P, 2, EU])
        wait_mark = sb("wait_mark", [P, 1])
        sq_scr = sb("sq_scr", [P, R, F])
        ssq = sb("ssq", [P, 2, R])
        egate = sb("egate", [P, 2, R])
        root_eps = sb("root_eps", [P, 1])
        xbias = sb("xbias", [P, 2, R])
        gate2 = sb("gate2", [P, 2, R])
        yscale = sb("yscale", [P, 2, R])


        hT_ps = ps("hT_ps", [P, 2, 512])
        y_ps = ps("y_ps", [P, R, 512])
        agg_ps = ps("agg_ps", [P, 512])
        carry_ps = ps("carry_ps", [P, 512])
        ehT_ps = hT_ps[:, 0, :]
        qk_ps = y_ps[:, 0, :]
        v_ps = y_ps[:, 1, 0:H * (D + 1)]
        sk_ps = y_ps[:, 2, 0:F + 1]
        keyrow_ps = y_ps[:, 3, :]
        scoreT_ps = hT_ps[0:R * H, 1, 0:P]
        eqT_ps = hT_ps[0:R * H, 1, P:2 * P]
        tmax_ps = hT_ps[:, 1, 2 * P:3 * P]
        cmax_ps = hT_ps[:, 1, 3 * P:3 * P + H]

        loaded = sem("weights_loaded")
        ident_ready = sem("ident_ready")
        setup_step = sem("setup_step")
        setup_done = sem("setup_done")
        x_loaded = [sem(f"x_loaded{s}") for s in range(XS)]
        u_stored = [sem(f"u_stored{s}") for s in range(US)]
        xstats_ready = sem("xstats_ready")
        xmv_ready = sem("xmv_ready")
        xvar_ready = sem("xvar_ready")
        xrow_ready = sem("xrow_ready")
        xrstd_ready = sem("xrstd_ready")
        xbias_ready = sem("xbias_ready")
        e_xbias_ready = sem("e_xbias_ready")
        xn_ready = sem("xn_ready")
        hTps_ready = sem("hTps_ready")
        hT_ready = sem("hT_ready")
        y_ready = sem("y_ready")
        ysq_ready = sem("ysq_ready")
        egate_ready = sem("egate_ready")
        yscaled = sem("yscaled")
        gate_var_ready = sem("gate_var_ready")
        yscale_ready = sem("yscale_ready")
        u_ready = sem("u_ready")
        pos_ready = sem("pos_ready")
        neg_ready = sem("neg_ready")
        row_ready = sem("row_ready")
        NLOAD = 9 + 4 * C
        e_stats_ready = sem("e_stats_ready")
        e_mv_ready = sem("e_mv_ready")
        e_rstd_ready = sem("e_rstd_ready")
        e_var_ready = sem("e_var_ready")
        e_xn_ready = sem("e_xn_ready")
        e_hTps_ready = sem("e_hTps_ready")
        e_hT_ready = sem("e_hT_ready")
        e_qk_ps_ready = sem("e_qk_ps_ready")
        e_vsk_ps_ready = sem("e_vsk_ps_ready")
        e_qk_copied = sem("e_qk_copied")
        e_vsk_copied = sem("e_vsk_copied")
        e_prod_ready = sem("e_prod_ready")
        e_score_ready = sem("e_score_ready")
        e_scoreT_ready = sem("e_scoreT_ready")
        e_scan = sem("e_scan")
        e_tmax_ps_ready = sem("e_tmax_ps_ready")
        e_tmax_ready = sem("e_tmax_ready")
        e_keyrow_ready = sem("e_keyrow_ready")
        e_same_ready = sem("e_same_ready")
        e_cmax_ps_ready = sem("e_cmax_ps_ready")
        e_cmax_ready = sem("e_cmax_ready")
        e_max_ready = sem("e_max_ready")
        e_meta_ready = sem("e_meta_ready")
        e_expo_ready = sem("e_expo_ready")
        e_aw_ready = sem("e_aw_ready")
        e_vals_ready = sem("e_vals_ready")
        e_agg_ps_ready = sem("e_agg_ps_ready")
        e_carried = sem("e_carried")
        e_state_ready = sem("e_state_ready")
        e_gate_step = sem("e_gate_step")
        e_logit_ready = sem("e_logit_ready")
        e_eexp_ready = sem("e_eexp_ready")
        e_mix = sem("e_mix")
        e_mmv_ready = sem("e_mmv_ready")
        e_mvar_ready = sem("e_mvar_ready")
        e_mrstd_ready = sem("e_mrstd_ready")
        e_scaled = sem("e_scaled")
        e_mbias_ready = sem("e_mbias_ready")
        e_mixn_ready = sem("e_mixn_ready")
        e_u_ready = sem("e_u_ready")
        e_neg_ready = sem("e_neg_ready")
        e_pos_ready = sem("e_pos_ready")
        e_row_ready = sem("e_row_ready")
        e_idx_ready = sem("e_idx_ready")
        table_step = sem("table_step")
        table_ps_ready = sem("table_ps_ready")
        table_ready = sem("table_ready")
        edges_loaded = sem("edges_loaded")
        dense_written = sem("dense_written")
        src_loaded = [sem(f"src_loaded{s}") for s in range(2)]
        dst_loaded = [sem(f"dst_loaded{s}") for s in range(XS)]
        scattered = [sem(f"scattered{s}") for s in range(US)]

        block = ctx.enter_context(nc.Block())

        loop_turn = [None]

        def steady(engine, step, first, last):
            for k in range(first, XS):
                step(k, k)
            with engine.Fori(1, MAIN) as i:
                loop_turn[0] = i
                for j in range(XS):
                    step(i * XS + j, j)
            for k in range(MAIN * XS, last):
                step(k, k % XS)

        def live(k, shift):
            return not isinstance(k, int) or 0 <= k + shift < BLOCKS

        def turns(k, j, n, shift):
            if isinstance(k, int):
                return (k + shift) // n
            return loop_turn[0] * (XS // n) + (j + shift) // n

        @block.sync
        def _(sp):
            for k in range(2):
                sp.dma_start(xt[:, k, :], block_rows(x, k)).then_inc(x_loaded[k], 16)
            sp.dma_start(gate_rows[:, :, :], w_gate.rearrange("(o a f) c -> o (a f c)", o=1, a=3).to_broadcast([P, 3 * F])).then_inc(loaded, 16)
            for c in range(C):
                for w_sb, w in ((wskip_sb[:, c, 0:F], w_skip), (wq_sb[:, c, :], w_q), (wk_sb[:, c, :], w_k)):
                    sp.dma_start(w_sb, w[c * P:(c + 1) * P, :]).then_inc(loaded, 16)
                sp.dma_start(wv_sb[:, c, :, 0:D], w_v[c * P:(c + 1) * P, :].rearrange("p (h d) -> p h d", h=H)).then_inc(loaded, 16)
            for row, vec, n in ((bskip_bc, b_skip, F), (bq_bc, b_q, F), (bk_bc, b_k, F), (bv_bc, b_v, F), (lns_bc, ln_scale, F), (lnb_bc, ln_bias, F),
                                (alpha_bc, prelu_alpha, 1), (bgate_bc, b_gate, 1)):
                sp.dma_start(row[:, 0:n], vec.rearrange("(o f) -> o f", o=1).to_broadcast([P, n])).then_inc(loaded, 16)

            def step(k, j):
                if live(k, AHEAD):
                    if not isinstance(k, int) or k + AHEAD >= XS:
                        sp.wait_ge(pos_ready, k + AHEAD - XS + 1)
                    s = (j + AHEAD) % XS
                    sp.dma_start(xt[:, s, :], block_rows(x, k + AHEAD)).then_inc(x_loaded[s], 16)
                if live(k, -3):
                    sp.wait_ge(row_ready, k - 2)
                    if isinstance(k, int) and k - 3 == BLOCKS - 1:
                        for s in range(US):
                            sp.wait_ge(u_stored[s], 16 * ((BLOCKS - 1) // US + (s < (BLOCKS - 1) % US)))
                    s = (j - 3) % US
                    sp.dma_start(block_rows(out, k - 3), ut[:, s, :]).then_inc(u_stored[s], 16)

            sp.wait_ge(table_step, 1)
            full = E // (2 * P)
            for n, (vec, shift) in enumerate(((src, 0), (dst, 0), (dst, 1))):
                left = E - full * 2 * P - shift
                sp.dma_start(nat_i[0:full, n, :], vec[shift:shift + full * 2 * P].rearrange("(p m) -> p m", p=full)).then_inc(edges_loaded, 16)
                sp.dma_start(nat_i[full:full + 1, n, 0:left],
                             vec[full * 2 * P + shift:E].rearrange("(p m) -> p m", p=1)).then_inc(edges_loaded, 16)

            for k in range(2, AHEAD):
                sp.dma_start(xt[:, k, :], block_rows(x, k)).then_inc(x_loaded[k], 16)
            steady(sp, step, 0, BLOCKS + 3)
            for s in range(US):
                sp.wait_ge(u_stored[s], 16 * (BLOCKS // US + (s < BLOCKS % US)))
            sp.sem_inc(dense_written, 1)

        def e_steady(engine, step, first, last):
            for g in range(first, EU):
                step(g, g)
            with engine.Fori(1, EMAIN) as i:
                loop_turn[0] = i
                for j in range(EU):
                    step(i * EU + j, j)
            for g in range(EMAIN * EU, last):
                step(g, g % EU)

        def e_live(g, shift):
            return not isinstance(g, int) or 0 <= g + shift < G

        def e_past(g, shift):
            return not isinstance(g, int) or g + shift >= 0

        def e_turns(g, j, n, shift):
            if isinstance(g, int):
                return (g + shift) // n
            return loop_turn[0] * (EU // n) + (j + shift) // n

        @block.gpsimd
        def _(pool):
            nc.gpsimd.memset(ones3[:, :], 1.0).then_inc(ident_ready, 1)
            nc.gpsimd.memset(nhalf[:, :], -0.5).then_inc(ident_ready, 1)
            nc.gpsimd.memset(var_scale[:, 0:R - 1], 1.0).then_inc(ident_ready, 1)
            nc.gpsimd.memset(var_scale[:, R - 1:R], 1.0 / F).then_inc(ident_ready, 1)
            nc.gpsimd.memset(root_eps[:, :], EPS ** 0.5).then_inc(ident_ready, 1)
            nc.gpsimd.memset(ones4[:, :], 1.0).then_inc(ident_ready, 1)
            nc.gpsimd.memset(eps4[:, :], EPS).then_inc(ident_ready, 1)
            nc.gpsimd.memset(ident[:, :], 0.0).then_inc(ident_ready, 1)
            nc.gpsimd.memset(last_row[:, :], 0.0).then_inc(ident_ready, 1)
            nc.gpsimd.memset(nat_i[:, 0, :], 0).then_inc(ident_ready, 1)
            nc.gpsimd.memset(nat_i[:, 1, :], N).then_inc(ident_ready, 1)
            nc.gpsimd.memset(nat_i[:, 2, :], N + 1).then_inc(ident_ready, 1)
            pool.wait_ge(ident_ready, 12)
            nc.gpsimd.affine_select(out=ident[:, :], in_=ident[:, :], compare_op=ALU.not_equal, fill=1.0, base=0,
                                    pattern=[[-1, P]], channel_multiplier=1).then_inc(ident_ready, 1)
            nc.gpsimd.affine_select(out=last_row[:, :], in_=last_row[:, :], compare_op=ALU.not_equal, fill=1.0, base=-(P - 1),
                                    pattern=[[0, P]], channel_multiplier=1).then_inc(ident_ready, 1)
            pool.wait_ge(ident_ready, 14)
            nc.gpsimd.memset(key_cols[:, 0:1], -1.0).then_inc(table_step, 1)

            last_node = pool.to_reg(N - 1)

            def x_rstd(k, b):
                if not isinstance(k, int) or k >= 2:
                    pool.wait_ge(xn_ready, k - 1)
                pool.wait_ge(xmv_ready, k + 1)
                pool.wait_ge(xrow_ready, 2 * k + 2)
                nc.gpsimd.tensor_tensor(xrstd[:, b, :], xmv[:, b, :, 1], var_scale[:, :], ALU.mult).then_inc(xvar_ready, 1)
                pool.wait_ge(xvar_ready, 2 * k + 1)
                nc.gpsimd.tensor_tensor(xrstd[:, b, :], xrstd[:, b, :], eps4[:, 0:R], ALU.add).then_inc(xvar_ready, 1)
                pool.wait_ge(xvar_ready, 2 * k + 2)
                nc.gpsimd.tensor_tensor(xrstd[:, b, :], xrstd[:, b, :], nhalf[:, 0:R], ALU.pow).then_inc(xrstd_ready, 1)

            def y_scale(k, b):
                pool.wait_ge(egate_ready, 2 * k + 2)
                nc.gpsimd.tensor_tensor(yscale[:, b, :], gate2[:, b, :], ssq[:, b, :], ALU.add).then_inc(gate_var_ready, 1)
                pool.wait_ge(gate_var_ready, k + 1)
                nc.gpsimd.tensor_tensor(yscale[:, b, :], yscale[:, b, :], nhalf[:, 0:R], ALU.pow).then_inc(yscale_ready, 1)

            def step(k, j):
                if live(k, -1):
                    y_scale(k - 1, (j - 1) % 2)
                if live(k, 3):
                    x_rstd(k + 3, (j + 1) % 2)
                if isinstance(k, int) and k == BLOCKS - 4:
                    gather_first(0, 0)
                if isinstance(k, int) and k == BLOCKS - 3:
                    gather_tiles(0, 0, R // 2, R)
                if isinstance(k, int) and k == BLOCKS - 2:
                    gather_first(1, 1)
                if isinstance(k, int) and k == BLOCKS - 1:
                    gather_tiles(1, 1, R // 2, R)

            def gather_first(g, j):
                if e_past(g, -EU):
                    pool.wait_ge(scattered[j % US], 16 * R * (e_turns(g, j, US, -EU) + 1))
                pool.wait_ge(table_ready, 1)
                if isinstance(g, int):
                    nc.gpsimd.tensor_copy(idx_b[:, j % EU, :], rows_idx[:, g, :]).then_inc(e_idx_ready, 1)
                else:
                    nc.gpsimd.tensor_copy(idx_b[:, j % EU, :], rows_idx[:, bass.ds(g, 1), :].rearrange("p a b -> p (a b)")).then_inc(e_idx_ready, 1)
                pool.wait_ge(e_idx_ready, g + 1)
                if e_past(g, -2):
                    pool.wait_ge(e_xn_ready, R * (g - 1))
                if e_past(g, -XS):
                    pool.wait_ge(e_pos_ready, g - XS + 1)
                else:
                    pool.wait_ge(pos_ready, BLOCKS - XS + g + 1)
                nc.gpsimd.tensor_tensor(pool_mark[:, 0, j % EU:j % EU + 1], ones4[:, 0:1], ones4[:, 0:1], ALU.add)
                gather_tiles(g, j, 0, R // 2)

            def gather_tiles(g, j, first, last):
                for r in range(first, last):
                    nc.gpsimd.indirect_dma_start(
                        out=xsrc[:, j % 2, r * F:(r + 1) * F], out_offset=None, in_=x[:, :],
                        in_offset=bass.IndirectOffsetOnAxis(ap=idx_b[:, j % EU, r:r + 1], axis=0),
                        bounds_check=last_node, oob_is_err=True).then_inc(src_loaded[j % 2], 16)
                    nc.gpsimd.indirect_dma_start(
                        out=xt[:, (j + FIRST_SLOT) % XS, r * F:(r + 1) * F], out_offset=None, in_=x[:, :],
                        in_offset=bass.IndirectOffsetOnAxis(ap=idx_b[:, j % EU, R + r:R + r + 1], axis=0),
                        bounds_check=last_node, oob_is_err=True).then_inc(dst_loaded[j % XS], 16)

            def edge_rstd(g, b):
                pool.wait_ge(e_mv_ready, g + 1)
                nc.gpsimd.tensor_tensor(erstd[:, b, :], emv[:, b, :, 1], eps4[:, :], ALU.add).then_inc(e_var_ready, 1)
                pool.wait_ge(e_var_ready, g + 1)
                nc.gpsimd.tensor_tensor(erstd[:, b, :], erstd[:, b, :], nhalf[:, :], ALU.pow).then_inc(e_rstd_ready, 1)

            x_rstd(0, 0)
            x_rstd(1, 1)
            x_rstd(2, 0)
            steady(pool, step, 0, BLOCKS + 2)

            def e_step(g, j):
                if e_live(g, 2):
                    gather_first(g + 2, j + 2)
                if e_live(g, 1):
                    edge_rstd(g + 1, (j + 1) % 2)
                if e_live(g, 2):
                    gather_tiles(g + 2, j + 2, R // 2, R)
                if e_live(g, -3):
                    pool.wait_ge(e_mmv_ready, g - 2)
                    nc.gpsimd.tensor_tensor(mrstd[:, :], mmv[:, :, 1], eps4[:, 0:R], ALU.add).then_inc(e_mvar_ready, 1)
                    pool.wait_ge(e_mvar_ready, g - 2)
                    nc.gpsimd.tensor_tensor(mrstd[:, :], mrstd[:, :], nhalf[:, 0:R], ALU.pow).then_inc(e_mrstd_ready, 1)
                if e_live(g, -4):
                    s = (j - 4) % US
                    if isinstance(g, int) and g == 4:
                        pool.wait_ge(dense_written, 1)
                    pool.wait_ge(e_row_ready, g - 3)
                    nc.gpsimd.tensor_tensor(pool_mark[:, 1, j % EU:j % EU + 1], ones4[:, 0:1], ones4[:, 0:1], ALU.add)
                    for r in range(R):
                        nc.gpsimd.indirect_dma_start(
                            out=out[:, :], out_offset=bass.IndirectOffsetOnAxis(ap=idx_b[:, (j - 4) % EU, 2 * R + r:2 * R + r + 1], axis=0),
                            in_=ut[:, s, r * F:(r + 1) * F], in_offset=None,
                            bounds_check=last_node, oob_is_err=False).then_inc(scattered[s], 16)

            edge_rstd(0, 0)
            e_steady(pool, e_step, 0, G + 4)
            for s in range(US):
                pool.wait_ge(scattered[s], 16 * R * (G // US + (s < G % US)))

        @block.vector
        def _(dve):
            setup_count = [0]

            def chain(ins):
                setup_count[0] += 1
                ins.then_inc(setup_step, 1)
                dve.wait_ge(setup_step, setup_count[0])

            def x_stats(k, j):
                b = j % 2
                dve.wait_ge(x_loaded[j % XS], 16 * (turns(k, j, XS, 0) + 1))
                for r in range(R - 1):
                    last = nc.vector.bn_stats(xstats[:, b, r, :], xt[:, j % XS, r * F:(r + 1) * F])
                last.then_inc(xstats_ready, 1)
                dve.wait_ge(xstats_ready, k + 1)
                nc.vector.memset(wait_mark[:, :], 0.0)
                for r in range(R - 1):
                    last = nc.vector.bn_aggr(xmv[:, b, r, :], xstats[:, b, r, :])
                last.then_inc(xmv_ready, 1)

            def x_bias(k, j):
                b = j % 2
                dve.wait_ge(xrstd_ready, k + 1)
                if not isinstance(k, int) or k >= 2:
                    dve.wait_ge(xn_ready, k - 1)
                nc.vector.scalar_tensor_tensor(out=xbias[:, b, :], in0=xmv[:, b, :, 0], scalar=-1.0, in1=xrstd[:, b, :],
                                               op0=ALU.mult, op1=ALU.mult).then_inc(xbias_ready, 1)

            def edge_stats(g, j):
                b = j % 2
                dve.wait_ge(src_loaded[j % 2], 16 * R * (e_turns(g, j, 2, 0) + 1))
                dve.wait_ge(dst_loaded[j % XS], 16 * R * (e_turns(g, j, XS, 0) + 1))
                for r in range(R):
                    nc.vector.bn_stats(estats[:, b, r, :], xsrc[:, j % 2, r * F:(r + 1) * F])
                for r in range(R):
                    last = nc.vector.bn_stats(estats[:, b, R + r, :], xt[:, (j + FIRST_SLOT) % XS, r * F:(r + 1) * F])
                last.then_inc(e_stats_ready, 1)
                dve.wait_ge(e_stats_ready, g + 1)
                nc.vector.memset(wait_mark[:, :], 0.0)
                for r in range(2 * R):
                    last = nc.vector.bn_aggr(emv[:, b, r, :], estats[:, b, r, :])
                last.then_inc(e_mv_ready, 1)

            def edge_bias(g, j):
                b = j % 2
                dve.wait_ge(e_rstd_ready, g + 1)
                nc.vector.scalar_tensor_tensor(out=ebias[:, b, :], in0=emv[:, b, :, 0], scalar=-1.0, in1=erstd[:, b, :],
                                               op0=ALU.mult, op1=ALU.mult).then_inc(e_xbias_ready, 1)

            def step(k, j):
                if live(k, 3):
                    x_stats(k + 3, j + 3)
                if live(k, 0):
                    for half in range(2):
                        dve.wait_ge(ysq_ready, 4 * k + 2 * half + 2)
                        sl = slice(2 * half, 2 * half + 2)
                        nc.vector.tensor_tensor(wy[:, j % 2, sl, :], y_ps[:, sl, 0:F + 1],
                                                lns_bc[:, None, :].to_broadcast([P, 2, F + 1]), ALU.mult).then_inc(yscaled, 1)
                if live(k, -3):
                    s = (j - 3) % US
                    dve.wait_ge(neg_ready, k - 2)
                    dve.wait_ge(pos_ready, k - 2)
                    nc.vector.scalar_tensor_tensor(out=ut[:, s, :], in0=neg[:, (j - 3) % 2, :], scalar=negalpha_bc[:, 0:1],
                                                   in1=pos[:, (j - 3) % 2, :], op0=ALU.mult, op1=ALU.add).then_inc(row_ready, 1)
                if live(k, 3):
                    x_bias(k + 3, j + 3)
                if live(k, -1):
                    s = (j - 1) % US
                    dve.wait_ge(yscale_ready, k)
                    dve.wait_ge(yscaled, 2 * k)
                    if not isinstance(k, int) or k - 1 >= US:
                        dve.wait_ge(u_stored[s], 16 * turns(k, j, US, -1))
                    for r in range(R):
                        last = nc.vector.scalar_tensor_tensor(out=ut[:, s, r * F:(r + 1) * F], in0=wy[:, (j - 1) % 2, r, 0:F],
                                                              scalar=yscale[:, (j - 1) % 2, r:r + 1], in1=lnb_bc[:, :],
                                                              op0=ALU.mult, op1=ALU.add)
                    last.then_inc(u_ready, 1)
                    dve.wait_ge(u_ready, k)
                    nc.vector.scalar_tensor_tensor(out=pos[:, (j - 1) % 2, :], in0=ut[:, s, :], scalar=0.0,
                                                   in1=xt[:, (j - 1) % XS, :], op0=ALU.max, op1=ALU.add).then_inc(pos_ready, 1)
                if isinstance(k, int) and k == BLOCKS:
                    edge_stats(0, 0)
                if isinstance(k, int) and k == BLOCKS + 1:
                    edge_bias(0, 0)

            def split_bias(lo, hi):
                row, left, sel = bias_row[:, lo:hi], bias_left[:, lo:hi], bias_sel[:, lo:hi]
                part = bias_part[:, :, lo:hi]
                chain(nc.vector.tensor_copy(part[:, 0, :], row))
                chain(nc.vector.tensor_tensor(left, row, part[:, 0, :], ALU.subtract))
                chain(nc.vector.tensor_copy(part[:, 1, :], left))
                chain(nc.vector.tensor_tensor(left, left, part[:, 1, :], ALU.subtract))
                chain(nc.vector.tensor_copy(part[:, 2, :], left))
                chain(nc.vector.tensor_scalar(sel, part[:, 0, :], ident[0:3, 0:1], None, ALU.mult))
                chain(nc.vector.scalar_tensor_tensor(out=sel, in0=part[:, 1, :], scalar=ident[0:3, 1:2],
                                                     in1=sel, op0=ALU.mult, op1=ALU.add))
                nc.vector.scalar_tensor_tensor(out=bias3[:, lo:hi], in0=part[:, 2, :], scalar=ident[0:3, 2:3],
                                               in1=sel, op0=ALU.mult, op1=ALU.add).then_inc(setup_done, 1)

            x_stats(0, 0)
            x_stats(1, 1)
            dve.wait_ge(loaded, 16 * NLOAD)
            dve.wait_ge(ident_ready, 14)
            chain(nc.vector.memset(lns_bc[:, F:F + 1], 1.0))
            chain(nc.vector.tensor_tensor(g13_bc[:, :], gate_rows[:, 0, :], gate_rows[:, 2, :], ALU.add))
            chain(nc.vector.tensor_tensor(g23_bc[:, :], gate_rows[:, 1, :], gate_rows[:, 2, :], ALU.subtract))
            for c in range(C):
                chain(nc.vector.reduce_sum(wmean[:, c:c + 1], wskip_sb[:, c, 0:F], AX.X))
                chain(nc.vector.tensor_scalar(wmean[:, c:c + 1], wmean[:, c:c + 1], 1.0 / F, None, ALU.mult))
                chain(nc.vector.tensor_scalar(wd_sb[:, c, 0:F], wskip_sb[:, c, 0:F], wmean[:, c:c + 1], None, ALU.subtract))
                chain(nc.vector.tensor_tensor_reduce(out=setup_scr[:, :], in0=wskip_sb[:, c, 0:F], in1=g13_bc[:, :], scale=1.0,
                                                     scalar=0.0, op0=ALU.mult, op1=ALU.add, accum_out=wd_sb[:, c, F:F + 1]))
            chain(nc.vector.reduce_sum(wmean[:, C:C + 1], bskip_bc[:, :], AX.X))
            chain(nc.vector.tensor_scalar(wmean[:, C:C + 1], wmean[:, C:C + 1], 1.0 / F, None, ALU.mult))
            bd = WB['d']
            chain(nc.vector.tensor_scalar(bias_row[:, bd:bd + F], bskip_bc[0:3, :], wmean[0:3, C:C + 1], None, ALU.subtract))
            chain(nc.vector.tensor_tensor_reduce(out=setup_scr[:, :], in0=bskip_bc[:, :], in1=g13_bc[:, :], scale=1.0,
                                                 scalar=0.0, op0=ALU.mult, op1=ALU.add, accum_out=wmean[:, C:C + 1]))
            chain(nc.vector.tensor_tensor(bias_row[:, bd + F:bd + F + 1], wmean[0:3, C:C + 1], bgate_bc[0:3, :], ALU.add))
            split_bias(WB['d'], BW)
            x_bias(0, 0)
            x_bias(1, 1)
            x_stats(2, 2)
            chain(nc.vector.tensor_scalar(negalpha_bc[:, :], alpha_bc[:, :], -1.0, None, ALU.mult))
            chain(nc.vector.memset(v_ring[:, :, :, 0], 1.0))
            chain(nc.vector.memset(seg_mask[:, :], 0.0))
            chain(nc.vector.memset(seg_maxT[:, :], 0.0))
            chain(nc.vector.memset(state[:, 1, R - 1, :], 0.0))
            chain(nc.vector.memset(maxes[:, 1, R - 1, :], 0.0))

            dve.wait_ge(edges_loaded, 16 * 6)
            SRC, DST, DSTROW, OUTROW, EQNEXT = range(5)
            chain(nc.vector.tensor_copy(nat_f[:, SRC, :], nat_i[:, 0, :]))
            chain(nc.vector.tensor_copy(nat_f[:, DST, :], nat_i[:, 1, :]))
            chain(nc.vector.tensor_copy(nat_f[:, DSTROW, :], nat_i[:, 2, :]))
            chain(nc.vector.tensor_tensor(nat_f[:, EQNEXT, :], nat_f[:, DST, :], nat_f[:, DSTROW, :], ALU.is_equal))
            chain(nc.vector.scalar_tensor_tensor(out=nat_f[:, OUTROW, :], in0=nat_f[:, EQNEXT, :], scalar=SKIP_ROW,
                                                 in1=nat_f[:, DST, :], op0=ALU.mult, op1=ALU.add))
            nc.vector.tensor_scalar(nat_f[:, DSTROW, :], nat_f[:, DST, :], float(N - 1), None, ALU.min).then_inc(table_step, 1)
            x_bias(2, 2)
            for c in range(C):
                chain(nc.vector.tensor_copy(wskip_sb[:, c, F:F + 1], wd_sb[:, c, F:F + 1]))
                chain(nc.vector.tensor_tensor(setup_scr[:, :].rearrange("p (h d) -> p h d", h=H), wv_sb[:, c, :, 0:D],
                                              g23_bc[:, :].rearrange("p (h d) -> p h d", h=H), ALU.mult))
                chain(nc.vector.reduce_sum(wv_sb[:, c, :, D], setup_scr[:, :].rearrange("p (h d) -> p h d", h=H), AX.X))
            chain(nc.vector.tensor_tensor(setup_scr[:, :], bv_bc[:, :], g23_bc[:, :], ALU.mult))
            chain(nc.vector.reduce_sum(ubias[:, :], setup_scr[:, :].rearrange("p (h d) -> p h d", h=H), AX.X))
            bv_row = bias_row[:, WB['v']:WB['v'] + H * (D + 1)].rearrange("p (h d) -> p h d", h=H)
            for row, val in ((bias_row[:, 0:F], bq_bc[0:3, :]), (bias_row[:, WB['k']:WB['k'] + F], bk_bc[0:3, :]),
                             (bv_row[:, :, 0:D], bv_bc[0:3, :].rearrange("p (h d) -> p h d", h=H)), (bv_row[:, :, D], ubias[0:3, :]),
                             (bias_row[:, WB['s']:WB['s'] + F], bskip_bc[0:3, :]),
                             (bias_row[:, WB['s'] + F:WB['s'] + F + 1], bias_row[:, bd + F:bd + F + 1])):
                chain(nc.vector.tensor_copy(row, val))
            split_bias(0, WB['d'])
            dve.wait_ge(table_ps_ready, 1)

            def column(n, h):
                return (agg_ps, carry_ps)[h][:, n * HALF:(n + 1) * HALF]

            for h in range(2):
                tiles = rows_idx[:, :, :].rearrange("p g (n r) -> p g n r", n=3)
                for n, k in ((SRC, 0), (DSTROW, 1), (OUTROW, 2)):
                    for q in range(R // 2):
                        chain(nc.vector.tensor_copy(tiles[:, :, k, 2 * q + h], column(n, h)[:, q:HALF:R // 2]))
                chain(nc.vector.tensor_copy(key_cols[:, 1 + h:1 + TP:2], column(DST, h)))
                chain(nc.vector.tensor_copy(eq_cols[:, h:TP:2], column(EQNEXT, h)))
            key_g = key_cols[:, 1:1 + TP].rearrange("p (g r) -> p g r", r=R)
            chain(nc.vector.tensor_copy(meta[:, :, 0:R], key_g))
            eq_g = eq_cols[:, :].rearrange("p (g r) -> p g r", r=R)
            for r in range(R):
                chain(nc.vector.tensor_copy(meta[:, :, 2 * R + r * H:2 * R + (r + 1) * H],
                                            eq_g[:, :, r:r + 1].to_broadcast([P, G, H])))
            nc.vector.memset(wait_mark[:, :], 0.0).then_inc(table_step, 1)
            dve.wait_ge(table_ps_ready, 2)
            last_key = agg_ps[:, 0:TP].rearrange("p (g r) -> p g r", r=R)
            chain(nc.vector.tensor_tensor(meta[:, :, R:2 * R], key_g, last_key, ALU.not_equal))
            nc.vector.tensor_scalar(meta[:, :, R:2 * R], meta[:, :, R:2 * R], -BIG, None, ALU.mult).then_inc(table_ready, 1)
            dve.wait_ge(table_ready, 1)

            steady(dve, step, 0, BLOCKS + 3)

            def edge_meta(g, j):
                rows = meta[:, g, :] if isinstance(g, int) else meta[:, bass.ds(g, 1), :].rearrange("p a b -> p (a b)")
                nc.vector.tensor_copy(meta_b[:, j % 2, :], rows).then_inc(e_meta_ready, 1)

            def edge_score(g, j):
                dve.wait_ge(e_qk_copied, R * g + R)
                if e_past(g, -1):
                    dve.wait_ge(e_scoreT_ready, g)
                q, k = qk_ring[:, j % 2, :, 0:F], qk_ring[:, j % 2, :, F:2 * F]
                nc.vector.tensor_tensor(q, q, k, ALU.mult).then_inc(e_prod_ready, 1)
                dve.wait_ge(e_prod_ready, g + 1)
                nc.vector.tensor_reduce(score[:, j % 2, :].rearrange("p (r h) -> p r h", h=H), q.rearrange("p r (h d) -> p r h d", h=H),
                                        AX.X, ALU.add).then_inc(e_score_ready, 1)

            def edge_scan(g, j):
                dve.wait_ge(e_scoreT_ready, g + 1)
                nc.vector.tensor_scalar(seg_mask[:, 1:P + 1], eqT_ps, 1.0, BIG, ALU.subtract, ALU.mult).then_inc(e_scan, 1)
                dve.wait_ge(e_scan, 2 * g + 1)
                nc.vector.tensor_tensor_scan(run_max[:, :], seg_mask[:, 0:P], scoreT_ps, -BIG, ALU.add, ALU.max).then_inc(e_scan, 1)
                dve.wait_ge(e_scan, 2 * g + 2)
                nc.vector.tensor_tensor_scan(seg_maxT[0:R * H, ::-1], seg_mask[:, P:0:-1], run_max[:, ::-1], -BIG,
                                             ALU.add, ALU.max).then_inc(e_tmax_ready, 1)

            def edge_tile_max(g, j):
                dve.wait_ge(e_tmax_ps_ready, g + 1)
                nc.vector.tensor_copy(tile_max[:, :], tmax_ps[:, 0:R * H]).then_inc(e_tmax_ready, 1)

            def edge_same(g, j):
                dve.wait_ge(e_keyrow_ready, g + 1)
                nc.vector.tensor_tensor(same[:, j % 2, :].rearrange("p (r e) -> p r e", r=R),
                                        keyrow_ps.rearrange("p (r e) -> p r e", r=R),
                                        meta_b[:, j % 2, 0:R].unsqueeze(2).to_broadcast([P, R, P]), ALU.is_equal).then_inc(e_same_ready, 1)

            def edge_max(g, j, r):
                dve.wait_ge(e_cmax_ps_ready, R * g + r + 1)
                if r == 0:
                    dve.wait_ge(e_tmax_ready, 2 * g + 2)
                nc.vector.tensor_tensor(carry_max[:, r, :], cmax_ps, meta_b[:, j % 2, R + r:R + r + 1].to_broadcast([P, H]), ALU.add).then_inc(e_cmax_ready, 1)
                dve.wait_ge(e_cmax_ready, R * g + r + 1)
                nc.vector.tensor_tensor(maxes[:, j % 2, r, :], tile_max[:, r * H:(r + 1) * H], carry_max[:, r, :],
                                        ALU.max).then_inc(e_max_ready, 1)

            def edge_exponents(g, j):
                if e_past(g, -1):
                    dve.wait_ge(e_aw_ready, g)
                dve.wait_ge(e_max_ready, R * g + R)
                m = maxes[:, j % 2, :, :].rearrange("p r h -> p (r h)")
                nc.vector.tensor_tensor(expo[:, 0, :], score[:, j % 2, :], m, ALU.subtract)
                nc.vector.tensor_tensor(expo[:, 1, :], carry_max[:, :, :].rearrange("p r h -> p (r h)"), m,
                                        ALU.subtract).then_inc(e_expo_ready, 1)

            def edge_values(g, j):
                dve.wait_ge(e_aw_ready, g + 1)
                dve.wait_ge(e_vsk_copied, 2 * (R * g + R))
                if e_past(g, -1):
                    dve.wait_ge(e_agg_ps_ready, R * g)
                nc.vector.tensor_tensor(vals[:, :, :].rearrange("p r (h v) -> p (r h) v", h=H), v_ring[:, j % 4, :, :],
                                        aw[:, j % 2, 0, :].unsqueeze(2).to_broadcast([P, R * H, V]), ALU.mult).then_inc(e_vals_ready, 1)

            def edge_aggregate(g, j, r):
                dve.wait_ge(e_agg_ps_ready, R * g + r + 1)
                dve.wait_ge(e_carried, R * g + r + 1)
                nc.vector.tensor_tensor(state[:, j % 2, r, :], agg_ps[:, 0:H * V], carried[:, :], ALU.add).then_inc(e_state_ready, 1)

            def edge_logit(g, j):
                st = state[:, j % 2, :, :].rearrange("p r (h v) -> p (r h) v", h=H)
                dve.wait_ge(e_state_ready, R * g + R)
                nc.vector.reciprocal(rden[:, :], st[:, :, 0]).then_inc(e_gate_step, 1)
                dve.wait_ge(e_gate_step, 6 * g + 1)
                nc.vector.tensor_tensor(ugate[:, :], st[:, :, V - 1], rden[:, :], ALU.mult).then_inc(e_gate_step, 1)
                dve.wait_ge(e_gate_step, 6 * g + 2)
                nc.vector.reduce_sum(logit[:, :], ugate[:, :].rearrange("p (r h) -> p r h", h=H), AX.X).then_inc(e_gate_step, 1)
                dve.wait_ge(e_gate_step, 6 * g + 3)
                nc.vector.tensor_tensor(logit[:, :], logit[:, :], sk_ring[:, j % 4, :, F], ALU.add).then_inc(e_logit_ready, 1)

            def edge_coefficients(g, j):
                dve.wait_ge(e_eexp_ready, g + 1)
                nc.vector.tensor_scalar(egt[:, :], eexp[:, j % 2, :], 1.0, None, ALU.add).then_inc(e_gate_step, 1)
                dve.wait_ge(e_gate_step, 6 * g + 4)
                nc.vector.reciprocal(egt[:, :], egt[:, :]).then_inc(e_gate_step, 1)
                dve.wait_ge(e_gate_step, 6 * g + 5)
                nc.vector.tensor_scalar(omg[:, :], egt[:, :], -1.0, 1.0, ALU.mult, ALU.add).then_inc(e_gate_step, 1)
                dve.wait_ge(e_gate_step, 6 * g + 6)
                nc.vector.tensor_tensor(coef[:, :].rearrange("p (r h) -> p r h", h=H), rden[:, :].rearrange("p (r h) -> p r h", h=H),
                                        omg[:, :].unsqueeze(2).to_broadcast([P, R, H]), ALU.mult).then_inc(e_mix, 1)

            def edge_mix(g, j):
                st = state[:, j % 2, :, :].rearrange("p r (h v) -> p (r h) v", h=H)
                dve.wait_ge(e_mix, 4 * g + 1)
                if e_past(g, -1):
                    dve.wait_ge(e_mixn_ready, g)
                nc.vector.tensor_tensor(mix.rearrange("p r (h d) -> p r h d", h=H),
                                        st[:, :, 1:D + 1].rearrange("p (r h) d -> p r h d", h=H),
                                        coef[:, :].rearrange("p (r h) -> p r h", h=H).unsqueeze(3).to_broadcast([P, R, H, D]),
                                        ALU.mult).then_inc(e_mix, 1)
                dve.wait_ge(e_mix, 4 * g + 2)
                for r in range(R):
                    last = nc.vector.scalar_tensor_tensor(out=mix[:, r, :], in0=sk_ring[:, j % 4, r, 0:F], scalar=egt[:, r:r + 1],
                                                          in1=mix[:, r, :], op0=ALU.mult, op1=ALU.add)
                last.then_inc(e_mix, 1)

            def edge_mix_stats(g, j):
                dve.wait_ge(e_mix, 4 * g + 3)
                for r in range(R):
                    last = nc.vector.bn_stats(mstats[:, r, :], mix[:, r, :])
                last.then_inc(e_mix, 1)
                dve.wait_ge(e_mix, 4 * g + 4)
                nc.vector.memset(wait_mark[:, :], 0.0)
                for r in range(R):
                    last = nc.vector.bn_aggr(mmv[:, r, :], mstats[:, r, :])
                last.then_inc(e_mmv_ready, 1)

            def edge_mix_bias(g, j):
                dve.wait_ge(e_mrstd_ready, g + 1)
                nc.vector.scalar_tensor_tensor(out=mbias[:, :], in0=mmv[:, :, 0], scalar=-1.0, in1=mrstd[:, :],
                                               op0=ALU.mult, op1=ALU.mult).then_inc(e_mbias_ready, 1)

            def edge_ln_scale(g, j):
                dve.wait_ge(e_mixn_ready, g + 1)
                nc.vector.tensor_tensor(mixn, mixn, lns_bc[:, None, 0:F].to_broadcast([P, R, F]), ALU.mult).then_inc(e_scaled, 1)

            def edge_ln_bias(g, j):
                s = j % US
                dve.wait_ge(e_scaled, g + 1)
                if isinstance(g, int) and g == 0:
                    dve.wait_ge(dense_written, 1)
                if e_past(g, -US):
                    dve.wait_ge(scattered[s], 16 * R * e_turns(g, j, US, 0))
                nc.vector.tensor_tensor(ut[:, s, :].rearrange("p (r f) -> p r f", r=R), mixn,
                                        lnb_bc[:, None, :].to_broadcast([P, R, F]), ALU.add).then_inc(e_u_ready, 1)

            def edge_positive(g, j):
                s = j % US
                dve.wait_ge(e_u_ready, g + 1)
                nc.vector.scalar_tensor_tensor(out=pos[:, j % 2, :], in0=ut[:, s, :], scalar=0.0,
                                               in1=xt[:, (j + FIRST_SLOT) % XS, :], op0=ALU.max, op1=ALU.add).then_inc(e_pos_ready, 1)

            def edge_row(g, j):
                dve.wait_ge(e_neg_ready, g + 1)
                dve.wait_ge(e_pos_ready, g + 1)
                nc.vector.scalar_tensor_tensor(out=ut[:, j % US, :], in0=neg[:, j % 2, :], scalar=negalpha_bc[:, 0:1],
                                               in1=pos[:, j % 2, :], op0=ALU.mult, op1=ALU.add).then_inc(e_row_ready, 1)

            def e_step(g, j):
                if e_live(g, -1):
                    edge_score(g - 1, j - 1)
                if e_live(g, -2):
                    edge_values(g - 2, j - 2)
                if e_live(g, -3):
                    edge_logit(g - 3, j - 3)
                if e_live(g, 1):
                    edge_stats(g + 1, j + 1)
                if e_live(g, 0):
                    edge_meta(g, j)
                if e_live(g, -1):
                    edge_scan(g - 1, j - 1)
                if e_live(g, -3):
                    edge_coefficients(g - 3, j - 3)
                if e_live(g, -2):
                    edge_aggregate(g - 2, j - 2, 0)
                if e_live(g, 1):
                    edge_bias(g + 1, j + 1)
                if e_live(g, -4):
                    edge_ln_scale(g - 4, j - 4)
                if e_live(g, -1):
                    edge_tile_max(g - 1, j - 1)
                    edge_max(g - 1, j - 1, 0)
                    edge_same(g - 1, j - 1)
                if e_live(g, -4):
                    edge_ln_bias(g - 4, j - 4)
                if e_live(g, -2):
                    edge_aggregate(g - 2, j - 2, 1)
                if e_live(g, -1):
                    edge_max(g - 1, j - 1, 1)
                if e_live(g, -4):
                    edge_positive(g - 4, j - 4)
                if e_live(g, -3):
                    edge_mix(g - 3, j - 3)
                if e_live(g, -2):
                    edge_aggregate(g - 2, j - 2, 2)
                if e_live(g, -1):
                    edge_max(g - 1, j - 1, 2)
                if e_live(g, -3):
                    edge_mix_stats(g - 3, j - 3)
                if e_live(g, -4):
                    edge_row(g - 4, j - 4)
                if e_live(g, -2):
                    edge_aggregate(g - 2, j - 2, 3)
                if e_live(g, -1):
                    edge_max(g - 1, j - 1, 3)
                    edge_exponents(g - 1, j - 1)
                if e_live(g, -3):
                    edge_mix_bias(g - 3, j - 3)

            e_steady(dve, e_step, 0, G + 4)

        @block.scalar
        def _(act):
            act.wait_ge(ident_ready, 14)

            def x_norm(k, j):
                b = j % 2
                act.wait_ge(xbias_ready, k + 1)
                if not isinstance(k, int) or k >= 2:
                    act.wait_ge(hTps_ready, 2 * (k - 1))
                for r in range(R):
                    last = nc.scalar.activation(xn[:, b, r * F:(r + 1) * F], xt[:, j % XS, r * F:(r + 1) * F], ACT.Identity,
                                                bias=xbias[:, b, r:r + 1], scale=xrstd[:, b, r:r + 1])
                last.then_inc(xn_ready, 1)

            def row_stats(k, j):
                b, row = j % 2, xt[:, j % XS, (R - 1) * F:R * F]
                act.wait_ge(x_loaded[j % XS], 16 * (turns(k, j, XS, 0) + 1))
                nc.scalar.activation(vals[:, 2 * b, 0:F], row, ACT.Identity, scale=1.0 / F,
                                     accum_out=xmv[:, b, R - 1, 0:1]).then_inc(xrow_ready, 1)
                act.wait_ge(xrow_ready, 2 * k + 1)
                nc.scalar.activation(vals[:, 2 * b + 1, 0:F], row, ACT.Square, scale=-1.0, bias=xmv[:, b, R - 1, 0:1],
                                     accum_out=xmv[:, b, R - 1, 1:2]).then_inc(xrow_ready, 1)

            def relu_transposed(k, b):
                if not isinstance(k, int) or k >= 2:
                    act.wait_ge(y_ready, 2 * (k - 1))
                for half in range(2):
                    act.wait_ge(hTps_ready, 2 * k + half + 1)
                    nc.scalar.activation(hT[:, b, half * 512:(half + 1) * 512], hT_ps[:, half, :], ACT.Relu).then_inc(hT_ready, 1)

            def step(k, j):
                if live(k, 3):
                    row_stats(k + 3, j + 3)
                if live(k, -1):
                    b = (j - 1) % 2
                    act.wait_ge(yscaled, 2 * k)
                    nc.scalar.activation(egate[:, b, :], wy[:, b, :, F], ACT.Exp, scale=-1.0).then_inc(egate_ready, 1)
                    act.wait_ge(egate_ready, 2 * k - 1)
                    nc.scalar.activation(gate2[:, b, :], egate[:, b, :], ACT.Square, scale=EPS ** 0.5,
                                         bias=root_eps[:, 0:1]).then_inc(egate_ready, 1)
                if live(k, 1):
                    relu_transposed(k + 1, (j + 1) % 2)
                if live(k, 2):
                    x_norm(k + 2, j + 2)
                if live(k, 0):
                    for r in range(R):
                        if r == 0 and (not isinstance(k, int) or k >= 2):
                            act.wait_ge(gate_var_ready, k - 1)
                        if r % 2 == 0:
                            act.wait_ge(y_ready, 2 * k + r // 2 + 1)
                        nc.scalar.activation(sq_scr[:, r, :], y_ps[:, r, 0:F], ACT.Square, scale=F ** -0.5,
                                             accum_out=ssq[:, j % 2, r:r + 1]).then_inc(ysq_ready, 1)
                if live(k, -2):
                    act.wait_ge(u_ready, k - 1)
                    if not isinstance(k, int) or k >= 4:
                        act.wait_ge(row_ready, k - 3)
                    nc.scalar.activation(neg[:, j % 2, :], ut[:, (j - 2) % US, :], ACT.Relu, scale=-1.0).then_inc(neg_ready, 1)

            row_stats(0, 0)
            row_stats(1, 1)
            x_norm(0, 0)
            row_stats(2, 2)
            x_norm(1, 1)
            relu_transposed(0, 0)
            steady(act, step, 0, BLOCKS + 2)

            def edge_norm(g, j, r):
                b = j % 2
                act.wait_ge(e_xbias_ready, g + 1)
                if e_past(g, -1):
                    act.wait_ge(e_hTps_ready, R * (g - 1) + r + 1)
                for side, rows in enumerate((xsrc[:, j % 2, :], xt[:, (j + FIRST_SLOT) % XS, :])):
                    c = side * R + r
                    last = nc.scalar.activation(xn[:, side, r * F:(r + 1) * F], rows[:, r * F:(r + 1) * F], ACT.Identity,
                                                bias=ebias[:, b, c:c + 1], scale=erstd[:, b, c:c + 1])
                last.then_inc(e_xn_ready, 1)

            def edge_relu(t, b):
                act.wait_ge(e_hTps_ready, t + 1)
                nc.scalar.activation(hT[:, b, 0:512], ehT_ps, ACT.Relu).then_inc(e_hT_ready, 1)

            def rescale_carried(g, j, r):
                act.wait_ge(e_agg_ps_ready, R * g + r + 1)
                act.wait_ge(e_aw_ready, g + 1)
                for h in range(H):
                    last = nc.scalar.activation(carried[:, h * V:(h + 1) * V], carry_ps[:, h * V:(h + 1) * V], ACT.Copy,
                                                scale=aw[:, j % 2, 1, r * H + h:r * H + h + 1])
                last.then_inc(e_carried, 1)

            def e_step(g, j):
                for r in range(R):
                    t = g * R + r
                    if e_live(g, 0):
                        act.wait_ge(e_qk_ps_ready, t + 1)
                        if r == 0 and e_past(g, -2):
                            act.wait_ge(e_score_ready, g - 1)
                        nc.scalar.copy(qk_ring[:, j % 2, r, :], qk_ps).then_inc(e_qk_copied, 1)
                        if r < R - 1 or e_live(g, 1):
                            if e_past(g, -1) or r >= 1:
                                act.wait_ge(e_vsk_ps_ready, t)
                            edge_relu(t + 1, (r + 1) % 2)
                    if r == 3 and e_live(g, -2):
                        rescale_carried(g - 2, j - 2, 2)
                    if e_live(g, 0):
                        act.wait_ge(e_vsk_ps_ready, t + 1)
                        if r == 0 and e_past(g, -4):
                            act.wait_ge(e_vals_ready, g - 3)
                            act.wait_ge(e_mmv_ready, g - 3)
                        nc.scalar.copy(v_ring[:, j % 4, r * H:(r + 1) * H, 1:V], v_ps.rearrange("p (h v) -> p h v", h=H)).then_inc(e_vsk_copied, 1)
                        nc.scalar.copy(sk_ring[:, j % 4, r, :], sk_ps).then_inc(e_vsk_copied, 1)
                    if r in (1, 2) and e_live(g, -2):
                        rescale_carried(g - 2, j - 2, r - 1)
                    if r == 0 and e_live(g, -2):
                        act.wait_ge(e_expo_ready, g - 1)
                        nc.scalar.activation(aw[:, j % 2, :, :], expo[:, :, :], ACT.Exp, scale=SCORE_SCALE).then_inc(e_aw_ready, 1)
                    if r == 0 and e_live(g, -3):
                        act.wait_ge(e_logit_ready, g - 2)
                        nc.scalar.activation(eexp[:, (j - 3) % 2, :], logit[:, :], ACT.Exp, scale=-1.0).then_inc(e_eexp_ready, 1)
                    if r == 2 and e_live(g, 1):
                        edge_norm(g + 1, j + 1, 0)
                        edge_norm(g + 1, j + 1, 1)
                    if r == 2 and e_live(g, -4):
                        act.wait_ge(e_u_ready, g - 3)
                        if e_past(g, -6):
                            act.wait_ge(e_row_ready, g - 5)
                        u = ut[:, (j - 4) % US, :]
                        nc.scalar.activation(neg[:, j % 2, :], u, ACT.Relu, scale=-1.0).then_inc(e_neg_ready, 1)
                    if r == 3 and e_live(g, 1):
                        edge_norm(g + 1, j + 1, 2)
                        edge_norm(g + 1, j + 1, 3)
                    if r == 1 and e_live(g, -4):
                        act.wait_ge(e_mbias_ready, g - 3)
                        if e_past(g, -5):
                            act.wait_ge(e_u_ready, g - 4)
                        for q in range(R):
                            last = nc.scalar.activation(mixn[:, q, :], mix[:, q, :], ACT.Identity,
                                                        bias=mbias[:, q:q + 1], scale=mrstd[:, q:q + 1])
                        last.then_inc(e_mixn_ready, 1)
                    if r == 3 and e_live(g, -2):
                        rescale_carried(g - 2, j - 2, 3)

            for r in range(R):
                edge_norm(0, 0, r)
            edge_relu(0, 0)
            e_steady(act, e_step, 0, G + 4)

        @block.tensor
        def _(pe):
            pe.wait_ge(ident_ready, 14)

            def transposes(k, b):
                pe.wait_ge(xn_ready, k + 1)
                for half in range(2):
                    if not isinstance(k, int) or k >= 1:
                        pe.wait_ge(hT_ready, 2 * (k - 1) + half + 1)
                    for q in range(4):
                        c = 4 * half + q
                        last = nc.tensor.transpose(hT_ps[:, half, q * P:(q + 1) * P], xn[:, b, c * P:(c + 1) * P], ident[:, :])
                    last.then_inc(hTps_ready, 1)

            def project(k, b):
                for r in range(R):
                    if r % 2 == 0:
                        pe.wait_ge(hT_ready, 2 * k + r // 2 + 1)
                        if not isinstance(k, int) or k >= 1:
                            pe.wait_ge(yscaled, 2 * (k - 1) + r // 2 + 1)
                    nc.tensor.matmul(y_ps[:, r, 0:F + 1], ones3[:, :], bias3[:, WB["d"]:WB["d"] + F + 1], start=True, stop=False)
                    for c in range(C):
                        last = nc.tensor.matmul(y_ps[:, r, 0:F + 1], hT[:, b, (C * r + c) * P:(C * r + c + 1) * P],
                                                wd_sb[:, c, :], start=False, stop=(c == C - 1))
                    if r % 2 == 1:
                        last.then_inc(y_ready, 1)

            def step(k, j):
                if live(k, 1):
                    transposes(k + 1, (j + 1) % 2)
                if live(k, 0):
                    project(k, j % 2)

            transposes(0, 0)
            pe.wait_ge(table_step, 2)
            for h in range(2):
                for n in range(5):
                    last = nc.tensor.transpose((agg_ps, carry_ps)[h][:, n * HALF:(n + 1) * HALF], nat_f[:, n, h * P:(h + 1) * P],
                                               ident[0:HALF, 0:HALF])
            last.then_inc(table_ps_ready, 1)
            pe.wait_ge(setup_done, 1)
            step(0, 0)
            pe.wait_ge(table_step, 3)
            nc.tensor.matmul(agg_ps[:, 0:TP], last_row[:, :], key_cols[:, 0:TP], start=True, stop=True).then_inc(table_ps_ready, 1)
            steady(pe, step, 1, BLOCKS)
            pe.wait_ge(setup_done, 2)
            pe.wait_ge(yscaled, 2 * BLOCKS)

            def edge_transposes(g, r):
                t = g * R + r
                pe.wait_ge(e_xn_ready, t + 1)
                if e_past(g, -1) or r >= 1:
                    pe.wait_ge(e_hT_ready, t)
                for side in range(2):
                    for c in range(C):
                        last = nc.tensor.transpose(ehT_ps[:, (side * C + c) * P:(side * C + c + 1) * P],
                                                   xn[:, side, (C * r + c) * P:(C * r + c + 1) * P], ident[:, :])
                last.then_inc(e_hTps_ready, 1)

            def project_edges(out_ps, side, r, weights, at, n):
                nc.tensor.matmul(out_ps, ones3[:, :], bias3[:, at:at + n], start=True, stop=False)
                for c in range(C):
                    last = nc.tensor.matmul(out_ps, hT[:, r % 2, (side * C + c) * P:(side * C + c + 1) * P], weights[c],
                                            start=False, stop=(c == C - 1))
                return last

            def score_rows(g, j):
                pe.wait_ge(e_score_ready, g + 1)
                pe.wait_ge(e_meta_ready, g + 1)
                if e_past(g, -1):
                    pe.wait_ge(e_max_ready, R * g)
                nc.tensor.transpose(scoreT_ps, score[:, j % 2, :], ident[:, :])
                nc.tensor.transpose(eqT_ps, meta_b[:, j % 2, 2 * R:META], ident[:, :]).then_inc(e_scoreT_ready, 1)

            def tile_maxima(g, j):
                pe.wait_ge(e_tmax_ready, 2 * g + 1)
                carried_max(g, j, 0)
                nc.tensor.transpose(tmax_ps, seg_maxT[:, :], ident[:, :]).then_inc(e_tmax_ps_ready, 1)
                if e_past(g, -1):
                    pe.wait_ge(e_same_ready, g)
                for r in range(R):
                    last = nc.tensor.transpose(keyrow_ps[:, r * P:(r + 1) * P], meta_b[:, j % 2, r:r + 1].to_broadcast([P, P]), ident[:, :])
                last.then_inc(e_keyrow_ready, 1)

            def carried_max(g, j, r):
                if e_past(g, -1) or r >= 1:
                    pe.wait_ge(e_max_ready, R * g + r)
                prev = maxes[:, (j - (r == 0)) % 2, (r - 1) % R, :]
                nc.tensor.matmul(cmax_ps, last_row[:, :], prev, start=True, stop=True).then_inc(e_cmax_ps_ready, 1)

            def aggregate(g, j, r):
                pe.wait_ge(e_vals_ready, g + 1)
                pe.wait_ge(e_same_ready, g + 1)
                if e_past(g, -1) or r >= 1:
                    pe.wait_ge(e_state_ready, R * g + r)
                nc.tensor.matmul(agg_ps[:, 0:H * V], same[:, j % 2, r * P:(r + 1) * P], vals[:, r, :], start=True, stop=True)
                prev = state[:, (j - (r == 0)) % 2, (r - 1) % R, :]
                nc.tensor.matmul(carry_ps[:, 0:H * V], last_row[:, :], prev, start=True, stop=True).then_inc(e_agg_ps_ready, 1)

            def e_step(g, j):
                for r in range(R):
                    t = g * R + r
                    if e_live(g, 0):
                        pe.wait_ge(e_hT_ready, t + 1)
                        if e_past(g, -1) or r >= 1:
                            pe.wait_ge(e_qk_copied, t)
                        project_edges(qk_ps[:, 0:F], 0, r, [wq_sb[:, c, :] for c in range(C)], WB['q'], F)
                        project_edges(qk_ps[:, F:2 * F], 1, r, [wk_sb[:, c, :] for c in range(C)], WB['k'], F).then_inc(e_qk_ps_ready, 1)
                        if r < R - 1:
                            edge_transposes(g, r + 1)
                        elif e_live(g, 1):
                            edge_transposes(g + 1, 0)
                    if e_live(g, -1):
                        if r == 1:
                            score_rows(g - 1, j - 1)
                        elif r == 2:
                            tile_maxima(g - 1, j - 1)
                        elif r == 3:
                            carried_max(g - 1, j - 1, 2)
                    if r == 3 and e_live(g, -2):
                        aggregate(g - 2, j - 2, 2)
                    if e_live(g, 0):
                        if e_past(g, -1) or r >= 1:
                            pe.wait_ge(e_vsk_copied, 2 * t)
                        project_edges(v_ps, 0, r, [wv_sb[:, c, :, :].rearrange("p h v -> p (h v)") for c in range(C)], WB['v'], H * (D + 1))
                        project_edges(sk_ps, 1, r, [wskip_sb[:, c, :] for c in range(C)], WB['s'], F + 1).then_inc(e_vsk_ps_ready, 1)
                    if r != 3 and r != 0 and e_live(g, -2):
                        aggregate(g - 2, j - 2, r - 1)
                    if r == 3 and e_live(g, -2):
                        aggregate(g - 2, j - 2, 3)
                    if r >= 2 and e_live(g, -1):
                        carried_max(g - 1, j - 1, 2 * r - 3)

            edge_transposes(0, 0)
            e_steady(pe, e_step, 0, G + 2)


_NAMES = ['x', 'src', 'dst', 'L0_gnn_Wq', 'L0_gnn_bq', 'L0_gnn_Wk', 'L0_gnn_bk', 'L0_gnn_Wv', 'L0_gnn_bv',
          'L0_gnn_Wskip', 'L0_gnn_bskip', 'L0_gnn_Wg', 'L0_gnn_bg', 'L0_gnn_ln_scale', 'L0_gnn_ln_bias',
          'L0_gnn_prelu_alpha']


def kernel(**inputs):
    import numpy as np
    import concourse.bacc as bacc
    from concourse.bass_utils import run_bass_kernel_spmd

    nc = bacc.Bacc("TRN2", target_bir_lowering=False, num_devices=1)
    arrays, args = {}, []
    for name in _NAMES:
        a = np.ascontiguousarray(inputs[name])
        if a.ndim == 0:
            a = a.reshape(1)
        arrays[f"in_{name}"] = a
        args.append(nc.dram_tensor(f"in_{name}", a.shape, mybir.dt.from_np(a.dtype), kind="ExternalInput").ap())
    shape = inputs['x'].shape
    args.append(nc.dram_tensor("out_rows", shape, mybir.dt.float32, kind="ExternalOutput").ap())
    gnn_layer(nc, *args)
    r = run_bass_kernel_spmd(nc, [arrays], core_ids=[0])
    return r.results[0]["out_rows"]
```
